# Optimizing a Trainium2 kernel written in Bass

```python
import numpy as np
import jax
import jax.numpy as jnp

def _softmax(x, axis=-1):
    return jax.nn.softmax(x, axis=axis)

def _gelu(x):
    return jax.nn.gelu(x, approximate=True)

def _silu(x):
    return jax.nn.silu(x)

def _sigmoid(x):
    return jax.nn.sigmoid(x)

def _layernorm(x, axis=-1, eps=1e-05):
    m = jnp.mean(x, axis=axis, keepdims=True)
    v = jnp.var(x, axis=axis, keepdims=True)
    return (x - m) / jnp.sqrt(v + eps)

def _scatter_add(tgt, idx, src, axis=0):
    return tgt.at[idx].add(src)

def _segment_sum(src, seg, n):
    return jax.ops.segment_sum(src, seg, n)
kernel_name = 'mk_early_fusion_d2_tok_img768_r4_ed4753'

def setup_inputs(seed: int=0):
    np.random.seed(seed)
    _w = jnp.asarray

    def _rec_inputs():
        import jax
        import jax.numpy as jnp
        _rk = jax.random.key(seed)
        x = -7.10856e-05 + 0.999911 * jax.random.normal(jax.random.fold_in(_rk, 1), (2, 32, 128, 128), jnp.float32)
        txt = -0.00271877 + 0.451779 * jax.random.normal(jax.random.fold_in(_rk, 2), (2, 32, 192), jnp.float32)
        return (x, txt)
    x, txt = _rec_inputs()

    def _L0_tok_setup():
        import jax, jax.numpy as jnp
        import numpy as np
        B, C, H, W = (8, 32, 128, 128)
        P = 8
        D = 128
        NH, DH = (8, 64)
        M = 512
        L = 2
        DOUT = 192
        INNER = NH * DH

        def _ln(x, g, b, eps=1e-05):
            mu = x.mean(-1, keepdims=True)
            xc = x - mu
            var = (xc * xc).mean(-1, keepdims=True)
            return xc * jax.lax.rsqrt(var + eps) * g + b

        def _forward(im, conv_w, conv_b, ln1_g, ln1_b, qkv_w, out_w, out_b, ln2_g, ln2_b, ff1_w, ff1_b, ff2_w, ff2_b, lnf_g, lnf_b, head_w, head_b):
            b, c, h, w = im.shape
            hp, wp = (h // P, w // P)
            patches = im.reshape(b, c, hp, P, wp, P)
            x = jnp.einsum('bchpwq,dcpq->bhwd', patches, conv_w)
            x = x.reshape(b, hp * wp, -1) + conv_b
            n = hp * wp
            scale = DH ** (-0.5)
            for i in range(ln1_g.shape[0]):
                y = _ln(x, ln1_g[i], ln1_b[i])
                qkv = y @ qkv_w[i]
                q, k, v = jnp.split(qkv, 3, axis=-1)
                to_heads = lambda t: t.reshape(b, n, NH, DH).transpose(0, 2, 1, 3)
                q, k, v = (to_heads(q), to_heads(k), to_heads(v))
                q = jax.nn.softmax(q, axis=-1) * scale
                k = jax.nn.softmax(k, axis=-2)
                ctx = jnp.einsum('bhnd,bhne->bhde', k, v)
                att = jnp.einsum('bhnd,bhde->bhne', q, ctx)
                att = att.transpose(0, 2, 1, 3).reshape(b, n, INNER)
                x = x + att @ out_w[i] + out_b[i]
                y = _ln(x, ln2_g[i], ln2_b[i])
                hdn = jax.nn.gelu(y @ ff1_w[i] + ff1_b[i], approximate=False)
                x = x + hdn @ ff2_w[i] + ff2_b[i]
            return _ln(x, lnf_g, lnf_b) @ head_w + head_b
        key = jax.random.key(seed)
        ks = iter(jax.random.split(key, 32))
        g = lambda shape, s=0.02: (jax.random.normal(next(ks), shape) * s).astype(jnp.float32)
        inp = {'im': jax.random.normal(next(ks), (B, C, H, W), dtype=jnp.float32), 'conv_w': g((D, C, P, P)), 'conv_b': jnp.zeros((D,), jnp.float32), 'ln1_g': jnp.ones((L, D), jnp.float32), 'ln1_b': jnp.zeros((L, D), jnp.float32), 'qkv_w': g((L, D, 3 * INNER)), 'out_w': g((L, INNER, D)), 'out_b': jnp.zeros((L, D), jnp.float32), 'ln2_g': jnp.ones((L, D), jnp.float32), 'ln2_b': jnp.zeros((L, D), jnp.float32), 'ff1_w': g((L, D, M)), 'ff1_b': jnp.zeros((L, M), jnp.float32), 'ff2_w': g((L, M, D)), 'ff2_b': jnp.zeros((L, D), jnp.float32), 'lnf_g': jnp.ones((D,), jnp.float32), 'lnf_b': jnp.zeros((D,), jnp.float32), 'head_w': g((D, DOUT)), 'head_b': jnp.zeros((DOUT,), jnp.float32)}
        return inp
    _L0_tok_all = _L0_tok_setup()
    _L0_tok_in = {k: v for k, v in _L0_tok_all.items() if k in ('conv_w', 'conv_b', 'ln1_g', 'ln1_b', 'qkv_w', 'out_w', 'out_b', 'ln2_g', 'ln2_b', 'ff1_w', 'ff1_b', 'ff2_w', 'ff2_b', 'lnf_g', 'lnf_b', 'head_w', 'head_b')}
    del _L0_tok_all

    def _L0_attn_setup():
        import jax, jax.numpy as jnp
        import numpy as np
        DIM = 192
        HEADS = 12
        HEAD_DIM = DIM // HEADS
        EPS = 1e-12

        def _l1_normalize(t):
            denom = jnp.maximum(jnp.sum(jnp.abs(t), axis=-2, keepdims=True), EPS)
            return t / denom
        key = jax.random.key(seed)
        k1, k2, k3 = jax.random.split(key, 3)
        x = jax.random.normal(k1, (8, 1024, DIM), dtype=jnp.float32)
        s = 1.0 / np.sqrt(DIM)
        w_qkv = jax.random.uniform(k2, (3 * DIM, DIM), dtype=jnp.float32, minval=-s, maxval=s)
        w_proj = jax.random.uniform(k3, (DIM, DIM), dtype=jnp.float32, minval=-s, maxval=s)
        b_proj = jnp.zeros((DIM,), dtype=jnp.float32)
        return {'x': x, 'w_qkv': w_qkv, 'w_proj': w_proj, 'b_proj': b_proj}
    _L0_attn_all = _L0_attn_setup()
    _L0_attn_in = {k: v for k, v in _L0_attn_all.items() if k in ('w_qkv', 'w_proj', 'b_proj')}
    del _L0_attn_all

    def _L0_ffn_setup():
        import jax, jax.numpy as jnp
        import numpy as np
        D_MODEL = 192
        D_EXPERT = 384
        N_EXPERTS = 8
        TOP_K = 2
        EPS = 1e-06

        def _rms_norm(x, w):
            var = jnp.mean(jnp.square(x), axis=-1, keepdims=True)
            return x * jax.lax.rsqrt(var + EPS) * w
        key = jax.random.key(seed)
        ks = jax.random.split(key, 6)
        s_in = 1.0 / np.sqrt(D_MODEL)
        s_mid = 1.0 / np.sqrt(D_EXPERT)
        return {'x': jax.random.normal(ks[0], (2, 512, D_MODEL), dtype=jnp.float32), 'norm_w': jnp.ones((D_MODEL,), dtype=jnp.float32), 'router_w': jax.random.normal(ks[1], (N_EXPERTS, D_MODEL), dtype=jnp.float32) * s_in, 'gate_w': jax.random.normal(ks[2], (N_EXPERTS, D_EXPERT, D_MODEL), dtype=jnp.float32) * s_in, 'up_w': jax.random.normal(ks[3], (N_EXPERTS, D_EXPERT, D_MODEL), dtype=jnp.float32) * s_in, 'down_w': jax.random.normal(ks[4], (N_EXPERTS, D_MODEL, D_EXPERT), dtype=jnp.float32) * s_mid}
    _L0_ffn_all = _L0_ffn_setup()
    _L0_ffn_in = {k: v for k, v in _L0_ffn_all.items() if k in ('norm_w', 'router_w', 'gate_w', 'up_w', 'down_w')}
    del _L0_ffn_all

    def _L1_attn_setup():
        import jax, jax.numpy as jnp
        import numpy as np
        L = 8
        D = 192
        H = 12
        DH = D // H
        MLP_D = 4 * D
        B, S = (32, 577)
        EPS = 1e-05

        def _layernorm(x, g, b):
            m = jnp.mean(x, axis=-1, keepdims=True)
            v = jnp.mean((x - m) ** 2, axis=-1, keepdims=True)
            return (x - m) * jax.lax.rsqrt(v + EPS) * g + b

        def _msa(xn, qw, qb, kw, kb, vw, vb):
            xh = xn.reshape(xn.shape[0], xn.shape[1], H, DH)
            q = jnp.einsum('bshd,hed->bshe', xh, qw) + qb
            k = jnp.einsum('bshd,hed->bshe', xh, kw) + kb
            v = jnp.einsum('bshd,hed->bshe', xh, vw) + vb
            scores = jnp.einsum('bshe,bthe->bhst', q, k) / jnp.sqrt(jnp.float32(DH))
            attn = jax.nn.softmax(scores, axis=-1)
            out = jnp.einsum('bhst,bthd->bshd', attn, v)
            return out.reshape(xn.shape[0], xn.shape[1], D)
        key = jax.random.key(seed)
        ks = jax.random.split(key, 16)
        s = 0.02
        inp = {'x': jax.random.normal(ks[0], (B, S, D), dtype=jnp.float32), 'ln1_g': jnp.ones((L, D), jnp.float32), 'ln1_b': jnp.zeros((L, D), jnp.float32), 'qw': jax.random.normal(ks[1], (L, H, DH, DH), jnp.float32) * s, 'qb': jax.random.normal(ks[2], (L, H, DH), jnp.float32) * s, 'kw': jax.random.normal(ks[3], (L, H, DH, DH), jnp.float32) * s, 'kb': jax.random.normal(ks[4], (L, H, DH), jnp.float32) * s, 'vw': jax.random.normal(ks[5], (L, H, DH, DH), jnp.float32) * s, 'vb': jax.random.normal(ks[6], (L, H, DH), jnp.float32) * s, 'ln2_g': jnp.ones((L, D), jnp.float32), 'ln2_b': jnp.zeros((L, D), jnp.float32), 'w1': jax.random.normal(ks[7], (L, MLP_D, D), jnp.float32) * s, 'b1': jnp.zeros((L, MLP_D), jnp.float32), 'w2': jax.random.normal(ks[8], (L, D, MLP_D), jnp.float32) * s, 'b2': jnp.zeros((L, D), jnp.float32)}
        return inp
    _L1_attn_all = _L1_attn_setup()
    _L1_attn_in = {k: v for k, v in _L1_attn_all.items() if k in ('ln1_g', 'ln1_b', 'qw', 'qb', 'kw', 'kb', 'vw', 'vb', 'ln2_g', 'ln2_b', 'w1', 'b1', 'w2', 'b2')}
    del _L1_attn_all

    def _L1_ffn_setup():
        import jax, jax.numpy as jnp
        import numpy as np
        B, SEQ, D = (2, 256, 192)
        E, H = (8, 768)
        CAPACITY = 2
        key = jax.random.key(seed)
        ks = jax.random.split(key, 6)
        x = jax.random.normal(ks[0], (B, SEQ, D), dtype=jnp.float32)
        gate_weight = jax.random.normal(ks[1], (E, D), dtype=jnp.float32) * 0.006
        w1 = jax.random.normal(ks[2], (E, D, H), dtype=jnp.float32) * (1.0 / np.sqrt(D))
        b1 = jnp.zeros((E, H), dtype=jnp.float32)
        w2 = jax.random.normal(ks[3], (E, H, D), dtype=jnp.float32) * (1.0 / np.sqrt(H))
        b2 = jnp.zeros((E, D), dtype=jnp.float32)
        return {'x': x, 'gate_weight': gate_weight, 'w1': w1, 'b1': b1, 'w2': w2, 'b2': b2}
    _L1_ffn_all = _L1_ffn_setup()
    _L1_ffn_in = {k: v for k, v in _L1_ffn_all.items() if k in ('gate_weight', 'w1', 'b1', 'w2', 'b2')}
    del _L1_ffn_all
    return {'x': x, 'txt': txt, 'L0_tok_conv_w': _L0_tok_in['conv_w'], 'L0_tok_conv_b': _L0_tok_in['conv_b'], 'L0_tok_ln1_g': _L0_tok_in['ln1_g'], 'L0_tok_ln1_b': _L0_tok_in['ln1_b'], 'L0_tok_qkv_w': _L0_tok_in['qkv_w'], 'L0_tok_out_w': _L0_tok_in['out_w'], 'L0_tok_out_b': _L0_tok_in['out_b'], 'L0_tok_ln2_g': _L0_tok_in['ln2_g'], 'L0_tok_ln2_b': _L0_tok_in['ln2_b'], 'L0_tok_ff1_w': _L0_tok_in['ff1_w'], 'L0_tok_ff1_b': _L0_tok_in['ff1_b'], 'L0_tok_ff2_w': _L0_tok_in['ff2_w'], 'L0_tok_ff2_b': _L0_tok_in['ff2_b'], 'L0_tok_lnf_g': _L0_tok_in['lnf_g'], 'L0_tok_lnf_b': _L0_tok_in['lnf_b'], 'L0_tok_head_w': _L0_tok_in['head_w'], 'L0_tok_head_b': _L0_tok_in['head_b'], 'L0_attn_w_qkv': _L0_attn_in['w_qkv'], 'L0_attn_w_proj': _L0_attn_in['w_proj'], 'L0_attn_b_proj': _L0_attn_in['b_proj'], 'L0_ffn_norm_w': _L0_ffn_in['norm_w'], 'L0_ffn_router_w': _L0_ffn_in['router_w'], 'L0_ffn_gate_w': _L0_ffn_in['gate_w'], 'L0_ffn_up_w': _L0_ffn_in['up_w'], 'L0_ffn_down_w': _L0_ffn_in['down_w'], 'L1_attn_ln1_g': _L1_attn_in['ln1_g'], 'L1_attn_ln1_b': _L1_attn_in['ln1_b'], 'L1_attn_qw': _L1_attn_in['qw'], 'L1_attn_qb': _L1_attn_in['qb'], 'L1_attn_kw': _L1_attn_in['kw'], 'L1_attn_kb': _L1_attn_in['kb'], 'L1_attn_vw': _L1_attn_in['vw'], 'L1_attn_vb': _L1_attn_in['vb'], 'L1_attn_ln2_g': _L1_attn_in['ln2_g'], 'L1_attn_ln2_b': _L1_attn_in['ln2_b'], 'L1_attn_w1': _L1_attn_in['w1'], 'L1_attn_b1': _L1_attn_in['b1'], 'L1_attn_w2': _L1_attn_in['w2'], 'L1_attn_b2': _L1_attn_in['b2'], 'L1_ffn_gate_weight': _L1_ffn_in['gate_weight'], 'L1_ffn_w1': _L1_ffn_in['w1'], 'L1_ffn_b1': _L1_ffn_in['b1'], 'L1_ffn_w2': _L1_ffn_in['w2'], 'L1_ffn_b2': _L1_ffn_in['b2']}

def reference(x, txt, L0_tok_conv_w, L0_tok_conv_b, L0_tok_ln1_g, L0_tok_ln1_b, L0_tok_qkv_w, L0_tok_out_w, L0_tok_out_b, L0_tok_ln2_g, L0_tok_ln2_b, L0_tok_ff1_w, L0_tok_ff1_b, L0_tok_ff2_w, L0_tok_ff2_b, L0_tok_lnf_g, L0_tok_lnf_b, L0_tok_head_w, L0_tok_head_b, L0_attn_w_qkv, L0_attn_w_proj, L0_attn_b_proj, L0_ffn_norm_w, L0_ffn_router_w, L0_ffn_gate_w, L0_ffn_up_w, L0_ffn_down_w, L1_attn_ln1_g, L1_attn_ln1_b, L1_attn_qw, L1_attn_qb, L1_attn_kw, L1_attn_kb, L1_attn_vw, L1_attn_vb, L1_attn_ln2_g, L1_attn_ln2_b, L1_attn_w1, L1_attn_b1, L1_attn_w2, L1_attn_b2, L1_ffn_gate_weight, L1_ffn_w1, L1_ffn_b1, L1_ffn_w2, L1_ffn_b2):
    import jax
    import jax.numpy as jnp

    def _L0_tok_ref(im, conv_w, conv_b, ln1_g, ln1_b, qkv_w, out_w, out_b, ln2_g, ln2_b, ff1_w, ff1_b, ff2_w, ff2_b, lnf_g, lnf_b, head_w, head_b):
        import jax, jax.numpy as jnp
        import numpy as np
        B, C, H, W = (8, 32, 128, 128)
        P = 8
        D = 128
        NH, DH = (8, 64)
        M = 512
        L = 2
        DOUT = 192
        INNER = NH * DH

        def _ln(x, g, b, eps=1e-05):
            mu = x.mean(-1, keepdims=True)
            xc = x - mu
            var = (xc * xc).mean(-1, keepdims=True)
            return xc * jax.lax.rsqrt(var + eps) * g + b

        def _forward(im, conv_w, conv_b, ln1_g, ln1_b, qkv_w, out_w, out_b, ln2_g, ln2_b, ff1_w, ff1_b, ff2_w, ff2_b, lnf_g, lnf_b, head_w, head_b):
            b, c, h, w = im.shape
            hp, wp = (h // P, w // P)
            patches = im.reshape(b, c, hp, P, wp, P)
            x = jnp.einsum('bchpwq,dcpq->bhwd', patches, conv_w)
            x = x.reshape(b, hp * wp, -1) + conv_b
            n = hp * wp
            scale = DH ** (-0.5)
            for i in range(ln1_g.shape[0]):
                y = _ln(x, ln1_g[i], ln1_b[i])
                qkv = y @ qkv_w[i]
                q, k, v = jnp.split(qkv, 3, axis=-1)
                to_heads = lambda t: t.reshape(b, n, NH, DH).transpose(0, 2, 1, 3)
                q, k, v = (to_heads(q), to_heads(k), to_heads(v))
                q = jax.nn.softmax(q, axis=-1) * scale
                k = jax.nn.softmax(k, axis=-2)
                ctx = jnp.einsum('bhnd,bhne->bhde', k, v)
                att = jnp.einsum('bhnd,bhde->bhne', q, ctx)
                att = att.transpose(0, 2, 1, 3).reshape(b, n, INNER)
                x = x + att @ out_w[i] + out_b[i]
                y = _ln(x, ln2_g[i], ln2_b[i])
                hdn = jax.nn.gelu(y @ ff1_w[i] + ff1_b[i], approximate=False)
                x = x + hdn @ ff2_w[i] + ff2_b[i]
            return _ln(x, lnf_g, lnf_b) @ head_w + head_b
        return _forward(im, conv_w, conv_b, ln1_g, ln1_b, qkv_w, out_w, out_b, ln2_g, ln2_b, ff1_w, ff1_b, ff2_w, ff2_b, lnf_g, lnf_b, head_w, head_b)

    def _L0_attn_ref(x, w_qkv, w_proj, b_proj):
        import jax, jax.numpy as jnp
        import numpy as np
        DIM = 192
        HEADS = 12
        HEAD_DIM = DIM // HEADS
        EPS = 1e-12

        def _l1_normalize(t):
            denom = jnp.maximum(jnp.sum(jnp.abs(t), axis=-2, keepdims=True), EPS)
            return t / denom
        B, N, C = x.shape
        hd = C // HEADS
        qkv = x @ w_qkv.T
        qkv = qkv.reshape(B, N, 3, HEADS, hd).transpose(2, 0, 3, 1, 4)
        q, k, v = (qkv[0], qkv[1], qkv[2])
        q = _l1_normalize(q)
        k = _l1_normalize(k)
        if N < hd:
            out = jnp.einsum('bhnd,bhmd,bhme->bhne', q, k, v)
        else:
            kv = jnp.einsum('bhnd,bhne->bhde', k, v)
            out = jnp.einsum('bhnd,bhde->bhne', q, kv)
        out = out.transpose(0, 2, 1, 3).reshape(B, N, C)
        return out @ w_proj.T + b_proj

    def _L0_ffn_ref(x, norm_w, router_w, gate_w, up_w, down_w):
        import jax, jax.numpy as jnp
        import numpy as np
        D_MODEL = 192
        D_EXPERT = 384
        N_EXPERTS = 8
        TOP_K = 2
        EPS = 1e-06

        def _rms_norm(x, w):
            var = jnp.mean(jnp.square(x), axis=-1, keepdims=True)
            return x * jax.lax.rsqrt(var + EPS) * w
        residual = x
        B, S, D = x.shape
        xn = _rms_norm(x, norm_w)
        xf = xn.reshape(-1, D)
        logits = xf @ router_w.T
        probs = jax.nn.softmax(logits, axis=-1)
        _, top_idx = jax.lax.top_k(probs, TOP_K)
        sel = jax.nn.one_hot(top_idx, N_EXPERTS, dtype=probs.dtype).sum(axis=1)
        comb_w = probs * sel
        g = jnp.einsum('td,efd->tef', xf, gate_w)
        u = jnp.einsum('td,efd->tef', xf, up_w)
        h = jax.nn.silu(g) * u
        h = h * comb_w[:, :, None]
        y = jnp.einsum('tef,edf->td', h, down_w)
        return y.reshape(B, S, D) + residual

    def _L1_attn_ref(x, ln1_g, ln1_b, qw, qb, kw, kb, vw, vb, ln2_g, ln2_b, w1, b1, w2, b2):
        import jax, jax.numpy as jnp
        import numpy as np
        L = 8
        D = 192
        H = 12
        DH = D // H
        MLP_D = 4 * D
        B, S = (32, 577)
        EPS = 1e-05

        def _layernorm(x, g, b):
            m = jnp.mean(x, axis=-1, keepdims=True)
            v = jnp.mean((x - m) ** 2, axis=-1, keepdims=True)
            return (x - m) * jax.lax.rsqrt(v + EPS) * g + b

        def _msa(xn, qw, qb, kw, kb, vw, vb):
            xh = xn.reshape(xn.shape[0], xn.shape[1], H, DH)
            q = jnp.einsum('bshd,hed->bshe', xh, qw) + qb
            k = jnp.einsum('bshd,hed->bshe', xh, kw) + kb
            v = jnp.einsum('bshd,hed->bshe', xh, vw) + vb
            scores = jnp.einsum('bshe,bthe->bhst', q, k) / jnp.sqrt(jnp.float32(DH))
            attn = jax.nn.softmax(scores, axis=-1)
            out = jnp.einsum('bhst,bthd->bshd', attn, v)
            return out.reshape(xn.shape[0], xn.shape[1], D)
        out = x
        for l in range(L):
            out = out + _msa(_layernorm(out, ln1_g[l], ln1_b[l]), qw[l], qb[l], kw[l], kb[l], vw[l], vb[l])
            h = _layernorm(out, ln2_g[l], ln2_b[l])
            h = jax.nn.gelu(h @ w1[l].T + b1[l], approximate=False)
            out = out + (h @ w2[l].T + b2[l])
        return out

    def _L1_ffn_ref(x, gate_weight, w1, b1, w2, b2):
        import jax, jax.numpy as jnp
        import numpy as np
        B, SEQ, D = (2, 256, 192)
        E, H = (8, 768)
        CAPACITY = 2
        Bb, s, d = x.shape
        xf = x.reshape(-1, d)
        S = xf.shape[0]
        k = S * CAPACITY
        logits = xf @ gate_weight.T
        scores = jax.nn.softmax(logits, axis=-1).T
        vals, idx = jax.lax.top_k(scores.reshape(-1), k)
        gate = jnp.zeros((E * S,), dtype=x.dtype).at[idx].add(vals).reshape(E, S)
        h = jax.nn.gelu(jnp.einsum('sd,edh->esh', xf, w1) + b1[:, None, :], approximate=True)
        out = jnp.einsum('esh,ehd->esd', h, w2) + b2[:, None, :]
        y = jnp.einsum('es,esd->sd', gate, out)
        return y.reshape(Bb, s, d)
    h = _L0_tok_ref(x, L0_tok_conv_w, L0_tok_conv_b, L0_tok_ln1_g, L0_tok_ln1_b, L0_tok_qkv_w, L0_tok_out_w, L0_tok_out_b, L0_tok_ln2_g, L0_tok_ln2_b, L0_tok_ff1_w, L0_tok_ff1_b, L0_tok_ff2_w, L0_tok_ff2_b, L0_tok_lnf_g, L0_tok_lnf_b, L0_tok_head_w, L0_tok_head_b)
    h = jnp.concatenate([h, txt], axis=1)
    h = h + _L0_attn_ref(_layernorm(h, axis=-1), L0_attn_w_qkv, L0_attn_w_proj, L0_attn_b_proj)
    h = h + _L0_ffn_ref(_layernorm(h, axis=-1), L0_ffn_norm_w, L0_ffn_router_w, L0_ffn_gate_w, L0_ffn_up_w, L0_ffn_down_w)
    h = h + _L1_attn_ref(_layernorm(h, axis=-1), L1_attn_ln1_g, L1_attn_ln1_b, L1_attn_qw, L1_attn_qb, L1_attn_kw, L1_attn_kb, L1_attn_vw, L1_attn_vb, L1_attn_ln2_g, L1_attn_ln2_b, L1_attn_w1, L1_attn_b1, L1_attn_w2, L1_attn_b2)
    h = h + _L1_ffn_ref(_layernorm(h, axis=-1), L1_ffn_gate_weight, L1_ffn_w1, L1_ffn_b1, L1_ffn_w2, L1_ffn_b2)
    return h

_drawn_inputs = setup_inputs


def setup_inputs(seed=0):
    import zlib

    import numpy as np

    out = dict(_drawn_inputs(seed))
    spreads = {'L0_tok_conv_b': (0.0, 0.1),
     'L0_tok_ln1_g': (1.0, 0.6),
     'L0_tok_ln1_b': (0.0, 0.8),
     'L0_tok_out_b': (0.0, 0.1),
     'L0_tok_ln2_g': (1.0, 0.6),
     'L0_tok_ln2_b': (0.0, 0.595),
     'L0_tok_ff1_b': (0.0, 0.1),
     'L0_tok_ff2_b': (0.0, 0.1),
     'L0_tok_lnf_g': (1.0, 0.2),
     'L0_tok_lnf_b': (0.0, 0.1),
     'L0_tok_head_b': (0.0, 0.1),
     'L0_attn_b_proj': (0.0, 0.1),
     'L0_ffn_norm_w': (1.0, 0.2),
     'L1_attn_ln1_g': (1.0, 0.6),
     'L1_attn_ln1_b': (0.0, 0.659),
     'L1_attn_ln2_g': (1.0, 0.6),
     'L1_attn_ln2_b': (0.0, 0.666),
     'L1_attn_b1': (0.0, 0.1),
     'L1_attn_b2': (0.0, 0.1),
     'L1_ffn_b1': (0.0, 0.8),
     'L1_ffn_b2': (0.0, 0.8)}
    factors = {'L0_tok_qkv_w': 5.545,
     'L0_tok_out_w': 8.0,
     'L0_attn_w_qkv': 4.915,
     'L0_attn_w_proj': 4.599,
     'L1_attn_qw': 8.0,
     'L1_attn_qb': 47.306,
     'L1_attn_kw': 8.0,
     'L1_attn_kb': 64.0}
    for name, (base, spread) in spreads.items():
        noise = np.random.default_rng([zlib.crc32(name.encode()), seed]).standard_normal(out[name].shape)
        drawn = base * np.exp(spread * noise) if base else spread * noise
        out[name] = jnp.asarray(drawn.astype(out[name].dtype))
    for name, factor in factors.items():
        out[name] = (out[name] * factor).astype(out[name].dtype)
    return out
```

```python
from contextlib import ExitStack

import numpy as np

import concourse.bass as bass
from concourse import mybir

F32 = mybir.dt.float32
F32R = mybir.dt.float32r
I32 = mybir.dt.int32
ALU = mybir.AluOpType
ACT = mybir.ActivationFunctionType
AX = mybir.AxisListType

B = 2
D = 192
CH = (128, 64)
TILE = 96
NT = 3
TILES = B * NT
TOK = NT * TILE
IMG = 256
TXT = TOK - IMG

DT, T_LAYERS, T_HEADS, T_DH, T_FF = 128, 2, 8, 64, 512
INNER = T_HEADS * T_DH
PATCH_K = 32 * 8 * 8
PK = PATCH_K // 128
PATCH_LOADS = 4
T_ROWS = (TILE, TILE, IMG - 2 * TILE)
IC = INNER // 128
FC = T_FF // 128
HEADS, DH = 12, 16
E1, F1, F1C = 8, 384, 3
LAYERS, MLP, MLPC = 8, 768, 6
GROUPS = HEADS // 2
STACK = 64
SHIFT_ROW = 48
QUADS = 3
E2, H2, H2C = 8, 768, 6
CAPACITY = 2
PICKED = B * TOK * CAPACITY

C_CONVB = 0
C_T = 1
C_T_N = 4 + FC
C_LNF = C_T + T_LAYERS * C_T_N
C_NORMW = C_LNF + 2
C_MASK = C_NORMW + 2
C_N = C_MASK + 4
L_G1, L_B1, L_G2, L_B2 = 0, 2, 4, 6
L_MB = 8
L_BQ = L_MB + MLPC
L_N = L_BQ + 4 * GROUPS


def build(nc, a, out):
    ctx = ExitStack()

    def sb(name, shape, dt=F32):
        return ctx.enter_context(nc.sbuf_tensor(name, shape, dt))

    def sem(name):
        return ctx.enter_context(nc.semaphore(name))

    with ctx:
        bank = ctx.enter_context(nc.psum_tensor("bank", [128, 8, 512], F32))

        ident = sb("ident", [128, 128])
        ones = sb("ones", [128, 128])
        lower = sb("lower", [128, TILE])
        head64 = sb("head64", [128, 128])
        head16 = sb("head16", [128, 128])
        rank8 = sb("rank8", [TILE, 1, E1])
        minus_half = sb("minus_half", [TILE, TILES])
        eps5 = sb("eps5", [TILE, TILES])
        eps6 = sb("eps6", [TILE, TILES])
        carrier = sb("carrier", [1, 1])
        cols = sb("cols", [128, C_N])
        H = sb("H", [TILE, TILES, D])
        xn = sb("xn", [TILE, TILES, D])
        xT = sb("xT", [128, 2, B, TOK])
        stats = sb("stats", [TILE, TILES, 6])
        mv = sb("mv", [TILE, TILES, 2])
        veps = sb("veps", [TILE, TILES])
        rstd = sb("rstd", [TILE, TILES])

        consts_ready = sem("consts_ready")
        pool_const = sem("pool_const")
        masks_ready = sem("masks_ready")
        cols_in = sem("cols_in")
        link = sem("link")
        var_ready = sem("var_ready")
        rstd_ready = sem("rstd_ready")
        pool_step = sem("pool_step")
        normed = sem("normed")
        turned = sem("turned")
        xT_ready = sem("xT_ready")
        stored = sem("stored")

        NORM_T = 0
        NORM_A = 2 * T_LAYERS + 1
        NORM_M = NORM_A + 1
        NORM_R = NORM_M + 2
        NORM_L = NORM_R + 1
        NORM_E = NORM_L + 2 * LAYERS
        TURN_A = NORM_A
        def turn_base(n_tok, n_full):
            return n_tok * B + n_full * 2 * B

        n_link = [0]

        def linked(dve, ins):
            n_link[0] += 1
            ins.then_inc(link, 1)
            dve.wait_ge(link, n_link[0])

        def loop_linker(dve, signal, base):
            n = [0]

            def step(ins):
                n[0] += 1
                ins.then_inc(signal, 1)
                dve.wait_ge(signal, base + n[0])
            return step, n

        def norm_stats(dve, step, src, rows, norm, rms=False):
            for i in range(TILES):
                last = nc.vector.bn_stats(stats[0:rows[i % NT], i, :], src(i))
            step(last)
            nc.vector.memset(carrier[:, :], 0.0)
            for i in range(TILES):
                r = rows[i % NT]
                last = nc.vector.bn_aggr(mv[0:r, i, :], stats[0:r, i, :])
            if rms:
                step(last)
                step(nc.vector.tensor_tensor(veps[:, :], mv[:, :, 0], mv[:, :, 0], ALU.mult))
                step(nc.vector.tensor_tensor(mv[:, :, 1], mv[:, :, 1], veps[:, :], ALU.add))
                last = nc.vector.memset(mv[:, :, 0], 0.0)
            last.then_inc(var_ready, 1)

        def norm_rstd(pool, norm, eps, n_step):
            pool.wait_ge(var_ready, norm + 1)
            nc.gpsimd.tensor_tensor(veps[:, :], mv[:, :, 1], eps[:, :], ALU.add).then_inc(pool_step, 1)
            pool.wait_ge(pool_step, n_step + 1)
            nc.gpsimd.tensor_tensor(rstd[:, :], veps[:, :], minus_half[:, :], ALU.pow).then_inc(rstd_ready, 1)

        def norm_apply(dve, src, dst, rows, norm):
            dve.wait_ge(rstd_ready, norm + 1)
            for i in range(TILES):
                r = rows[i % NT]
                nc.vector.tensor_scalar(dst(i), src(i), mv[0:r, i, 0:1], rstd[0:r, i:i + 1],
                                        ALU.subtract, ALU.mult).then_inc(normed, 1)

        def turn(pe, src, rows, chunks, signal, base, first=4):
            for b in range(B):
                for c in range(chunks):
                    for j in range(NT):
                        i = b * NT + j
                        r = rows[j]
                        if c == 0:
                            pe.wait_ge(signal, base + i + 1)
                        last = nc.tensor.transpose(bank[0:CH[c], first + b * chunks + c, j * TILE:j * TILE + r],
                                                   src[0:r, i, c * 128:c * 128 + CH[c]], ident[0:r, 0:r])
                    last.then_inc(turned, 1)

        def turned_out(dve, tokens, chunks, base, gain=None, shift=None, first=4):
            for b in range(B):
                for c in range(chunks):
                    n = CH[c]
                    src = bank[0:n, first + b * chunks + c, 0:tokens]
                    dve.wait_ge(turned, base + b * chunks + c + 1)
                    if gain is None:
                        ins = nc.vector.tensor_copy(xT[0:n, c, b, 0:tokens], src)
                    elif shift is None:
                        ins = nc.vector.tensor_scalar(xT[0:n, c, b, 0:tokens], src, gain(c), None, ALU.mult)
                    else:
                        ins = nc.vector.tensor_scalar(xT[0:n, c, b, 0:tokens], src, gain(c), shift(c),
                                                      ALU.mult, ALU.add)
                    ins.then_inc(xT_ready, 1)

        full = (TILE,) * NT

        a_w = sb("a_w", [128, 2, 3 * D])
        a_proj_w = sb("a_proj_w", [128, 2, D])
        a_row = sb("a_row", [TILE, D])
        router_w = sb("router_w", [128, 2, E1])
        gate_up_w = sb("gate_up_w", [128, 2, 2 * F1])
        down_w = sb("down_w", [128, F1C, D])
        l_cols = sb("l_cols", [128, L_N])
        l_rows = sb("l_rows", [TILE, 2, D])
        l_qk_w = sb("l_qk_w", [128, 2, 2, 128])
        l_v_w = sb("l_v_w", [128, D])
        w1 = sb("w1", [128, 2, MLP])
        w2 = sb("w2", [128, MLPC, D])
        gate2_w = sb("gate2_w", [128, 2, E2])
        b2_rows = sb("b2_rows", [E2, D])
        b1_cols = sb("b1_cols", [128, E2, H2C])

        stage = ExitStack()

        def tb(name, shape, dt=F32):
            return stage.enter_context(nc.sbuf_tensor(name, shape, dt))

        patches = tb("patches", [128, PK, B * IMG])
        conv_w = tb("conv_w", [128, PK, DT])
        t_qkv_w = tb("t_qkv_w", [128, T_LAYERS, 3 * INNER])
        t_out_w = tb("t_out_w", [128, T_LAYERS, IC, DT])
        t_ff1_w = tb("t_ff1_w", [128, T_LAYERS, T_FF])
        t_ff2_w = tb("t_ff2_w", [128, T_LAYERS, FC, DT])
        t_head_w = tb("t_head_w", [128, D])
        t_rows = tb("t_rows", [TILE, T_LAYERS * 2 * DT + D])
        convT = tb("convT", [128, B, IMG])
        X = tb("X", [TILE, TILES, DT])
        tq = tb("tq", [TILE, TILES, INNER])
        tv = tb("tv", [TILE, TILES, INNER])
        tk = tb("tk", [TILE, TILES, INNER])
        tkT = tb("tkT", [128, IC, B, IMG])
        tqT = tb("tqT", [128, IC, B, IMG])
        tctx = tb("tctx", [128, B, IC, 128])
        tq_max = tb("tq_max", [TILE, TILES, T_HEADS])
        tq_sum = tb("tq_sum", [TILE, TILES, T_HEADS])
        tk_max = tb("tk_max", [128, IC, B])
        tk_sum = tb("tk_sum", [128, IC, B])
        tk_rec = tb("tk_rec", [128, IC, B])

        patches_in = [sem(f"patches_in{n}") for n in range(PATCH_LOADS)]
        t_w_in = [sem(f"t_w_in{n}") for n in range(3)]
        txt_in = sem("txt_in")
        conv_done = sem("conv_done")
        convT_ready = sem("convT_ready")
        x_turned = sem("x_turned")
        x_ready = sem("x_ready")
        tq_done = sem("tq_done")
        tv_done = sem("tv_done")
        tkT_done = sem("tkT_done")
        tv_copied = sem("tv_copied")
        tq_maxed = sem("tq_maxed")
        tq_exp = sem("tq_exp")
        tq_norm = sem("tq_norm")
        tk_maxed = sem("tk_maxed")
        tk_exp = sem("tk_exp")
        tk_turned = sem("tk_turned")
        tk_ready = sem("tk_ready")
        tq_turned = sem("tq_turned")
        tqT_ready = sem("tqT_ready")
        tctx_done = sem("tctx_done")
        tctx_ready = sem("tctx_ready")
        tatt_done = sem("tatt_done")
        tatt_ready = sem("tatt_ready")
        tproj_done = sem("tproj_done")
        x_attn = sem("x_attn")
        tff1_done = sem("tff1_done")
        tff1_act = sem("tff1_act")
        tff2_done = sem("tff2_done")
        head_done = sem("head_done")
        h_tok = sem("h_tok")

        def tok_tile(t, i):
            return t[0:T_ROWS[i % NT], i, :]

        def tokenizer_sync(sp):
            sp.dma_start(conv_w[:, :, :], a["conv_w"]).then_inc(patches_in[0], 16)
            n = PK // PATCH_LOADS
            for k in range(PATCH_LOADS):
                sp.dma_start(patches[:, k * n:(k + 1) * n, :], a["patches"][:, k * n:(k + 1) * n, :]).then_inc(patches_in[k], 16)
            sp.dma_start(t_qkv_w[:, :, :], a["t_qkv_w"]).then_inc(t_w_in[0], 16)
            sp.dma_start(t_out_w[:, :, :, :], a["t_out_w"]).then_inc(t_w_in[1], 16)
            sp.dma_start(t_rows[:, :], a["t_rows"].to_broadcast([TILE, T_LAYERS * 2 * DT + D])).then_inc(t_w_in[1], 16)
            sp.dma_start(t_ff1_w[:, :, :], a["t_ff1_w"]).then_inc(t_w_in[2], 16)
            sp.dma_start(t_ff2_w[:, :, :, :], a["t_ff2_w"]).then_inc(t_w_in[2], 16)
            sp.dma_start(t_head_w[:, :], a["t_head_w"]).then_inc(t_w_in[2], 16)
            for b in range(B):
                sp.dma_start(H[T_ROWS[2]:TILE, b * NT + 2, :], a["txt"][b]).then_inc(txt_in, 16)

        def tokenizer_tensor(pe):
            n = PK // PATCH_LOADS
            for k in range(PK):
                if k % n == 0:
                    pe.wait_ge(patches_in[k // n], 32 if k == 0 else 16)
                last = nc.tensor.matmul(bank[:, 0, :], conv_w[:, k, :], patches[:, k, :], start=(k == 0), stop=(k == PK - 1))
            last.then_inc(conv_done, 1)
            pe.wait_ge(consts_ready, 4)
            pe.wait_ge(convT_ready, 1)
            for b in range(B):
                for j in range(NT):
                    r = T_ROWS[j]
                    last = nc.tensor.transpose(bank[0:r, 1 + b, j * 128:(j + 1) * 128],
                                               convT[:, b, j * TILE:j * TILE + r], ident[:, :])
                last.then_inc(x_turned, 1)
            for l in range(T_LAYERS):
                turn(pe, xn, T_ROWS, 1, normed, 2 * l * TILES)
                pe.wait_ge(t_w_in[0], 16)
                for which, signal in ((0, tq_done), (2, tv_done)):
                    for i in range(TILES):
                        b, j = divmod(i, NT)
                        if i == 0 and which == 0:
                            pe.wait_ge(xT_ready, turn_base(2 * l, 0) + B)
                        if which == 0 and i >= 4:
                            pe.wait_ge(tq_maxed, l * TILES + i - 3)
                        if which == 2:
                            if i < 4:
                                pe.wait_ge(tq_maxed, l * TILES + min(i + 5, TILES) if i < 2 else l * TILES + i + 1)
                            else:
                                pe.wait_ge(tv_copied, l * TILES + i - 3)
                        nc.tensor.matmul(bank[0:T_ROWS[j], i % 4, :], xT[:, 0, b, j * TILE:j * TILE + T_ROWS[j]],
                                         t_qkv_w[:, l, which * INNER:(which + 1) * INNER],
                                         start=True, stop=True).then_inc(signal, 1)
                for c in range(IC):
                    nc.tensor.matmul(bank[:, 4 + c, :].rearrange("p (b n) -> p b n", b=B),
                                     t_qkv_w[:, l, INNER + c * 128:INNER + (c + 1) * 128],
                                     xT[:, 0, :, 0:IMG], start=True, stop=True).then_inc(tkT_done, 1)
                for i in range(TILES):
                    b, j = divmod(i, NT)
                    r = T_ROWS[j]
                    if i < 4:
                        pe.wait_ge(tv_copied, l * TILES + (i + 5 if i < 2 else i + 1))
                    else:
                        pe.wait_ge(tk_ready, l * TILES + i - 3)
                    for c in range(IC):
                        if j == 0:
                            pe.wait_ge(tk_exp, (l * B + b) * IC + c + 1)
                        last = nc.tensor.transpose(bank[0:r, i % 4, c * 128:(c + 1) * 128],
                                                   tkT[:, c, b, j * TILE:j * TILE + r], ident[:, :])
                    last.then_inc(tk_turned, 1)
                for c in range(IC):
                    if c == 0:
                        pe.wait_ge(tk_exp, (l + 1) * B * IC)
                        pe.wait_ge(tq_norm, (l + 1) * TILES)
                    for i in range(TILES):
                        b, j = divmod(i, NT)
                        r = T_ROWS[j]
                        last = nc.tensor.transpose(bank[:, 4 + c, b * IMG + j * TILE:b * IMG + j * TILE + r],
                                                   tq[0:r, i, c * 128:(c + 1) * 128], ident[0:r, 0:r])
                    last.then_inc(tq_turned, 1)
                pe.wait_ge(tk_ready, (l + 1) * TILES)
                for b in range(B):
                    for c in range(IC):
                        if b == 1:
                            pe.wait_ge(tctx_ready, l * B * IC + c + 1)
                        for j in range(NT):
                            i = b * NT + j
                            r = T_ROWS[j]
                            last = nc.tensor.matmul(bank[:, c, 0:128], tk[0:r, i, c * 128:(c + 1) * 128],
                                                    tv[0:r, i, c * 128:(c + 1) * 128], start=(j == 0), stop=(j == NT - 1))
                        last.then_inc(tctx_done, 1)
                for c in range(IC):
                    pe.wait_ge(tqT_ready, l * IC + c + 1)
                    pe.wait_ge(tctx_ready, l * B * IC + IC + c + 1)
                    for b in range(B):
                        last = nc.tensor.matmul(bank[:, 4 + c, b * IMG:(b + 1) * IMG], tctx[:, b, c, :], tqT[:, c, b, :],
                                                start=True, stop=True)
                    last.then_inc(tatt_done, 1)
                pe.wait_ge(t_w_in[1], 32)
                for i in range(TILES):
                    b, j = divmod(i, NT)
                    r = T_ROWS[j]
                    if i == 0:
                        pe.wait_ge(tatt_ready, (l + 1) * IC)
                    if i >= 4:
                        pe.wait_ge(x_attn, l * TILES + i - 3)
                    for c in range(IC):
                        last = nc.tensor.matmul(bank[0:r, i % 4, 0:DT], tqT[:, c, b, j * TILE:j * TILE + r],
                                                t_out_w[:, l, c, :], start=(c == 0), stop=(c == IC - 1))
                    last.then_inc(tproj_done, 1)
                turn(pe, xn, T_ROWS, 1, normed, (2 * l + 1) * TILES)
                pe.wait_ge(t_w_in[2], 48)
                pe.wait_ge(xT_ready, turn_base(2 * l + 1, 0) + B)
                for c in range(FC):
                    nc.tensor.matmul(bank[:, c, :].rearrange("p (b n) -> p b n", b=B), t_ff1_w[:, l, c * 128:(c + 1) * 128],
                                     xT[:, 0, :, 0:IMG], start=True, stop=True).then_inc(tff1_done, 1)
                for i in range(TILES):
                    b, j = divmod(i, NT)
                    r = T_ROWS[j]
                    if i == 0:
                        pe.wait_ge(tff1_act, (l + 1) * FC)
                    if i >= 2:
                        pe.wait_ge(x_ready, l * TILES + i - 1)
                    for c in range(FC):
                        last = nc.tensor.matmul(bank[0:r, 6 + i % 2, 0:DT], tqT[:, c, b, j * TILE:j * TILE + r],
                                                t_ff2_w[:, l, c, :], start=(c == 0), stop=(c == FC - 1))
                    last.then_inc(tff2_done, 1)
            turn(pe, xn, T_ROWS, 1, normed, 2 * T_LAYERS * TILES)
            pe.wait_ge(xT_ready, turn_base(2 * T_LAYERS, 0) + B)
            for i in range(TILES):
                b, j = divmod(i, NT)
                r = T_ROWS[j]
                if i >= 4:
                    pe.wait_ge(h_tok, i - 3)
                nc.tensor.matmul(bank[0:r, i % 4, 0:D], xT[:, 0, b, j * TILE:j * TILE + r], t_head_w[:, :],
                                 start=True, stop=True).then_inc(head_done, 1)

        def tokenizer_scalar(act):
            act.wait_ge(cols_in, 16)
            act.wait_ge(conv_done, 1)
            nc.scalar.activation(convT[:, :, :].rearrange("p b n -> p (b n)"), bank[:, 0, :], ACT.Identity,
                                 bias=cols[:, C_CONVB:C_CONVB + 1]).then_inc(convT_ready, 1)
            for l in range(T_LAYERS):
                c0 = C_T + l * C_T_N
                for i in range(TILES):
                    act.wait_ge(tq_maxed, l * TILES + i + 1)
                    nc.scalar.activation(tok_tile(tq, i), tok_tile(tq, i), ACT.Exp).then_inc(tq_exp, 1)
                for i in range(TILES):
                    act.wait_ge(tv_done, l * TILES + i + 1)
                    nc.scalar.activation(tok_tile(tv, i), bank[0:T_ROWS[i % NT], i % 4, :], ACT.Copy).then_inc(tv_copied, 1)
                for b in range(B):
                    for c in range(IC):
                        act.wait_ge(tk_maxed, l * IC + c + 1)
                        nc.scalar.activation(tkT[:, c, b, :], bank[:, 4 + c, b * IMG:(b + 1) * IMG], ACT.Exp,
                                             bias=tk_max[:, c, b:b + 1],
                                             accum_out=tk_sum[:, c, b:b + 1]).then_inc(tk_exp, 1)
                for i in range(TILES):
                    act.wait_ge(tk_turned, l * TILES + i + 1)
                    nc.scalar.activation(tok_tile(tk, i), bank[0:T_ROWS[i % NT], i % 4, :], ACT.Copy).then_inc(tk_ready, 1)
                for c in range(IC):
                    act.wait_ge(tq_turned, l * IC + c + 1)
                    nc.scalar.activation(tqT[:, c, :, :].rearrange("p b n -> p (b n)"), bank[:, 4 + c, :],
                                         ACT.Copy).then_inc(tqT_ready, 1)
                for c in range(IC):
                    act.wait_ge(tatt_done, l * IC + c + 1)
                    nc.scalar.activation(tqT[:, c, :, :].rearrange("p b n -> p (b n)"), bank[:, 4 + c, :],
                                         ACT.Copy).then_inc(tatt_ready, 1)
                for c in range(FC):
                    act.wait_ge(tff1_done, l * FC + c + 1)
                    nc.scalar.activation(tqT[:, c, :, :].rearrange("p b n -> p (b n)"), bank[:, c, :], ACT.Gelu,
                                         bias=cols[:, c0 + 4 + c:c0 + 5 + c]).then_inc(tff1_act, 1)

        def tokenizer_pool(pool):
            for n in range(2 * T_LAYERS + 1):
                norm_rstd(pool, n, eps5, n)

        def tokenizer_vector(dve):
            def step(ins):
                linked(dve, ins)
            step(nc.vector.memset(mv[:, :, :], 1.0))
            for b in range(B):
                dve.wait_ge(x_turned, b + 1)
                src = bank[:, 1 + b, :].rearrange("p (j n) -> p j n", n=128)
                nc.vector.tensor_copy(X[:, b * NT:b * NT + 2, :], src[0:TILE, 0:2, :])
                last = nc.vector.tensor_copy(X[0:T_ROWS[2], b * NT + 2, :], src[0:T_ROWS[2], 2, :])
            step(last)
            dve.wait_ge(t_w_in[1], 32)
            for l in range(T_LAYERS):
                c0 = C_T + l * C_T_N
                norm_stats(dve, step, lambda i: tok_tile(X, i), T_ROWS, 2 * l)
                norm_apply(dve, lambda i: tok_tile(X, i), lambda i: xn[0:T_ROWS[i % NT], i, 0:DT], T_ROWS, 2 * l)
                turned_out(dve, IMG, 1, turn_base(2 * l, 0), lambda c: cols[:, c0:c0 + 1], lambda c: cols[:, c0 + 1:c0 + 2])
                for i in range(TILES):
                    r = T_ROWS[i % NT]
                    dve.wait_ge(tq_done, l * TILES + i + 1)
                    q = bank[0:r, i % 4, :].rearrange("p (h d) -> p h d", h=T_HEADS)
                    step(nc.vector.tensor_reduce(tq_max[0:r, i, :], q, AX.X, ALU.max))
                    nc.vector.tensor_tensor(tok_tile(tq, i).rearrange("p (h d) -> p h d", h=T_HEADS), q,
                                            tq_max[0:r, i, :].unsqueeze(2).to_broadcast([r, T_HEADS, T_DH]),
                                            ALU.subtract).then_inc(tq_maxed, 1)
                for c in range(IC):
                    dve.wait_ge(tkT_done, l * IC + c + 1)
                    nc.vector.tensor_reduce(tk_max[:, c, :], bank[:, 4 + c, :].rearrange("p (b n) -> p b n", b=B),
                                            AX.X, ALU.max, negate=True).then_inc(tk_maxed, 1)
                for i in range(TILES):
                    r = T_ROWS[i % NT]
                    dve.wait_ge(tq_exp, l * TILES + i + 1)
                    q = tok_tile(tq, i).rearrange("p (h d) -> p h d", h=T_HEADS)
                    step(nc.vector.tensor_reduce(tq_max[0:r, i, :], q, AX.X, ALU.add))
                    step(nc.vector.reciprocal(tq_sum[0:r, i, :], tq_max[0:r, i, :]))
                    nc.vector.tensor_tensor(q, q, tq_sum[0:r, i, :].unsqueeze(2).to_broadcast([r, T_HEADS, T_DH]),
                                            ALU.mult).then_inc(tq_norm, 1)
                dve.wait_ge(tk_exp, (l + 1) * B * IC)
                step(nc.vector.reciprocal(tk_rec[:, :, :], tk_sum[:, :, :]))
                for b in range(B):
                    for c in range(IC):
                        dve.wait_ge(tctx_done, (l * B + b) * IC + c + 1)
                        nc.vector.scalar_tensor_tensor(tctx[:, b, c, :], bank[:, c, 0:128], tk_rec[:, c, b:b + 1],
                                                       head64[:, :], ALU.mult, ALU.mult).then_inc(tctx_ready, 1)
                rb = l * 2 * DT
                for i in range(TILES):
                    r = T_ROWS[i % NT]
                    last = nc.vector.tensor_tensor(tok_tile(X, i), tok_tile(X, i), t_rows[0:r, rb:rb + DT], ALU.add)
                step(last)
                for i in range(TILES):
                    r = T_ROWS[i % NT]
                    dve.wait_ge(tproj_done, l * TILES + i + 1)
                    last = nc.vector.tensor_tensor(tok_tile(X, i), tok_tile(X, i), bank[0:r, i % 4, 0:DT], ALU.add)
                    last.then_inc(x_attn, 1)
                dve.wait_ge(x_attn, (l + 1) * TILES)
                norm_stats(dve, step, lambda i: tok_tile(X, i), T_ROWS, 2 * l + 1)
                norm_apply(dve, lambda i: tok_tile(X, i), lambda i: xn[0:T_ROWS[i % NT], i, 0:DT], T_ROWS, 2 * l + 1)
                turned_out(dve, IMG, 1, turn_base(2 * l + 1, 0), lambda c: cols[:, c0 + 2:c0 + 3],
                           lambda c: cols[:, c0 + 3:c0 + 4])
                for i in range(TILES):
                    r = T_ROWS[i % NT]
                    last = nc.vector.tensor_tensor(tok_tile(X, i), tok_tile(X, i), t_rows[0:r, rb + DT:rb + 2 * DT], ALU.add)
                step(last)
                for i in range(TILES):
                    r = T_ROWS[i % NT]
                    dve.wait_ge(tff2_done, l * TILES + i + 1)
                    nc.vector.tensor_tensor(tok_tile(X, i), tok_tile(X, i), bank[0:r, 6 + i % 2, 0:DT],
                                            ALU.add).then_inc(x_ready, 1)
                dve.wait_ge(x_ready, (l + 1) * TILES)
            norm_stats(dve, step, lambda i: tok_tile(X, i), T_ROWS, 2 * T_LAYERS)
            norm_apply(dve, lambda i: tok_tile(X, i), lambda i: xn[0:T_ROWS[i % NT], i, 0:DT], T_ROWS, 2 * T_LAYERS)
            turned_out(dve, IMG, 1, turn_base(2 * T_LAYERS, 0), lambda c: cols[:, C_LNF:C_LNF + 1],
                       lambda c: cols[:, C_LNF + 1:C_LNF + 2])
            for i in range(TILES):
                r = T_ROWS[i % NT]
                dve.wait_ge(head_done, i + 1)
                nc.vector.tensor_tensor(H[0:r, i, :], bank[0:r, i % 4, 0:D], t_rows[0:r, T_LAYERS * 2 * DT:], ALU.add).then_inc(h_tok, 1)

        stage.close()
        later = ExitStack()

        def lb(name, shape, dt=F32):
            return later.enter_context(nc.sbuf_tensor(name, shape, dt))

        a_qT = lb("a_qT", [128, 2, B, TOK])
        a_kv = lb("a_kv", [TILE, TILES, 2 * D])
        a_kabs = lb("a_kabs", [TILE, TILES, D])
        a_qsum = lb("a_qsum", [128, 2, B])
        a_ksum = lb("a_ksum", [128, B, 2])
        a_rec = lb("a_rec", [128, B, 2])
        a_ctx = lb("a_ctx", [128, B, 2, 128])
        a_attT = lb("a_attT", [128, 2, B, TOK])
        m_in = lb("m_in", [TILE, TILES, D])
        m_prob = lb("m_prob", [TILE, E1, TILES])
        m_work = lb("m_work", [TILE, TILES, E1])
        m_pick = lb("m_pick", [TILE, TILES, E1])
        m_rest = lb("m_rest", [TILE, TILES, E1])
        m_p = lb("m_p", [TILE, TILES, E1])
        m_one = lb("m_one", [TILE, TILES])
        m_two = lb("m_two", [TILE, TILES])
        siluT = lb("siluT", [128, 2, B, TOK])
        hidT = lb("hidT", [128, MLPC, B, TOK])
        layer_tensors = ExitStack()

        def rb(name, shape, dt=F32):
            return layer_tensors.enter_context(nc.sbuf_tensor(name, shape, dt))

        R = rb("R", [TILE, TILES, D])
        q_stack = rb("q_stack", [128, GROUPS, B, TOK], F32R)
        k_stack = rb("k_stack", [128, GROUPS, B, TOK], F32R)
        stack_hi = rb("stack_hi", [128, 2, B, TOK], F32R)
        stack_lo = rb("stack_lo", [128, 2, B, TOK])
        shifts = rb("shifts", [TILE, TILES, HEADS * STACK])
        probs = rb("probs", [TILE, 6, 2, TOK])
        v_ext = rb("v_ext", [TILE, TILES, HEADS, 32])
        oT = rb("oT", [128, 2, TOK])
        o_rec = rb("o_rec", [TILE, NT, 4])
        o_tmp = rb("o_tmp", [TILE, NT, 4, DH])

        layer_tensors.close()

        a_in = sem("a_in")
        a_q_done = sem("a_q_done")
        a_kv_done = sem("a_kv_done")
        a_qT_ready = sem("a_qT_ready")
        a_kv_ready = sem("a_kv_ready")
        a_kabs_ready = sem("a_kabs_ready")
        a_ctx_done = sem("a_ctx_done")
        a_ctx_ready = sem("a_ctx_ready")
        a_att_done = sem("a_att_done")
        a_att_ready = sem("a_att_ready")
        a_proj_done = sem("a_proj_done")
        h_attn = sem("h_attn")

        def attn_sync(sp):
            sp.dma_start(a_w[:, 0, :], a["a_w"][0:128]).then_inc(a_in, 16)
            sp.dma_start(a_w[0:64, 1, :], a["a_w"][128:D]).then_inc(a_in, 16)
            sp.dma_start(a_proj_w[:, 0, :], a["a_proj_w"][0:128]).then_inc(a_in, 16)
            sp.dma_start(a_proj_w[0:64, 1, :], a["a_proj_w"][128:D]).then_inc(a_in, 16)
            sp.dma_start(a_row[:, :], a["a_row"].to_broadcast([TILE, D])).then_inc(a_in, 16)

        def two_chunks(out_ap, lhs, rhs):
            for c in range(2):
                last = nc.tensor.matmul(out_ap, lhs(c), rhs(c), start=(c == 0), stop=(c == 1))
            return last

        def attn_tensor(pe):
            turn(pe, xn, full, 2, normed, NORM_A * TILES)
            pe.wait_ge(a_in, 80)
            pe.wait_ge(xT_ready, turn_base(TURN_A, 1))
            for m in range(2):
                for b in range(B):
                    last = two_chunks(bank[0:CH[m], 2 * m + b, 0:TOK],
                                      lambda c: a_w[0:CH[c], c, m * 128:m * 128 + CH[m]],
                                      lambda c: xT[0:CH[c], c, b, :])
                last.then_inc(a_q_done, 1)
            for i in range(TILES):
                b, j = divmod(i, NT)
                if i >= 4:
                    pe.wait_ge(a_kv_ready, i - 3)
                two_chunks(bank[0:TILE, 4 + i % 4, 0:2 * D], lambda c: xT[0:CH[c], c, b, j * TILE:(j + 1) * TILE],
                           lambda c: a_w[0:CH[c], c, D:3 * D]).then_inc(a_kv_done, 1)
            for b in range(B):
                for m in range(2):
                    n = CH[m]
                    if b == 0:
                        pe.wait_ge(a_qT_ready, m + 1)
                    else:
                        pe.wait_ge(a_ctx_ready, m + 1)
                    pe.wait_ge(a_kabs_ready, (b + 1) * NT)
                    for j in range(NT):
                        i = b * NT + j
                        nc.tensor.matmul(bank[0:n, m, 0:n], a_kv[:, i, m * 128:m * 128 + n],
                                         a_kv[:, i, D + m * 128:D + m * 128 + n], start=(j == 0), stop=(j == NT - 1))
                    for j in range(NT):
                        last = nc.tensor.matmul(bank[0:n, m, 256:257], a_kabs[:, b * NT + j, m * 128:m * 128 + n],
                                                ones[0:TILE, 0:1], start=(j == 0), stop=(j == NT - 1))
                    last.then_inc(a_ctx_done, 1)
            for b in range(B):
                for m in range(2):
                    n = CH[m]
                    if b == 0 and m == 0:
                        pe.wait_ge(a_kv_ready, TILES)
                    pe.wait_ge(a_ctx_ready, b * 2 + m + 1)
                    nc.tensor.matmul(bank[0:n, 4 + b * 2 + m, 0:TOK], a_ctx[0:n, b, m, 0:n], a_qT[0:n, m, b, :],
                                     start=True, stop=True).then_inc(a_att_done, 1)
            for i in range(TILES):
                b, j = divmod(i, NT)
                pe.wait_ge(a_att_ready, 2 * (b + 1))
                if i >= 4:
                    pe.wait_ge(h_attn, i - 3)
                two_chunks(bank[0:TILE, i % 4, 0:D], lambda c: a_attT[0:CH[c], c, b, j * TILE:(j + 1) * TILE],
                           lambda c: a_proj_w[0:CH[c], c, :]).then_inc(a_proj_done, 1)

        def attn_scalar(act):
            for m in range(2):
                act.wait_ge(a_q_done, m + 1)
                nc.scalar.activation(a_qT[0:CH[m], m, :, :], bank[0:CH[m], 2 * m:2 * m + 2, 0:TOK],
                                     ACT.Copy).then_inc(a_qT_ready, 1)
            for i in range(TILES):
                act.wait_ge(a_kv_done, i + 1)
                nc.scalar.activation(a_kv[:, i, :], bank[0:TILE, 4 + i % 4, 0:2 * D], ACT.Copy).then_inc(a_kv_ready, 1)
            for b in range(B):
                for m in range(2):
                    act.wait_ge(a_att_done, b * 2 + m + 1)
                    nc.scalar.activation(a_attT[0:CH[m], m, b, :], bank[0:CH[m], 4 + b * 2 + m, 0:TOK],
                                         ACT.Copy).then_inc(a_att_ready, 1)

        def attn_vector(dve):
            def step(ins):
                linked(dve, ins)
            dve.wait_ge(txt_in, 16 * B)
            dve.wait_ge(h_tok, TILES)
            norm_stats(dve, step, lambda i: H[:, i, :], full, NORM_A)
            norm_apply(dve, lambda i: H[:, i, :], lambda i: xn[:, i, :], full, NORM_A)
            turned_out(dve, TOK, 2, turn_base(TURN_A, 0))
            dve.wait_ge(a_in, 80)
            step(nc.vector.tensor_tensor(H[:, :, :], H[:, :, :], a_row[:, :].unsqueeze(1).to_broadcast([TILE, TILES, D]), ALU.add))
            for i in range(TILES):
                dve.wait_ge(a_kv_ready, i + 1)
                nc.vector.scalar_tensor_tensor(a_kabs[:, i, :], a_kv[:, i, 0:D], -1.0, a_kv[:, i, 0:D],
                                               ALU.mult, ALU.max).then_inc(a_kabs_ready, 1)
            for m in range(2):
                n = CH[m]
                dve.wait_ge(a_qT_ready, m + 1)
                nc.vector.tensor_reduce(a_qsum[0:n, m, :], a_qT[0:n, m, :, :], AX.X, ALU.add, apply_absolute_value=True)
            for b in range(B):
                for m in range(2):
                    n = CH[m]
                    dve.wait_ge(a_ctx_done, b * 2 + m + 1)
                    step(nc.vector.tensor_scalar(a_ksum[0:n, b, m:m + 1], bank[0:n, m, 256:257], 1e-12, None, ALU.max))
                    step(nc.vector.tensor_scalar(a_qsum[0:n, m, b:b + 1], a_qsum[0:n, m, b:b + 1], 1e-12, None, ALU.max))
                    step(nc.vector.reciprocal(a_ksum[0:n, b, m:m + 1], a_ksum[0:n, b, m:m + 1]))
                    step(nc.vector.reciprocal(a_qsum[0:n, m, b:b + 1], a_qsum[0:n, m, b:b + 1]))
                    step(nc.vector.tensor_tensor(a_rec[0:n, b, m:m + 1], a_ksum[0:n, b, m:m + 1],
                                                 a_qsum[0:n, m, b:b + 1], ALU.mult))
                    nc.vector.scalar_tensor_tensor(a_ctx[0:n, b, m, 0:n], bank[0:n, m, 0:n], a_rec[0:n, b, m:m + 1],
                                                   head16[0:n, 0:n], ALU.mult, ALU.mult).then_inc(a_ctx_ready, 1)
            for i in range(TILES):
                dve.wait_ge(a_proj_done, i + 1)
                nc.vector.tensor_tensor(H[:, i, :], H[:, i, :], bank[0:TILE, i % 4, 0:D], ALU.add).then_inc(h_attn, 1)
            dve.wait_ge(h_attn, TILES)

        router_in = sem("router_in")
        gate_up_in = sem("gate_up_in")
        down_in = sem("down_in")
        router_done = sem("router_done")
        m_exp_in = sem("m_exp_in")
        m_exp_done = sem("m_exp_done")
        gate_done = sem("gate_done")
        up_done = sem("up_done")
        silu_done = sem("silu_done")
        mid_ready = sem("mid_ready")
        down_done = sem("down_done")
        m_added = sem("m_added")

        def load_gate_up(sp, e):
            sp.dma_start(gate_up_w[:, 0, :], a["gate_up_a"][e]).then_inc(gate_up_in, 16)
            sp.dma_start(gate_up_w[0:64, 1, :], a["gate_up_b"][e]).then_inc(gate_up_in, 16)

        def dyn(t, e):
            return t[bass.ds(e, 1)].squeeze(0)

        def mix_sync(sp):
            sp.dma_start(router_w[:, 0, :], a["router"][0:128]).then_inc(router_in, 16)
            sp.dma_start(router_w[0:64, 1, :], a["router"][128:D]).then_inc(router_in, 16)
            load_gate_up(sp, 0)
            sp.dma_start(down_w[:, :, :], a["down"][0]).then_inc(down_in, 16)

        def mix_sync_loop(sp):
            with sp.Fori(0, E1 - 1) as e:
                sp.wait_ge(up_done, e * F1C + F1C)
                sp.dma_start(gate_up_w[:, 0, :], a["gate_up_a"][bass.ds(e + 1, 1)].rearrange("e p n -> (e p) n")).then_inc(gate_up_in, 16)
                sp.dma_start(gate_up_w[0:64, 1, :], a["gate_up_b"][bass.ds(e + 1, 1)].rearrange("e p n -> (e p) n")).then_inc(gate_up_in, 16)
                sp.wait_ge(down_done, e * TILES + TILES)
                sp.dma_start(down_w[:, :, :], a["down"][bass.ds(e + 1, 1)].rearrange("e p c n -> (e p) c n")).then_inc(down_in, 16)

        def mix_tensor(pe):
            turn(pe, xn, full, 2, normed, (NORM_M + 1) * TILES)
            pe.wait_ge(router_in, 32)
            pe.wait_ge(xT_ready, turn_base(TURN_A, 2))
            for i in range(TILES):
                b, j = divmod(i, NT)
                last = two_chunks(bank[0:TILE, 6, i * E1:(i + 1) * E1], lambda c: xT[0:CH[c], c, b, j * TILE:(j + 1) * TILE],
                                  lambda c: router_w[0:CH[c], c, :])
            last.then_inc(router_done, 1)
            with pe.Fori(0, E1) as e:
                pe.wait_ge(gate_up_in, e * 32 + 32)
                for m in range(F1C):
                    for up, signal in ((0, gate_done), (1, up_done)):
                        u = 2 * m + up
                        if u == 3 or u == 5:
                            pe.wait_ge(silu_done, e * F1C + (u - 3) // 2 + 1)
                        if u == 4:
                            pe.wait_ge(mid_ready, e * F1C + 1)
                        for b in range(B):
                            last = two_chunks(bank[:, 2 * (u % 3) + b, 0:TOK],
                                              lambda c: gate_up_w[0:CH[c], c, up * F1 + m * 128:up * F1 + (m + 1) * 128],
                                              lambda c: xT[0:CH[c], c, b, :])
                        last.then_inc(signal, 1)
                pe.wait_ge(down_in, e * 16 + 16)
                pe.wait_ge(mid_ready, e * F1C + F1C)
                for i in range(TILES):
                    b, j = divmod(i, NT)
                    if i >= 2:
                        pe.wait_ge(m_added, e * TILES + i - 1)
                    for c in range(F1C):
                        last = nc.tensor.matmul(bank[0:TILE, 6 + i % 2, 0:D], hidT[:, c, b, j * TILE:(j + 1) * TILE],
                                                down_w[:, c, :], start=(c == 0), stop=(c == F1C - 1))
                    last.then_inc(down_done, 1)

        def mix_scalar(act):
            act.wait_ge(m_exp_in, 1)
            nc.scalar.activation(m_work[:, :, :], m_work[:, :, :], ACT.Exp).then_inc(m_exp_done, 1)
            with act.Fori(0, E1) as e:
                for m in range(F1C):
                    act.wait_ge(gate_done, e * F1C + m + 1)
                    if m >= 2:
                        act.wait_ge(mid_ready, e * F1C + m - 1)
                    nc.scalar.activation(siluT[:, m % 2, :, :], bank[:, 2 * (2 * m % 3):2 * (2 * m % 3) + 2, 0:TOK],
                                         ACT.Silu).then_inc(silu_done, 1)

        def mix_pool(pool):
            norm_rstd(pool, NORM_M, eps5, NORM_M)
            norm_rstd(pool, NORM_M + 1, eps6, NORM_M + 1)

        def softmax8(dve, step, logits, exp_in, exp_done, shape):
            step(nc.vector.tensor_reduce(m_one[:, :], logits, AX.X, ALU.max))
            nc.vector.tensor_tensor(m_work[:, :, :], logits, m_one[:, :].unsqueeze(2).to_broadcast(shape),
                                    ALU.subtract).then_inc(exp_in, 1)
            dve.wait_ge(exp_done, 1)
            step(nc.vector.tensor_reduce(m_one[:, :], m_work[:, :, :], AX.X, ALU.add))
            step(nc.vector.reciprocal(m_two[:, :], m_one[:, :]))
            step(nc.vector.tensor_tensor(m_p[:, :, :], m_work[:, :, :], m_two[:, :].unsqueeze(2).to_broadcast(shape), ALU.mult))

        def mix_vector(dve):
            def step(ins):
                linked(dve, ins)
            shape = [TILE, TILES, E1]
            norm_stats(dve, step, lambda i: H[:, i, :], full, NORM_M)
            norm_apply(dve, lambda i: H[:, i, :], lambda i: m_in[:, i, :], full, NORM_M)
            dve.wait_ge(normed, (NORM_M + 1) * TILES)
            norm_stats(dve, step, lambda i: m_in[:, i, :], full, NORM_M + 1, rms=True)
            norm_apply(dve, lambda i: m_in[:, i, :], lambda i: xn[:, i, :], full, NORM_M + 1)
            turned_out(dve, TOK, 2, turn_base(TURN_A, 1), lambda c: cols[0:CH[c], C_NORMW + c:C_NORMW + c + 1])
            step(nc.vector.tensor_tensor(H[:, :, :], H[:, :, :], m_in[:, :, :], ALU.add))
            dve.wait_ge(router_done, 1)
            softmax8(dve, step, bank[0:TILE, 6, 0:TILES * E1].rearrange("p (i e) -> p i e", e=E1), m_exp_in, m_exp_done,
                     shape)
            rank = rank8[:, :, :].to_broadcast(shape)

            def best(src, dst):
                step(nc.vector.tensor_reduce(m_one[:, :], src[:, :, :], AX.X, ALU.max))
                step(nc.vector.tensor_tensor(m_work[:, :, :], src[:, :, :], m_one[:, :].unsqueeze(2).to_broadcast(shape),
                                             ALU.is_equal))
                step(nc.vector.tensor_tensor(m_work[:, :, :], m_work[:, :, :], rank, ALU.mult))
                step(nc.vector.tensor_reduce(m_one[:, :], m_work[:, :, :], AX.X, ALU.max))
                step(nc.vector.tensor_tensor(dst[:, :, :], m_work[:, :, :], m_one[:, :].unsqueeze(2).to_broadcast(shape),
                                             ALU.is_equal))
            best(m_p, m_pick)
            step(nc.vector.scalar_tensor_tensor(m_rest[:, :, :], m_pick[:, :, :], -2.0, m_p[:, :, :], ALU.mult, ALU.add))
            best(m_rest, m_rest)
            step(nc.vector.tensor_tensor(m_pick[:, :, :], m_pick[:, :, :], m_rest[:, :, :], ALU.add))
            step(nc.vector.tensor_tensor(m_prob[:, :, :].rearrange("p e i -> p i e"), m_p[:, :, :], m_pick[:, :, :], ALU.mult))
            with dve.Fori(0, E1) as e:
                for m in range(F1C):
                    dve.wait_ge(silu_done, e * F1C + m + 1)
                    dve.wait_ge(up_done, e * F1C + m + 1)
                    s = 2 * ((2 * m + 1) % 3)
                    nc.vector.tensor_tensor(hidT[:, m, :, :], siluT[:, m % 2, :, :], bank[:, s:s + 2, 0:TOK],
                                            ALU.mult).then_inc(mid_ready, 1)
                for i in range(TILES):
                    dve.wait_ge(down_done, e * TILES + i + 1)
                    nc.vector.scalar_tensor_tensor(H[:, i, :], bank[0:TILE, 6 + i % 2, 0:D],
                                                   m_prob[:, bass.ds(e, 1), i:i + 1].rearrange("p e i -> p (e i)"), H[:, i, :],
                                                   ALU.mult, ALU.add).then_inc(m_added, 1)
            dve.wait_ge(m_added, E1 * TILES)

        l_qkv_in = sem("l_qkv_in")
        l_vec_in = sem("l_vec_in")
        w1_in = sem("w1_in")
        w2_in = sem("w2_in")
        v_preset = sem("v_preset")
        shifts_preset = sem("shifts_preset")
        layer_link = sem("layer_link")
        stack_done = sem("stack_done")
        stack_read = sem("stack_read")
        stack_ready = sem("stack_ready")
        v_done = sem("v_done")
        v_ready = sem("v_ready")
        row_scores = sem("row_scores")
        row_taken = sem("row_taken")
        scores_done = sem("scores_done")
        probs_ready = sem("probs_ready")
        pv_done = sem("pv_done")
        o_copied = sem("o_copied")
        o_turned = sem("o_turned")
        o_added = sem("o_added")
        up1_done = sem("up1_done")
        act1_ready = sem("act1_ready")
        down2_done = sem("down2_done")
        r_biased = sem("r_biased")
        r_ready = sem("r_ready")

        ROW_UNITS = NT * GROUPS + GROUPS // 2
        STEPS = QUADS * NT

        def one(name, n):
            t = a[name][bass.ds(n, 1)] if not isinstance(n, int) else a[name][n:n + 1]
            return t.rearrange("e p n -> (e p) n")

        def load_w1(sp, n):
            sp.dma_start(w1[:, 0, :], one("w1_a", n)).then_inc(w1_in, 16)
            sp.dma_start(w1[0:64, 1, :], one("w1_b", n)).then_inc(w1_in, 16)

        def load_w2(sp, n):
            sp.dma_start(w2[:, :, :].rearrange("p c n -> p (c n)"), one("w2", n)).then_inc(w2_in, 16)

        def load_qkv(sp, n):
            sp.dma_start(l_qk_w[:, 0, :, :].rearrange("p q n -> p (q n)"), one("qk_a", n)).then_inc(l_qkv_in, 16)
            sp.dma_start(l_qk_w[0:64, 1, :, :].rearrange("p q n -> p (q n)"), one("qk_b", n)).then_inc(l_qkv_in, 16)
            sp.dma_start(l_v_w[:, :], one("v_w", n)).then_inc(l_qkv_in, 16)

        def load_vectors(sp, n):
            sp.dma_start(l_cols[:, :], one("l_cols", n)).then_inc(l_vec_in, 16)
            sp.dma_start(l_rows[:, :, :].rearrange("p r n -> p (r n)"), one("l_rows", n).to_broadcast([TILE, 2 * D])).then_inc(l_vec_in, 16)

        def layers_sync(sp):
            load_qkv(sp, 0)
            load_vectors(sp, 0)
            load_w1(sp, 0)
            load_w2(sp, 0)

        def layers_sync_loop(sp):
            def mlp_loads(n):
                sp.wait_ge(up1_done, n * MLPC + MLPC)
                load_w1(sp, n + 1)

            with sp.Fori(0, LAYERS - 1) as n:
                sp.wait_ge(v_done, n * TILES + TILES)
                load_qkv(sp, n + 1)
                mlp_loads(n)
                sp.wait_ge(act1_ready, n * MLPC + MLPC)
                sp.wait_ge(r_biased, n + 1)
                load_vectors(sp, n + 1)
                sp.wait_ge(down2_done, n * TILES + TILES)
                load_w2(sp, n + 1)
            with sp.Fori(LAYERS - 1, LAYERS + E2 - 1) as n:
                mlp_loads(n)
                sp.wait_ge(down2_done, n * TILES + TILES)
                load_w2(sp, n + 1)

        def layers_tensor(pe):
            pe.wait_ge(v_preset, 2)
            with pe.Fori(0, LAYERS) as n:
                turn(pe, xn, full, 2, normed, (NORM_L + 2 * n) * TILES)
                pe.wait_ge(l_qkv_in, n * 48 + 48)
                pe.wait_ge(xT_ready, turn_base(TURN_A, 2) + n * 8 + 4)
                for g in range(GROUPS):
                    c, r = g // 4, 32 * (g % 4)
                    for which in range(2):
                        u = 2 * g + which
                        if u >= 4:
                            pe.wait_ge(stack_read, n * 2 * GROUPS + u - 3)
                        for b in range(B):
                            last = nc.tensor.matmul(bank[:, 2 * (u % 4) + b, 0:TOK], l_qk_w[r:r + 32, c, which, :],
                                                    xT[r:r + 32, c, b, :], start=True, stop=True)
                        last.then_inc(stack_done, 1)
                for i in range(TILES):
                    b, j = divmod(i, NT)
                    pe.wait_ge(stack_read, n * 2 * GROUPS + 9 + i // 2)
                    nc.tensor.matmul(bank[0:TILE, i, 0:128], xT[:, 0, b, j * TILE:(j + 1) * TILE], l_v_w[:, 0:128],
                                     start=True, stop=True)
                    nc.tensor.matmul(bank[0:TILE, i, 128:D], xT[0:64, 1, b, j * TILE:(j + 1) * TILE], l_v_w[0:64, 128:D],
                                     start=True, stop=True).then_inc(v_done, 1)
                for b in range(B):
                    for j in range(NT):
                        for g in range(GROUPS):
                            u = j * GROUPS + g
                            if b == 0 and u < 4:
                                pe.wait_ge(stack_ready, n * 2 * GROUPS + (2 * g + 2))
                                if u == 3:
                                    pe.wait_ge(stack_read, n * 2 * GROUPS + 12)
                                else:
                                    pe.wait_ge(v_ready, n * TILES + 2 * u + 2)
                            elif b == 0 and j == 0:
                                pe.wait_ge(stack_ready, n * 2 * GROUPS + (2 * g + 2))
                            U = b * ROW_UNITS + u
                            if U >= 4:
                                pe.wait_ge(row_taken, n * B * ROW_UNITS + U - 3)
                            for r in range(2):
                                rows = slice(STACK * r, STACK * r + STACK)
                                last = nc.tensor.matmul(bank[0:TILE, 2 * (U % 4) + r, 0:TOK],
                                                        q_stack[rows, g, b, j * TILE:(j + 1) * TILE],
                                                        k_stack[rows, g, b, :], start=True, stop=True)
                            last.then_inc(row_scores, 1)
                    for t in range(GROUPS // 2):
                        U = b * ROW_UNITS + NT * GROUPS + t
                        if t == 0:
                            pe.wait_ge(row_taken, n * B * ROW_UNITS + b * ROW_UNITS + NT * GROUPS)
                        for h in range(2):
                            g = 2 * t + h
                            for j in range(NT):
                                last = nc.tensor.transpose(bank[:, 2 * (U % 4) + h, j * TILE:(j + 1) * TILE],
                                                           shifts[:, b * NT + j, g * 128:(g + 1) * 128], ident[0:TILE, 0:TILE])
                        last.then_inc(row_scores, 1)

                def scores(b, k):
                    quad, t = divmod(k, NT)
                    for h in range(2):
                        u = (b * STEPS + k) * 2 + h
                        g = 2 * quad + h
                        if u == 0:
                            pe.wait_ge(row_taken, n * B * ROW_UNITS + B * ROW_UNITS)
                        if u >= 3:
                            pe.wait_ge(probs_ready, n * 4 * STEPS + u - 2)
                        for r in range(2):
                            rows = slice(STACK * r, STACK * r + STACK)
                            last = nc.tensor.matmul(bank[0:TILE, 2 * (u % 3) + r, 0:TOK],
                                                    k_stack[rows, g, b, t * TILE:(t + 1) * TILE],
                                                    q_stack[rows, g, b, :], start=True, stop=True)
                        last.then_inc(scores_done, 1)

                def values(b, k):
                    quad, t = divmod(k, NT)
                    o = b * QUADS + quad
                    if t == 0 and o >= 2:
                        pe.wait_ge(o_added, n * B * QUADS + o - 1)
                    pe.wait_ge(probs_ready, n * 4 * STEPS + (b * STEPS + k) * 2 + 2)
                    for r in range(4):
                        u = (b * STEPS + k) * 2 + r // 2
                        last = nc.tensor.matmul(bank[32 * r:32 * r + 32, 6 + o % 2, 0:TOK], v_ext[:, b * NT + t, 4 * quad + r, :],
                                                probs[:, u % 6, r % 2, :], start=(t == 0), stop=(t == NT - 1))
                    last.then_inc(pv_done, 1)

                def o_turn(o):
                    pe.wait_ge(o_copied, n * B * QUADS + o + 1)
                    for j in range(NT):
                        last = nc.tensor.transpose(bank[0:TILE, 6 + o % 2, j * 128:(j + 1) * 128],
                                                   oT[:, o % 2, j * TILE:(j + 1) * TILE], ident[:, :])
                    last.then_inc(o_turned, 1)

                steps = [(b, k) for b in range(B) for k in range(STEPS)]
                for s, (b, k) in enumerate(steps):
                    if s == 0:
                        scores(b, k)
                    if s + 1 < len(steps):
                        scores(*steps[s + 1])
                    values(b, k)
                    if s >= NT and s % NT == 1:
                        o_turn(s // NT - 1)
                o_turn(B * QUADS - 1)
                turn(pe, xn, full, 2, normed, (NORM_L + 2 * n + 1) * TILES)
                pe.wait_ge(xT_ready, turn_base(TURN_A, 2) + n * 8 + 8)
                mlp_tensor(pe, n)

        def mlp_tensor(pe, n):
            pe.wait_ge(w1_in, n * 32 + 32)
            for m in range(MLPC):
                if m == 3:
                    pe.wait_ge(act1_ready, n * MLPC + 1)
                if m >= 4:
                    pe.wait_ge(act1_ready, n * MLPC + m - 3)
                for b in range(B):
                    last = two_chunks(bank[:, 2 * (m % 4) + b, 0:TOK], lambda c: w1[0:CH[c], c, m * 128:(m + 1) * 128],
                                      lambda c: xT[0:CH[c], c, b, :])
                last.then_inc(up1_done, 1)
            pe.wait_ge(w2_in, n * 16 + 16)
            pe.wait_ge(act1_ready, n * MLPC + MLPC)
            for i in range(TILES):
                b, j = divmod(i, NT)
                for c in range(MLPC):
                    last = nc.tensor.matmul(bank[0:TILE, 2 + i, 0:D], hidT[:, c, b, j * TILE:(j + 1) * TILE], w2[:, c, :],
                                            start=(c == 0), stop=(c == MLPC - 1))
                last.then_inc(down2_done, 1)

        def layers_scalar(act):
            with act.Fori(0, LAYERS) as n:
                act.wait_ge(l_vec_in, n * 32 + 32)
                for g in range(GROUPS):
                    for which in range(2):
                        u = 2 * g + which
                        bq = L_BQ + 2 * GROUPS * which + g
                        act.wait_ge(stack_done, n * 2 * GROUPS + u + 1)
                        if u >= 2:
                            act.wait_ge(stack_ready, n * 2 * GROUPS + u - 1)
                        src = bank[:, 2 * (u % 4):2 * (u % 4) + 2, 0:TOK]
                        nc.scalar.activation(stack_hi[:, u % 2, :, :], src, ACT.Identity, bias=l_cols[:, bq:bq + 1])
                        nc.scalar.activation(stack_lo[:, u % 2, :, :], src, ACT.Identity, bias=l_cols[:, bq + GROUPS:bq + GROUPS + 1],
                                             scale=cols[:, C_MASK + 2 * which:C_MASK + 2 * which + 1]).then_inc(stack_read, 1)
                for u in range(4 * STEPS):
                    act.wait_ge(scores_done, n * 4 * STEPS + u + 1)
                    if u >= 6:
                        act.wait_ge(pv_done, n * 2 * STEPS + (u - 6) // 2 + 1)
                    nc.scalar.activation(probs[:, u % 6, :, :], bank[0:TILE, 2 * (u % 3):2 * (u % 3) + 2, 0:TOK], ACT.Exp,
                                         scale=float(DH) ** -0.5).then_inc(probs_ready, 1)
                for m in range(MLPC):
                    act.wait_ge(up1_done, n * MLPC + m + 1)
                    nc.scalar.activation(hidT[:, m, :, :], bank[:, 2 * (m % 4):2 * (m % 4) + 2, 0:TOK], ACT.Gelu,
                                         bias=l_cols[:, L_MB + m:L_MB + m + 1]).then_inc(act1_ready, 1)

        def layers_pool(pool):
            norm_rstd(pool, NORM_R, eps5, NORM_R)
            with pool.Fori(0, LAYERS) as n:
                norm_rstd(pool, NORM_L + 2 * n, eps5, NORM_L + 2 * n)
                norm_rstd(pool, NORM_L + 2 * n + 1, eps5, NORM_L + 2 * n + 1)

        def layers_vector(dve):
            def step0(ins):
                linked(dve, ins)
            nc.vector.memset(shifts[:, :, :], 0.0).then_inc(v_preset, 1)
            nc.vector.memset(v_ext[:, :, :, DH + 1:32], 0.0)
            nc.vector.memset(v_ext[:, :, :, DH:DH + 1], 1.0).then_inc(v_preset, 1)
            norm_stats(dve, step0, lambda i: H[:, i, :], full, NORM_R)
            norm_apply(dve, lambda i: H[:, i, :], lambda i: R[:, i, :], full, NORM_R)
            dve.wait_ge(normed, (NORM_R + 1) * TILES)
            with dve.Fori(0, LAYERS) as n:
                step, counted = loop_linker(dve, layer_link, n * LINKS)
                norm = NORM_L + 2 * n
                norm_stats(dve, step, lambda i: R[:, i, :], full, norm)
                norm_apply(dve, lambda i: R[:, i, :], lambda i: xn[:, i, :], full, norm)
                dve.wait_ge(l_vec_in, n * 32 + 32)
                turned_out(dve, TOK, 2, turn_base(TURN_A, 2) + n * 8, lambda c: l_cols[0:CH[c], L_G1 + c:L_G1 + c + 1],
                           lambda c: l_cols[0:CH[c], L_B1 + c:L_B1 + c + 1])
                for g in range(GROUPS):
                    for which, stack in ((0, q_stack), (1, k_stack)):
                        u = 2 * g + which
                        dve.wait_ge(stack_read, n * 2 * GROUPS + u + 1)
                        f = C_MASK + 2 * which + 1
                        nc.vector.scalar_tensor_tensor(stack[:, g, :, :], stack_hi[:, u % 2, :, :].bitcast(F32), cols[:, f:f + 1],
                                                       stack_lo[:, u % 2, :, :], ALU.mult, ALU.add).then_inc(stack_ready, 1)
                for i in range(TILES):
                    dve.wait_ge(v_done, n * TILES + i + 1)
                    nc.vector.tensor_tensor(v_ext[:, i, :, 0:DH], bank[0:TILE, i, 0:D].rearrange("p (h d) -> p h d", d=DH),
                                            l_rows[:, 0, :].rearrange("p (h d) -> p h d", d=DH), ALU.add).then_inc(v_ready, 1)
                for b in range(B):
                    for j in range(NT):
                        for g in range(GROUPS):
                            U = b * ROW_UNITS + j * GROUPS + g
                            dve.wait_ge(row_scores, n * B * ROW_UNITS + U + 1)
                            col = g * 128 + SHIFT_ROW
                            nc.vector.tensor_reduce(shifts[:, b * NT + j, col:col + STACK + 1:STACK],
                                                    bank[0:TILE, 2 * (U % 4):2 * (U % 4) + 2, 0:TOK], AX.X, ALU.max,
                                                    negate=True).then_inc(row_taken, 1)
                    for t in range(GROUPS // 2):
                        U = b * ROW_UNITS + NT * GROUPS + t
                        dve.wait_ge(row_scores, n * B * ROW_UNITS + U + 1)
                        q = q_stack[:, 2 * t:2 * t + 2, b, :]
                        nc.vector.tensor_tensor(q, q.bitcast(F32), bank[:, 2 * (U % 4):2 * (U % 4) + 2, 0:TOK],
                                                ALU.add).then_inc(row_taken, 1)
                for o in range(B * QUADS):
                    b, quad = divmod(o, QUADS)
                    dve.wait_ge(pv_done, n * 2 * STEPS + (o + 1) * NT)
                    nc.vector.tensor_copy(oT[:, o % 2, :], bank[:, 6 + o % 2, 0:TOK]).then_inc(o_copied, 1)
                    dve.wait_ge(o_turned, n * B * QUADS + o + 1)
                    src = bank[0:TILE, 6 + o % 2, 0:NT * 128].rearrange("p (j h d) -> p j h d", j=NT, d=32)
                    step(nc.vector.reciprocal(o_rec[:, :, :], src[:, :, :, DH]))
                    step(nc.vector.tensor_tensor(o_tmp[:, :, :, :], src[:, :, :, 0:DH],
                                                 o_rec[:, :, :].unsqueeze(3).to_broadcast([TILE, NT, 4, DH]), ALU.mult))
                    dst = R[:, b * NT:(b + 1) * NT, quad * 64:(quad + 1) * 64].rearrange("p j (h d) -> p j h d", d=DH)
                    nc.vector.tensor_tensor(dst, dst, o_tmp[:, :, :, :], ALU.add).then_inc(o_added, 1)
                dve.wait_ge(o_added, n * B * QUADS + B * QUADS)
                norm_stats(dve, step, lambda i: R[:, i, :], full, norm + 1)
                norm_apply(dve, lambda i: R[:, i, :], lambda i: xn[:, i, :], full, norm + 1)
                turned_out(dve, TOK, 2, turn_base(TURN_A, 2) + n * 8 + 4, lambda c: l_cols[0:CH[c], L_G2 + c:L_G2 + c + 1],
                           lambda c: l_cols[0:CH[c], L_B2 + c:L_B2 + c + 1])
                nc.vector.tensor_tensor(R[:, :, :], R[:, :, :], l_rows[:, 1, :].unsqueeze(1).to_broadcast([TILE, TILES, D]),
                                        ALU.add).then_inc(r_biased, 1)
                dve.wait_ge(r_biased, n + 1)
                for i in range(TILES):
                    dve.wait_ge(down2_done, n * TILES + i + 1)
                    nc.vector.tensor_tensor(R[:, i, :], R[:, i, :], bank[0:TILE, 2 + i, 0:D], ALU.add).then_inc(r_ready, 1)
                dve.wait_ge(r_ready, n * TILES + TILES)
            assert counted[0] == LINKS, counted
            nc.vector.tensor_tensor(H[:, :, :], H[:, :, :], R[:, :, :], ALU.add).then_inc(h_layers, 1)
            dve.wait_ge(h_layers, 1)

        LINKS = 2 + 2 * B * QUADS
        h_layers = sem("h_layers")

        raw = lb("raw", [TILE, E2, TILES, D])
        s_score = lb("s_score", [TILE, E2, TILES])
        s_mark = lb("s_mark", [TILE, E2, TILES])
        s_above = lb("s_above", [TILE, E2, TILES])
        s_rank = lb("s_rank", [TILE, E2, TILES])
        s_zero = lb("s_zero", [TILE, E2 * TILES])
        s_gate = lb("s_gate", [TILE, E2, TILES])
        s_least = lb("s_least", [TILE, 1])
        s_try = lb("s_try", [TILE, 1])
        s_ok = lb("s_ok", [TILE, 1])
        s_count = lb("s_count", [TILE, 1])
        s_total = lb("s_total", [TILE, 1])
        s_gateT = lb("s_gateT", [E2, B, TOK])

        g_in = sem("g_in")
        g_logits = sem("g_logits")
        g_exp_in = sem("g_exp_in")
        g_exp_done = sem("g_exp_done")
        bits_counted = sem("bits_counted")
        bits_total = sem("bits_total")
        ties_marked = sem("ties_marked")
        ties_ranked = sem("ties_ranked")
        gate_ready = sem("gate_ready")
        gate_turned = sem("gate_turned")
        gateT_ready = sem("gateT_ready")
        bias_done = sem("bias_done")
        raw_ready = sem("raw_ready")
        y_ready = sem("y_ready")
        y_added = sem("y_added")
        search_link = sem("search_link")

        BITS = 30
        EARLY = 5

        def mix2_sync(sp):
            sp.dma_start(gate2_w[:, 0, :], a["gate2"][0:128]).then_inc(g_in, 16)
            sp.dma_start(gate2_w[0:64, 1, :], a["gate2"][128:D]).then_inc(g_in, 16)
            sp.dma_start(b2_rows[:, :], a["mix_b2"]).then_inc(g_in, 16)
            sp.dma_start(b1_cols[:, :, :], a["mix_b1"]).then_inc(g_in, 16)

        def mix2_store(sp):
            for b in range(B):
                sp.wait_ge(y_ready, (b + 1) * NT)
                sp.dma_start(out[b].rearrange("(j p) d -> p j d", p=TILE), H[:, b * NT:(b + 1) * NT, :]).then_inc(stored, 16)
            sp.wait_ge(stored, 16 * B)

        def mix2_tensor(pe):
            turn(pe, xn, full, 2, normed, NORM_E * TILES)
            pe.wait_ge(g_in, 64)
            pe.wait_ge(xT_ready, turn_base(TURN_A, 3) + LAYERS * 8)
            for i in range(TILES):
                b, j = divmod(i, NT)
                last = two_chunks(bank[0:TILE, 0, i * E2:(i + 1) * E2], lambda c: xT[0:CH[c], c, b, j * TILE:(j + 1) * TILE],
                                  lambda c: gate2_w[0:CH[c], c, :])
            last.then_inc(g_logits, 1)
            pe.wait_ge(g_exp_in, 1)

            def experts(first, end):
                with pe.Fori(first, end) as e:
                    mlp_tensor(pe, LAYERS + e)
                    pe.wait_ge(raw_ready, e * TILES + 4)
            experts(0, EARLY)
            pe.wait_ge(raw_ready, EARLY * TILES)
            pe.wait_ge(ties_marked, 1)
            mark = s_mark[:, :, :].rearrange("p e i -> p (e i)")
            nc.tensor.matmul(bank[0:TILE, 0, 0:E2 * TILES], lower[0:TILE, :], mark, start=True, stop=True)
            nc.tensor.matmul(bank[0:TILE, 1, 0:E2 * TILES], ones[0:TILE, 0:TILE], mark, start=True, stop=True).then_inc(ties_ranked, 1)
            pe.wait_ge(gate_ready, 1)
            for i in range(TILES):
                last = nc.tensor.transpose(bank[0:E2, 2 + i // NT, (i % NT) * TILE:(i % NT + 1) * TILE], s_gate[:, :, i],
                                           ident[0:TILE, 0:TILE])
            last.then_inc(gate_turned, 1)
            pe.wait_ge(gateT_ready, 1)
            experts(EARLY, E2)
            pe.wait_ge(raw_ready, E2 * TILES)
            for i in range(TILES):
                b, j = divmod(i, NT)
                nc.tensor.matmul(bank[0:TILE, i, 0:D], s_gateT[:, b, j * TILE:(j + 1) * TILE], b2_rows[:, :],
                                 start=True, stop=True).then_inc(bias_done, 1)

        def mix2_scalar(act):
            act.wait_ge(g_exp_in, 1)
            nc.scalar.activation(m_work[:, :, :], m_work[:, :, :], ACT.Exp).then_inc(g_exp_done, 1)
            act.wait_ge(g_in, 64)
            with act.Fori(0, E2) as e:
                for m in range(MLPC):
                    act.wait_ge(up1_done, (e + LAYERS) * MLPC + m + 1)
                    nc.scalar.activation(hidT[:, m, :, :], bank[:, 2 * (m % 4):2 * (m % 4) + 2, 0:TOK], ACT.Gelu_apprx_tanh,
                                         bias=b1_cols[:, bass.ds(e, 1), m:m + 1].rearrange("p e m -> p (e m)")).then_inc(act1_ready, 1)
                for i in range(TILES):
                    act.wait_ge(down2_done, (e + LAYERS) * TILES + i + 1)
                    nc.scalar.activation(raw[:, bass.ds(e, 1), i, :].rearrange("p e d -> p (e d)"), bank[0:TILE, 2 + i, 0:D],
                                         ACT.Copy).then_inc(raw_ready, 1)

        def mix2_pool(pool):
            norm_rstd(pool, NORM_E, eps5, NORM_E)
            for t in range(BITS):
                pool.wait_ge(bits_counted, t + 1)
                nc.gpsimd.partition_all_reduce(s_total[:, :], s_count[:, :], TILE, bass.bass_isa.ReduceOp.add).then_inc(bits_total, 1)
            pool.wait_ge(bits_counted, BITS + 1)
            nc.gpsimd.partition_all_reduce(s_total[:, :], s_count[:, :], TILE, bass.bass_isa.ReduceOp.add).then_inc(bits_total, 1)

        def mix2_vector(dve):
            def step(ins):
                linked(dve, ins)
            shape = [TILE, TILES, E2]
            norm_stats(dve, step, lambda i: H[:, i, :], full, NORM_E)
            norm_apply(dve, lambda i: H[:, i, :], lambda i: xn[:, i, :], full, NORM_E)
            turned_out(dve, TOK, 2, turn_base(TURN_A, 2) + LAYERS * 8)
            dve.wait_ge(g_logits, 1)
            softmax8(dve, step, bank[0:TILE, 0, 0:TILES * E2].rearrange("p (i e) -> p i e", e=E2), g_exp_in, g_exp_done,
                     shape)
            step(nc.vector.tensor_copy(s_score[:, :, :].rearrange("p e i -> p i e"), m_p[:, :, :]))
            nc.vector.memset(s_zero[:, :], 0.0)
            step(nc.vector.memset(s_least[:, :], 0.0))
            score = s_score[:, :, :].rearrange("p e i -> p (e i)")
            markf = s_mark[:, :, :].rearrange("p e i -> p (e i)")
            above = s_above[:, :, :].rearrange("p e i -> p (e i)")
            for t in range(BITS):
                step(nc.vector.tensor_scalar(s_try[:, :].bitcast(I32), s_least[:, :].bitcast(I32), 1 << (BITS - 1 - t), None,
                                             ALU.bitwise_or))
                nc.vector.tensor_scalar(markf, score, s_try[:, 0:1], None, ALU.is_ge, ALU.add,
                                        accum_out=s_count[:, :]).then_inc(bits_counted, 1)
                dve.wait_ge(bits_total, t + 1)
                step(nc.vector.tensor_scalar(s_ok[:, :], s_total[:, :], float(PICKED), s_try[:, 0:1], ALU.is_ge, ALU.mult))
                step(nc.vector.tensor_tensor(s_least[:, :], s_least[:, :], s_ok[:, :], ALU.max))
            nc.vector.tensor_scalar(above, score, s_least[:, 0:1], None, ALU.is_gt, ALU.add,
                                    accum_out=s_count[:, :]).then_inc(bits_counted, 1)
            nc.vector.tensor_scalar(markf, score, s_least[:, 0:1], None, ALU.is_equal).then_inc(ties_marked, 1)
            dve.wait_ge(ties_ranked, 1)
            dve.wait_ge(bits_total, BITS + 1)
            step(nc.vector.tensor_scalar(s_ok[:, :], s_total[:, :], -1.0, float(PICKED), ALU.mult, ALU.add))
            rank = s_rank[:, :, :].rearrange("p e i -> p (e i)")
            step(nc.vector.tensor_copy(s_gate[:, :, :].rearrange("p e i -> p (e i)"), bank[0:TILE, 1, 0:E2 * TILES]))
            gate = s_gate[:, :, :].rearrange("p e i -> p (e i)")
            step(nc.vector.tensor_tensor_scan(rank, gate, s_zero[:, :], 0.0, ALU.add, ALU.add))
            step(nc.vector.tensor_tensor(rank, rank, gate, ALU.subtract))
            step(nc.vector.tensor_tensor(rank, rank, bank[0:TILE, 0, 0:E2 * TILES], ALU.add))
            step(nc.vector.scalar_tensor_tensor(rank, rank, s_ok[:, 0:1], markf, ALU.is_lt, ALU.mult))
            step(nc.vector.tensor_tensor(rank, rank, above, ALU.add))
            nc.vector.tensor_tensor(gate, rank, score, ALU.mult).then_inc(gate_ready, 1)
            dve.wait_ge(gate_turned, 1)
            nc.vector.tensor_copy(s_gateT[:, :, :], bank[0:E2, 2:4, 0:TOK]).then_inc(gateT_ready, 1)
            dve.wait_ge(gate_ready, 1)
            with dve.Fori(0, E2) as e:
                for i in range(TILES):
                    dve.wait_ge(raw_ready, e * TILES + i + 1)
                    nc.vector.scalar_tensor_tensor(H[:, i, :], raw[:, bass.ds(e, 1), i, :].rearrange("p e d -> p (e d)"),
                                                   s_gate[:, bass.ds(e, 1), i:i + 1].rearrange("p e i -> p (e i)"), H[:, i, :],
                                                   ALU.mult, ALU.add).then_inc(y_added, 1)
                dve.wait_ge(y_added, e * TILES + TILES)
            for i in range(TILES):
                dve.wait_ge(bias_done, i + 1)
                nc.vector.tensor_tensor(H[:, i, :], H[:, i, :], bank[0:TILE, i, 0:D], ALU.add).then_inc(y_ready, 1)

        later.close()

        block = ctx.enter_context(nc.Block())

        @block.sync
        def _(sp):
            sp.dma_start(cols[:, :], a["cols"]).then_inc(cols_in, 16)
            tokenizer_sync(sp)
            attn_sync(sp)
            mix_sync(sp)
            layers_sync(sp)
            mix2_sync(sp)
            mix_sync_loop(sp)
            layers_sync_loop(sp)
            mix2_store(sp)

        @block.gpsimd
        def _(pool):
            nc.gpsimd.memset(minus_half[:, :], -0.5)
            nc.gpsimd.memset(eps5[:, :], 1e-5)
            nc.gpsimd.memset(eps6[:, :], 1e-6)
            nc.gpsimd.memset(ident[:, :], 0.0)
            nc.gpsimd.memset(ones[:, :], 1.0)
            nc.gpsimd.memset(lower[:, :], 1.0)
            nc.gpsimd.memset(head64[:, :], float(T_DH) ** -0.5)
            nc.gpsimd.memset(head16[:, :], 1.0).then_inc(pool_const, 1)
            pool.wait_ge(pool_const, 1)
            nc.gpsimd.affine_select(out=ident[:, :], in_=ident[:, :], compare_op=ALU.not_equal, fill=1.0, base=0,
                                    pattern=[[-1, 128]], channel_multiplier=1).then_inc(consts_ready, 4)
            nc.gpsimd.affine_select(out=lower[:, :], in_=lower[:, :], compare_op=ALU.is_gt, fill=0.0, base=0,
                                    pattern=[[1, TILE]], channel_multiplier=-1).then_inc(pool_const, 1)
            n = 2
            for mask, width in ((head64, T_DH), (head16, DH)):
                view = mask[:, :].rearrange("p (h d) -> p h d", d=width)
                nc.gpsimd.affine_select(out=view, in_=view, compare_op=ALU.is_ge, fill=0.0, base=0,
                                        pattern=[[-width, 128 // width], [0, width]], channel_multiplier=1).then_inc(pool_const, 1)
                n += 1
                pool.wait_ge(pool_const, n)
                nc.gpsimd.affine_select(out=view, in_=view, compare_op=ALU.is_ge, fill=0.0, base=width - 1,
                                        pattern=[[width, 128 // width], [0, width]], channel_multiplier=-1).then_inc(pool_const, 1)
                n += 1
                pool.wait_ge(pool_const, n)
            nc.gpsimd.iota(rank8[:, 0, :], pattern=[[-1, E1]], base=E1, channel_multiplier=0,
                           allow_small_or_imprecise_dtypes=True).then_inc(masks_ready, 1)
            tokenizer_pool(pool)
            norm_rstd(pool, NORM_A, eps5, NORM_A)
            mix_pool(pool)
            layers_pool(pool)
            mix2_pool(pool)

        @block.tensor
        def _(pe):
            tokenizer_tensor(pe)
            attn_tensor(pe)
            mix_tensor(pe)
            layers_tensor(pe)
            mix2_tensor(pe)

        @block.scalar
        def _(act):
            tokenizer_scalar(act)
            attn_scalar(act)
            mix_scalar(act)
            layers_scalar(act)
            mix2_scalar(act)

        @block.vector
        def _(dve):
            dve.wait_ge(cols_in, 16)
            dve.wait_ge(masks_ready, 1)
            tokenizer_vector(dve)
            attn_vector(dve)
            mix_vector(dve)
            layers_vector(dve)
            mix2_vector(dve)


def layout(x):
    f = lambda n: np.asarray(x[n])
    rows = lambda m, n=128: np.ascontiguousarray(m.reshape(-1, n, m.shape[-1]).transpose(1, 0, 2))
    col = lambda v: np.pad(v.reshape(-1, 1), ((0, 128 - v.size), (0, 0)))
    cut = lambda v: [col(v[k:k + 128]) for k in range(0, v.size, 128)]
    p = {}
    im = f("x").reshape(B, 32, 16, 8, 16, 8).transpose(1, 3, 5, 0, 2, 4).reshape(PATCH_K, B * IMG)
    p["patches"] = rows(im)
    p["conv_w"] = rows(f("L0_tok_conv_w").transpose(1, 2, 3, 0).reshape(PATCH_K, DT))
    p["t_qkv_w"] = f("L0_tok_qkv_w").transpose(1, 0, 2)
    p["t_out_w"] = f("L0_tok_out_w").reshape(T_LAYERS, IC, 128, DT).transpose(2, 0, 1, 3)
    p["t_ff1_w"] = f("L0_tok_ff1_w").transpose(1, 0, 2)
    p["t_ff2_w"] = f("L0_tok_ff2_w").reshape(T_LAYERS, FC, 128, DT).transpose(2, 0, 1, 3)
    p["t_head_w"] = f("L0_tok_head_w")
    p["t_rows"] = np.concatenate([v for l in range(T_LAYERS) for v in (f("L0_tok_out_b")[l], f("L0_tok_ff2_b")[l])]
                                 + [f("L0_tok_head_b")])[None]
    p["txt"] = f("txt")
    c = cut(f("L0_tok_conv_b"))
    for l in range(T_LAYERS):
        for n in ("ln1_g", "ln1_b", "ln2_g", "ln2_b", "ff1_b"):
            c += cut(f("L0_tok_" + n)[l])
    c += cut(f("L0_tok_lnf_g")) + cut(f("L0_tok_lnf_b")) + cut(f("L0_ffn_norm_w"))
    parts = np.zeros((128, 4), np.float32)
    for h in (0, STACK):
        parts[h:h + SHIFT_ROW, 1] = parts[h:h + SHIFT_ROW, 3] = 1
        parts[h + 32:h + 48, 0], parts[h + 32:h + 48, 1] = 1, -1
        parts[h + 16:h + 32, 2], parts[h + 16:h + 32, 3] = 1, -1
    p["cols"] = np.concatenate(c + [parts], 1)
    p["a_w"] = f("L0_attn_w_qkv").T
    p["a_proj_w"] = f("L0_attn_w_proj").T
    p["a_row"] = f("L0_attn_b_proj")[None]
    p["router"] = f("L0_ffn_router_w").T
    gu = np.concatenate([f("L0_ffn_gate_w").transpose(0, 2, 1), f("L0_ffn_up_w").transpose(0, 2, 1)], 2)
    p["gate_up_a"], p["gate_up_b"] = gu[:, :128], gu[:, 128:]
    p["down"] = f("L0_ffn_down_w").transpose(0, 2, 1).reshape(E1, F1C, 128, D).transpose(0, 2, 1, 3)
    qk = np.zeros((LAYERS, D, 2, 128), np.float32)
    vw = np.zeros((LAYERS, 128, D), np.float32)
    bias = np.zeros((LAYERS, 128, 4, GROUPS), np.float32)
    for h in range(HEADS):
        s = STACK * (h % 2)
        for which, n in enumerate("qk"):
            w = f(f"L1_attn_{n}w")[:, h].transpose(0, 2, 1)
            bv = f(f"L1_attn_{n}b")[:, h]
            low = 2 if which == 0 else 1
            for part in range(3):
                at = s + DH * part
                qk[:, DH * h:DH * (h + 1), which, at:at + DH] = w
                bias[:, at:at + DH, 2 * which, h // 2] = bv
            bias[:, s + DH * low:s + DH * (low + 1), 2 * which + 1, h // 2] = bv
        bias[:, s + SHIFT_ROW, 3, h // 2] = 1
        r = DH * h % 128
        vw[:, r:r + DH, DH * h:DH * (h + 1)] = f("L1_attn_vw")[:, h].transpose(0, 2, 1)
    qk = qk.reshape(LAYERS, D, 256)
    p["qk_a"], p["qk_b"], p["v_w"] = qk[:, :128], qk[:, 128:], vw
    per = []
    for l in range(LAYERS):
        c = []
        for n in ("ln1_g", "ln1_b", "ln2_g", "ln2_b", "b1"):
            c += cut(f("L1_attn_" + n)[l])
        per.append(np.concatenate(c + [bias[l].reshape(128, 4 * GROUPS)], 1))
    p["l_cols"] = np.stack(per)
    p["l_rows"] = np.concatenate([f("L1_attn_vb").reshape(LAYERS, 1, D), f("L1_attn_b2").reshape(LAYERS, 1, D)], 2)
    first = np.concatenate([f("L1_attn_w1").transpose(0, 2, 1), f("L1_ffn_w1")])
    second = np.concatenate([f("L1_attn_w2").transpose(0, 2, 1), f("L1_ffn_w2")])
    p["w1_a"], p["w1_b"] = first[:, :128], first[:, 128:]
    p["w2"] = second.reshape(LAYERS + E2, MLPC, 128, D).transpose(0, 2, 1, 3).reshape(LAYERS + E2, 128, MLPC * D)
    p["gate2"] = f("L1_ffn_gate_weight").T
    p["mix_b1"] = f("L1_ffn_b1").reshape(E2, H2C, 128).transpose(2, 0, 1)
    p["mix_b2"] = f("L1_ffn_b2")
    return {n: np.ascontiguousarray(v) for n, v in p.items()}


def kernel(**inputs):
    import concourse.bacc as bacc
    from concourse.bass_utils import run_bass_kernel_spmd

    arrays = layout(inputs)
    nc = bacc.Bacc("TRN2", target_bir_lowering=False, num_devices=1)
    a = {n: nc.dram_tensor("in_" + n, v.shape, mybir.dt.from_np(v.dtype), kind="ExternalInput").ap() for n, v in arrays.items()}
    out = nc.dram_tensor("out", (B, TOK, D), F32, kind="ExternalOutput").ap()
    build(nc, a, out)
    r = run_bass_kernel_spmd(nc, [{"in_" + n: v for n, v in arrays.items()}], core_ids=[0])
    return r.results[0]["out"]
```

```python
from contextlib import ExitStack

import numpy as np

import concourse.bass as bass
from concourse import mybir

F32 = mybir.dt.float32
F32R = mybir.dt.float32r
I32 = mybir.dt.int32
ALU = mybir.AluOpType
ACT = mybir.ActivationFunctionType
AX = mybir.AxisListType

B = 2
D = 192
CH = (128, 64)
TILE = 96
NT = 3
TILES = B * NT
TOK = NT * TILE
IMG = 256
TXT = TOK - IMG

DT, T_LAYERS, T_HEADS, T_DH, T_FF = 128, 2, 8, 64, 512
INNER = T_HEADS * T_DH
PATCH_K = 32 * 8 * 8
PK = PATCH_K // 128
PATCH_LOADS = 4
T_ROWS = (TILE, TILE, IMG - 2 * TILE)
IC = INNER // 128
FC = T_FF // 128
HEADS, DH = 12, 16
E1, F1, F1C = 8, 384, 3
LAYERS, MLP, MLPC = 8, 768, 6
GROUPS = HEADS // 2
STACK = 64
SHIFT_ROW = 48
QUADS = 3
E2, H2, H2C = 8, 768, 6
CAPACITY = 2
PICKED = B * TOK * CAPACITY

C_CONVB = 0
C_T = 1
C_T_N = 4 + FC
C_LNF = C_T + T_LAYERS * C_T_N
C_NORMW = C_LNF + 2
C_N = C_NORMW + 2

P_N = 4
M_B1 = 4
M_N = M_B1 + MLPC


def build(nc, a, out):
    ctx = ExitStack()

    def sb(name, shape, dt=F32):
        return ctx.enter_context(nc.sbuf_tensor(name, shape, dt))

    def sem(name):
        return ctx.enter_context(nc.semaphore(name))

    with ctx:
        bank = ctx.enter_context(nc.psum_tensor("bank", [128, 8, 512], F32))

        ident = sb("ident", [128, 128])
        ones = sb("ones", [128, 128])
        lower = sb("lower", [128, TILE])
        head64 = sb("head64", [128, 128])
        head16 = sb("head16", [128, 128])
        rank8 = sb("rank8", [TILE, 1, E1])
        minus_half = sb("minus_half", [TILE, TILES])
        eps5 = sb("eps5", [TILE, TILES])
        eps6 = sb("eps6", [TILE, TILES])
        carrier = sb("carrier", [1, 1])
        cols = sb("cols", [128, C_N])
        H = sb("H", [TILE, TILES, D])
        xn = sb("xn", [TILE, TILES, D])
        xT = sb("xT", [128, 2, B, TOK])
        stats = sb("stats", [TILE, TILES, 6])
        mv = sb("mv", [TILE, TILES, 2])
        veps = sb("veps", [TILE, TILES])
        rstd = sb("rstd", [TILE, TILES])

        consts_ready = sem("consts_ready")
        pool_const = sem("pool_const")
        masks_ready = sem("masks_ready")
        padded = sem("padded")
        cols_in = sem("cols_in")
        link = sem("link")
        var_ready = sem("var_ready")
        rstd_ready = sem("rstd_ready")
        pool_step = sem("pool_step")
        normed = sem("normed")
        turned = sem("turned")
        xT_ready = sem("xT_ready")
        stored = sem("stored")

        NORM_T = 0
        NORM_A = 2 * T_LAYERS + 1
        NORM_M = NORM_A + 1
        NORM_R = NORM_M + 2
        NORM_E = NORM_R + 1
        TURN_A = NORM_A
        def turn_base(n_tok, n_full):
            return n_tok * B + n_full * 2 * B

        n_link = [0]

        def linked(dve, ins):
            n_link[0] += 1
            ins.then_inc(link, 1)
            dve.wait_ge(link, n_link[0])

        def loop_linker(dve, signal, base):
            n = [0]

            def step(ins):
                n[0] += 1
                ins.then_inc(signal, 1)
                dve.wait_ge(signal, base + n[0])
            return step, n

        def norm_stats(dve, step, src, rows, norm, rms=False):
            for i in range(TILES):
                last = nc.vector.bn_stats(stats[0:rows[i % NT], i, :], src(i))
            step(last)
            nc.vector.memset(carrier[:, :], 0.0)
            for i in range(TILES):
                r = rows[i % NT]
                last = nc.vector.bn_aggr(mv[0:r, i, :], stats[0:r, i, :])
            if rms:
                step(last)
                step(nc.vector.tensor_tensor(veps[:, :], mv[:, :, 0], mv[:, :, 0], ALU.mult))
                step(nc.vector.tensor_tensor(mv[:, :, 1], mv[:, :, 1], veps[:, :], ALU.add))
                last = nc.vector.memset(mv[:, :, 0], 0.0)
            last.then_inc(var_ready, 1)

        def norm_rstd(pool, norm, eps, n_step):
            pool.wait_ge(var_ready, norm + 1)
            nc.gpsimd.tensor_tensor(veps[:, :], mv[:, :, 1], eps[:, :], ALU.add).then_inc(pool_step, 1)
            pool.wait_ge(pool_step, n_step + 1)
            nc.gpsimd.tensor_tensor(rstd[:, :], veps[:, :], minus_half[:, :], ALU.pow).then_inc(rstd_ready, 1)

        def norm_apply(dve, src, dst, rows, norm):
            dve.wait_ge(rstd_ready, norm + 1)
            for i in range(TILES):
                r = rows[i % NT]
                nc.vector.tensor_scalar(dst(i), src(i), mv[0:r, i, 0:1], rstd[0:r, i:i + 1],
                                        ALU.subtract, ALU.mult).then_inc(normed, 1)

        def turn(pe, src, rows, chunks, signal, base, first=4):
            for b in range(B):
                for c in range(chunks):
                    for j in range(NT):
                        i = b * NT + j
                        r = rows[j]
                        if c == 0:
                            pe.wait_ge(signal, base + i + 1)
                        last = nc.tensor.transpose(bank[0:CH[c], first + b * chunks + c, j * TILE:j * TILE + r],
                                                   src[0:r, i, c * 128:c * 128 + CH[c]], ident[0:r, 0:r])
                    last.then_inc(turned, 1)

        def turned_out(dve, tokens, chunks, base, gain=None, shift=None, first=4):
            for b in range(B):
                for c in range(chunks):
                    n = CH[c]
                    src = bank[0:n, first + b * chunks + c, 0:tokens]
                    dve.wait_ge(turned, base + b * chunks + c + 1)
                    if gain is None:
                        ins = nc.vector.tensor_copy(xT[0:n, c, b, 0:tokens], src)
                    elif shift is None:
                        ins = nc.vector.tensor_scalar(xT[0:n, c, b, 0:tokens], src, gain(c), None, ALU.mult)
                    else:
                        ins = nc.vector.tensor_scalar(xT[0:n, c, b, 0:tokens], src, gain(c), shift(c),
                                                      ALU.mult, ALU.add)
                    ins.then_inc(xT_ready, 1)

        full = (TILE,) * NT

        a_w = sb("a_w", [128, 2, 3 * D])
        a_proj_w = sb("a_proj_w", [128, 2, D])
        a_row = sb("a_row", [TILE, D])
        router_w = sb("router_w", [128, 2, E1])
        gate_up_w = sb("gate_up_w", [128, 2, 2 * F1])
        down_w = sb("down_w", [128, F1C, D])
        p_cols = sb("p_cols", [128, P_N])
        m_cols = sb("m_cols", [128, M_N])
        p_row = sb("p_row", [TILE, 3 * D])
        m_row = sb("m_row", [TILE, D])
        l_qkv_w = sb("l_qkv_w", [128, 2, 3 * 128])
        w1 = sb("w1", [128, 2, MLP])
        w2 = sb("w2", [128, MLPC, D])
        gate2_w = sb("gate2_w", [128, 2, E2])
        b2_rows = sb("b2_rows", [E2, D])
        b1_cols = sb("b1_cols", [128, E2, H2C])

        stage = ExitStack()

        def tb(name, shape, dt=F32):
            return stage.enter_context(nc.sbuf_tensor(name, shape, dt))

        patches = tb("patches", [128, PK, B * IMG])
        conv_w = tb("conv_w", [128, PK, DT])
        t_qkv_w = tb("t_qkv_w", [128, T_LAYERS, 3 * INNER])
        t_out_w = tb("t_out_w", [128, T_LAYERS, IC, DT])
        t_ff1_w = tb("t_ff1_w", [128, T_LAYERS, T_FF])
        t_ff2_w = tb("t_ff2_w", [128, T_LAYERS, FC, DT])
        t_head_w = tb("t_head_w", [128, D])
        t_rows = tb("t_rows", [TILE, T_LAYERS * 2 * DT + D])
        convT = tb("convT", [128, B, IMG])
        X = tb("X", [TILE, TILES, DT])
        tq = tb("tq", [TILE, TILES, INNER])
        tv = tb("tv", [TILE, TILES, INNER])
        tk = tb("tk", [TILE, TILES, INNER])
        tkT = tb("tkT", [128, IC, B, IMG])
        tqT = tb("tqT", [128, IC, B, IMG])
        tctx = tb("tctx", [128, B, IC, 128])
        tq_max = tb("tq_max", [TILE, TILES, T_HEADS])
        tq_sum = tb("tq_sum", [TILE, TILES, T_HEADS])
        tk_max = tb("tk_max", [128, IC, B])
        tk_sum = tb("tk_sum", [128, IC, B])
        tk_rec = tb("tk_rec", [128, IC, B])

        patches_in = [sem(f"patches_in{n}") for n in range(PATCH_LOADS)]
        t_w_in = [sem(f"t_w_in{n}") for n in range(3)]
        txt_in = sem("txt_in")
        conv_done = sem("conv_done")
        convT_ready = sem("convT_ready")
        x_turned = sem("x_turned")
        x_ready = sem("x_ready")
        tq_done = sem("tq_done")
        tv_done = sem("tv_done")
        tkT_done = sem("tkT_done")
        tv_copied = sem("tv_copied")
        tq_maxed = sem("tq_maxed")
        tq_exp = sem("tq_exp")
        tq_norm = sem("tq_norm")
        tk_maxed = sem("tk_maxed")
        tk_exp = sem("tk_exp")
        tk_turned = sem("tk_turned")
        tk_ready = sem("tk_ready")
        tq_turned = sem("tq_turned")
        tqT_ready = sem("tqT_ready")
        tctx_done = sem("tctx_done")
        tctx_ready = sem("tctx_ready")
        tatt_done = sem("tatt_done")
        tatt_ready = sem("tatt_ready")
        tproj_done = sem("tproj_done")
        x_attn = sem("x_attn")
        tff1_done = sem("tff1_done")
        tff1_act = sem("tff1_act")
        tff2_done = sem("tff2_done")
        head_done = sem("head_done")
        h_tok = sem("h_tok")

        def tok_tile(t, i):
            return t[0:T_ROWS[i % NT], i, :]

        def tokenizer_sync(sp):
            sp.dma_start(conv_w[:, :, :], a["conv_w"]).then_inc(patches_in[0], 16)
            n = PK // PATCH_LOADS
            for k in range(PATCH_LOADS):
                sp.dma_start(patches[:, k * n:(k + 1) * n, :], a["patches"][:, k * n:(k + 1) * n, :]).then_inc(patches_in[k], 16)
            sp.dma_start(t_qkv_w[:, :, :], a["t_qkv_w"]).then_inc(t_w_in[0], 16)
            sp.dma_start(t_out_w[:, :, :, :], a["t_out_w"]).then_inc(t_w_in[1], 16)
            sp.dma_start(t_rows[:, :], a["t_rows"].to_broadcast([TILE, T_LAYERS * 2 * DT + D])).then_inc(t_w_in[1], 16)
            sp.dma_start(t_ff1_w[:, :, :], a["t_ff1_w"]).then_inc(t_w_in[2], 16)
            sp.dma_start(t_ff2_w[:, :, :, :], a["t_ff2_w"]).then_inc(t_w_in[2], 16)
            sp.dma_start(t_head_w[:, :], a["t_head_w"]).then_inc(t_w_in[2], 16)
            for b in range(B):
                sp.dma_start(H[T_ROWS[2]:TILE, b * NT + 2, :], a["txt"][b]).then_inc(txt_in, 16)

        def tokenizer_tensor(pe):
            n = PK // PATCH_LOADS
            for k in range(PK):
                if k % n == 0:
                    pe.wait_ge(patches_in[k // n], 32 if k == 0 else 16)
                last = nc.tensor.matmul(bank[:, 0, :], conv_w[:, k, :], patches[:, k, :], start=(k == 0), stop=(k == PK - 1))
            last.then_inc(conv_done, 1)
            pe.wait_ge(consts_ready, 4)
            pe.wait_ge(convT_ready, 1)
            for b in range(B):
                for j in range(NT):
                    r = T_ROWS[j]
                    last = nc.tensor.transpose(bank[0:r, 1 + b, j * 128:(j + 1) * 128],
                                               convT[:, b, j * TILE:j * TILE + r], ident[:, :])
                last.then_inc(x_turned, 1)
            for l in range(T_LAYERS):
                turn(pe, xn, T_ROWS, 1, normed, 2 * l * TILES)
                pe.wait_ge(t_w_in[0], 16)
                for which, signal in ((0, tq_done), (2, tv_done)):
                    for i in range(TILES):
                        b, j = divmod(i, NT)
                        if i == 0 and which == 0:
                            pe.wait_ge(xT_ready, turn_base(2 * l, 0) + B)
                        if which == 0 and i >= 4:
                            pe.wait_ge(tq_maxed, l * TILES + i - 3)
                        if which == 2:
                            if i < 4:
                                pe.wait_ge(tq_maxed, l * TILES + min(i + 5, TILES) if i < 2 else l * TILES + i + 1)
                            else:
                                pe.wait_ge(tv_copied, l * TILES + i - 3)
                        nc.tensor.matmul(bank[0:T_ROWS[j], i % 4, :], xT[:, 0, b, j * TILE:j * TILE + T_ROWS[j]],
                                         t_qkv_w[:, l, which * INNER:(which + 1) * INNER],
                                         start=True, stop=True).then_inc(signal, 1)
                for c in range(IC):
                    nc.tensor.matmul(bank[:, 4 + c, :].rearrange("p (b n) -> p b n", b=B),
                                     t_qkv_w[:, l, INNER + c * 128:INNER + (c + 1) * 128],
                                     xT[:, 0, :, 0:IMG], start=True, stop=True).then_inc(tkT_done, 1)
                for i in range(TILES):
                    b, j = divmod(i, NT)
                    r = T_ROWS[j]
                    if i < 4:
                        pe.wait_ge(tv_copied, l * TILES + (i + 5 if i < 2 else i + 1))
                    else:
                        pe.wait_ge(tk_ready, l * TILES + i - 3)
                    for c in range(IC):
                        if j == 0:
                            pe.wait_ge(tk_exp, (l * B + b) * IC + c + 1)
                        last = nc.tensor.transpose(bank[0:r, i % 4, c * 128:(c + 1) * 128],
                                                   tkT[:, c, b, j * TILE:j * TILE + r], ident[:, :])
                    last.then_inc(tk_turned, 1)
                for c in range(IC):
                    if c == 0:
                        pe.wait_ge(tk_exp, (l + 1) * B * IC)
                        pe.wait_ge(tq_norm, (l + 1) * TILES)
                    for i in range(TILES):
                        b, j = divmod(i, NT)
                        r = T_ROWS[j]
                        last = nc.tensor.transpose(bank[:, 4 + c, b * IMG + j * TILE:b * IMG + j * TILE + r],
                                                   tq[0:r, i, c * 128:(c + 1) * 128], ident[0:r, 0:r])
                    last.then_inc(tq_turned, 1)
                pe.wait_ge(tk_ready, (l + 1) * TILES)
                for b in range(B):
                    for c in range(IC):
                        if b == 1:
                            pe.wait_ge(tctx_ready, l * B * IC + c + 1)
                        for j in range(NT):
                            i = b * NT + j
                            r = T_ROWS[j]
                            last = nc.tensor.matmul(bank[:, c, 0:128], tk[0:r, i, c * 128:(c + 1) * 128],
                                                    tv[0:r, i, c * 128:(c + 1) * 128], start=(j == 0), stop=(j == NT - 1))
                        last.then_inc(tctx_done, 1)
                for c in range(IC):
                    pe.wait_ge(tqT_ready, l * IC + c + 1)
                    pe.wait_ge(tctx_ready, l * B * IC + IC + c + 1)
                    for b in range(B):
                        last = nc.tensor.matmul(bank[:, 4 + c, b * IMG:(b + 1) * IMG], tctx[:, b, c, :], tqT[:, c, b, :],
                                                start=True, stop=True)
                    last.then_inc(tatt_done, 1)
                pe.wait_ge(t_w_in[1], 32)
                for i in range(TILES):
                    b, j = divmod(i, NT)
                    r = T_ROWS[j]
                    if i == 0:
                        pe.wait_ge(tatt_ready, (l + 1) * IC)
                    if i >= 4:
                        pe.wait_ge(x_attn, l * TILES + i - 3)
                    for c in range(IC):
                        last = nc.tensor.matmul(bank[0:r, i % 4, 0:DT], tqT[:, c, b, j * TILE:j * TILE + r],
                                                t_out_w[:, l, c, :], start=(c == 0), stop=(c == IC - 1))
                    last.then_inc(tproj_done, 1)
                turn(pe, xn, T_ROWS, 1, normed, (2 * l + 1) * TILES)
                pe.wait_ge(t_w_in[2], 48)
                pe.wait_ge(xT_ready, turn_base(2 * l + 1, 0) + B)
                for c in range(FC):
                    nc.tensor.matmul(bank[:, c, :].rearrange("p (b n) -> p b n", b=B), t_ff1_w[:, l, c * 128:(c + 1) * 128],
                                     xT[:, 0, :, 0:IMG], start=True, stop=True).then_inc(tff1_done, 1)
                for i in range(TILES):
                    b, j = divmod(i, NT)
                    r = T_ROWS[j]
                    if i == 0:
                        pe.wait_ge(tff1_act, (l + 1) * FC)
                    if i >= 2:
                        pe.wait_ge(x_ready, l * TILES + i - 1)
                    for c in range(FC):
                        last = nc.tensor.matmul(bank[0:r, 6 + i % 2, 0:DT], tqT[:, c, b, j * TILE:j * TILE + r],
                                                t_ff2_w[:, l, c, :], start=(c == 0), stop=(c == FC - 1))
                    last.then_inc(tff2_done, 1)
            turn(pe, xn, T_ROWS, 1, normed, 2 * T_LAYERS * TILES)
            pe.wait_ge(xT_ready, turn_base(2 * T_LAYERS, 0) + B)
            for i in range(TILES):
                b, j = divmod(i, NT)
                r = T_ROWS[j]
                if i >= 4:
                    pe.wait_ge(h_tok, i - 3)
                nc.tensor.matmul(bank[0:r, i % 4, 0:D], xT[:, 0, b, j * TILE:j * TILE + r], t_head_w[:, :],
                                 start=True, stop=True).then_inc(head_done, 1)

        def tokenizer_scalar(act):
            act.wait_ge(cols_in, 16)
            act.wait_ge(conv_done, 1)
            nc.scalar.activation(convT[:, :, :].rearrange("p b n -> p (b n)"), bank[:, 0, :], ACT.Identity,
                                 bias=cols[:, C_CONVB:C_CONVB + 1]).then_inc(convT_ready, 1)
            for l in range(T_LAYERS):
                c0 = C_T + l * C_T_N
                for i in range(TILES):
                    act.wait_ge(tq_maxed, l * TILES + i + 1)
                    nc.scalar.activation(tok_tile(tq, i), tok_tile(tq, i), ACT.Exp).then_inc(tq_exp, 1)
                for i in range(TILES):
                    act.wait_ge(tv_done, l * TILES + i + 1)
                    nc.scalar.activation(tok_tile(tv, i), bank[0:T_ROWS[i % NT], i % 4, :], ACT.Copy).then_inc(tv_copied, 1)
                for b in range(B):
                    for c in range(IC):
                        act.wait_ge(tk_maxed, l * IC + c + 1)
                        nc.scalar.activation(tkT[:, c, b, :], bank[:, 4 + c, b * IMG:(b + 1) * IMG], ACT.Exp,
                                             bias=tk_max[:, c, b:b + 1],
                                             accum_out=tk_sum[:, c, b:b + 1]).then_inc(tk_exp, 1)
                for i in range(TILES):
                    act.wait_ge(tk_turned, l * TILES + i + 1)
                    nc.scalar.activation(tok_tile(tk, i), bank[0:T_ROWS[i % NT], i % 4, :], ACT.Copy).then_inc(tk_ready, 1)
                for c in range(IC):
                    act.wait_ge(tq_turned, l * IC + c + 1)
                    nc.scalar.activation(tqT[:, c, :, :].rearrange("p b n -> p (b n)"), bank[:, 4 + c, :],
                                         ACT.Copy).then_inc(tqT_ready, 1)
                for c in range(IC):
                    act.wait_ge(tatt_done, l * IC + c + 1)
                    nc.scalar.activation(tqT[:, c, :, :].rearrange("p b n -> p (b n)"), bank[:, 4 + c, :],
                                         ACT.Copy).then_inc(tatt_ready, 1)
                for c in range(FC):
                    act.wait_ge(tff1_done, l * FC + c + 1)
                    nc.scalar.activation(tqT[:, c, :, :].rearrange("p b n -> p (b n)"), bank[:, c, :], ACT.Gelu,
                                         bias=cols[:, c0 + 4 + c:c0 + 5 + c]).then_inc(tff1_act, 1)

        def tokenizer_pool(pool):
            for n in range(2 * T_LAYERS + 1):
                norm_rstd(pool, n, eps5, n)

        def tokenizer_vector(dve):
            def step(ins):
                linked(dve, ins)
            step(nc.vector.memset(mv[:, :, :], 1.0))
            for b in range(B):
                dve.wait_ge(x_turned, b + 1)
                src = bank[:, 1 + b, :].rearrange("p (j n) -> p j n", n=128)
                nc.vector.tensor_copy(X[:, b * NT:b * NT + 2, :], src[0:TILE, 0:2, :])
                last = nc.vector.tensor_copy(X[0:T_ROWS[2], b * NT + 2, :], src[0:T_ROWS[2], 2, :])
            step(last)
            dve.wait_ge(t_w_in[1], 32)
            for l in range(T_LAYERS):
                c0 = C_T + l * C_T_N
                norm_stats(dve, step, lambda i: tok_tile(X, i), T_ROWS, 2 * l)
                norm_apply(dve, lambda i: tok_tile(X, i), lambda i: xn[0:T_ROWS[i % NT], i, 0:DT], T_ROWS, 2 * l)
                turned_out(dve, IMG, 1, turn_base(2 * l, 0), lambda c: cols[:, c0:c0 + 1], lambda c: cols[:, c0 + 1:c0 + 2])
                for i in range(TILES):
                    r = T_ROWS[i % NT]
                    dve.wait_ge(tq_done, l * TILES + i + 1)
                    q = bank[0:r, i % 4, :].rearrange("p (h d) -> p h d", h=T_HEADS)
                    step(nc.vector.tensor_reduce(tq_max[0:r, i, :], q, AX.X, ALU.max))
                    nc.vector.tensor_tensor(tok_tile(tq, i).rearrange("p (h d) -> p h d", h=T_HEADS), q,
                                            tq_max[0:r, i, :].unsqueeze(2).to_broadcast([r, T_HEADS, T_DH]),
                                            ALU.subtract).then_inc(tq_maxed, 1)
                for c in range(IC):
                    dve.wait_ge(tkT_done, l * IC + c + 1)
                    nc.vector.tensor_reduce(tk_max[:, c, :], bank[:, 4 + c, :].rearrange("p (b n) -> p b n", b=B),
                                            AX.X, ALU.max, negate=True).then_inc(tk_maxed, 1)
                for i in range(TILES):
                    r = T_ROWS[i % NT]
                    dve.wait_ge(tq_exp, l * TILES + i + 1)
                    q = tok_tile(tq, i).rearrange("p (h d) -> p h d", h=T_HEADS)
                    step(nc.vector.tensor_reduce(tq_max[0:r, i, :], q, AX.X, ALU.add))
                    step(nc.vector.reciprocal(tq_sum[0:r, i, :], tq_max[0:r, i, :]))
                    nc.vector.tensor_tensor(q, q, tq_sum[0:r, i, :].unsqueeze(2).to_broadcast([r, T_HEADS, T_DH]),
                                            ALU.mult).then_inc(tq_norm, 1)
                dve.wait_ge(tk_exp, (l + 1) * B * IC)
                step(nc.vector.reciprocal(tk_rec[:, :, :], tk_sum[:, :, :]))
                for b in range(B):
                    for c in range(IC):
                        dve.wait_ge(tctx_done, (l * B + b) * IC + c + 1)
                        nc.vector.scalar_tensor_tensor(tctx[:, b, c, :], bank[:, c, 0:128], tk_rec[:, c, b:b + 1],
                                                       head64[:, :], ALU.mult, ALU.mult).then_inc(tctx_ready, 1)
                rb = l * 2 * DT
                for i in range(TILES):
                    r = T_ROWS[i % NT]
                    last = nc.vector.tensor_tensor(tok_tile(X, i), tok_tile(X, i), t_rows[0:r, rb:rb + DT], ALU.add)
                step(last)
                for i in range(TILES):
                    r = T_ROWS[i % NT]
                    dve.wait_ge(tproj_done, l * TILES + i + 1)
                    last = nc.vector.tensor_tensor(tok_tile(X, i), tok_tile(X, i), bank[0:r, i % 4, 0:DT], ALU.add)
                    last.then_inc(x_attn, 1)
                dve.wait_ge(x_attn, (l + 1) * TILES)
                norm_stats(dve, step, lambda i: tok_tile(X, i), T_ROWS, 2 * l + 1)
                norm_apply(dve, lambda i: tok_tile(X, i), lambda i: xn[0:T_ROWS[i % NT], i, 0:DT], T_ROWS, 2 * l + 1)
                turned_out(dve, IMG, 1, turn_base(2 * l + 1, 0), lambda c: cols[:, c0 + 2:c0 + 3],
                           lambda c: cols[:, c0 + 3:c0 + 4])
                for i in range(TILES):
                    r = T_ROWS[i % NT]
                    last = nc.vector.tensor_tensor(tok_tile(X, i), tok_tile(X, i), t_rows[0:r, rb + DT:rb + 2 * DT], ALU.add)
                step(last)
                for i in range(TILES):
                    r = T_ROWS[i % NT]
                    dve.wait_ge(tff2_done, l * TILES + i + 1)
                    nc.vector.tensor_tensor(tok_tile(X, i), tok_tile(X, i), bank[0:r, 6 + i % 2, 0:DT],
                                            ALU.add).then_inc(x_ready, 1)
                dve.wait_ge(x_ready, (l + 1) * TILES)
            norm_stats(dve, step, lambda i: tok_tile(X, i), T_ROWS, 2 * T_LAYERS)
            norm_apply(dve, lambda i: tok_tile(X, i), lambda i: xn[0:T_ROWS[i % NT], i, 0:DT], T_ROWS, 2 * T_LAYERS)
            turned_out(dve, IMG, 1, turn_base(2 * T_LAYERS, 0), lambda c: cols[:, C_LNF:C_LNF + 1],
                       lambda c: cols[:, C_LNF + 1:C_LNF + 2])
            for i in range(TILES):
                r = T_ROWS[i % NT]
                dve.wait_ge(head_done, i + 1)
                nc.vector.tensor_tensor(H[0:r, i, :], bank[0:r, i % 4, 0:D], t_rows[0:r, T_LAYERS * 2 * DT:], ALU.add).then_inc(h_tok, 1)

        stage.close()
        later = ExitStack()

        def lb(name, shape, dt=F32):
            return later.enter_context(nc.sbuf_tensor(name, shape, dt))

        a_qT = lb("a_qT", [128, 2, B, TOK])
        a_kv = lb("a_kv", [TILE, TILES, 2 * D])
        a_kabs = lb("a_kabs", [TILE, TILES, D])
        a_qsum = lb("a_qsum", [128, 2, B])
        a_ksum = lb("a_ksum", [128, B, 2])
        a_rec = lb("a_rec", [128, B, 2])
        a_ctx = lb("a_ctx", [128, B, 2, 128])
        a_attT = lb("a_attT", [128, 2, B, TOK])
        m_in = lb("m_in", [TILE, TILES, D])
        m_prob = lb("m_prob", [TILE, E1, TILES])
        m_work = lb("m_work", [TILE, TILES, E1])
        m_pick = lb("m_pick", [TILE, TILES, E1])
        m_rest = lb("m_rest", [TILE, TILES, E1])
        m_p = lb("m_p", [TILE, TILES, E1])
        m_one = lb("m_one", [TILE, TILES])
        m_two = lb("m_two", [TILE, TILES])
        siluT = lb("siluT", [128, 2, B, TOK])
        hidT = lb("hidT", [128, MLPC, B, TOK])
        layer_tensors = ExitStack()

        def rb(name, shape, dt=F32):
            return layer_tensors.enter_context(nc.sbuf_tensor(name, shape, dt))

        R = rb("R", [TILE, TILES, D])
        q_stack = rb("q_stack", [128, GROUPS, B, TOK], F32R)
        k_stack = rb("k_stack", [128, GROUPS, B, TOK], F32R)
        ident_r = rb("ident_r", [TILE, TILE], F32R)
        qk_sum = rb("qk_sum", [TILE, 2, NT, D])
        qk_parts = rb("qk_parts", [TILE, 2, NT, HEADS, STACK], F32R)
        probs = rb("probs", [TILE, 4, 2, TOK])
        v_ext = rb("v_ext", [TILE, TILES, HEADS, 32])
        oT = rb("oT", [128, 2, TOK])
        o_rec = rb("o_rec", [TILE, NT, 4])
        o_tmp = rb("o_tmp", [TILE, NT, 4, DH])

        layer_tensors.close()

        a_in = sem("a_in")
        a_q_done = sem("a_q_done")
        a_kv_done = sem("a_kv_done")
        a_qT_ready = sem("a_qT_ready")
        a_kv_ready = sem("a_kv_ready")
        a_kabs_ready = sem("a_kabs_ready")
        a_ctx_done = sem("a_ctx_done")
        a_ctx_ready = sem("a_ctx_ready")
        a_att_done = sem("a_att_done")
        a_att_ready = sem("a_att_ready")
        a_proj_done = sem("a_proj_done")
        h_attn = sem("h_attn")

        def attn_sync(sp):
            sp.dma_start(a_w[:, 0, :], a["a_w"][0:128]).then_inc(a_in, 16)
            sp.dma_start(a_w[0:64, 1, :], a["a_w"][128:D]).then_inc(a_in, 16)
            sp.dma_start(a_proj_w[:, 0, :], a["a_proj_w"][0:128]).then_inc(a_in, 16)
            sp.dma_start(a_proj_w[0:64, 1, :], a["a_proj_w"][128:D]).then_inc(a_in, 16)
            sp.dma_start(a_row[:, :], a["a_row"].to_broadcast([TILE, D])).then_inc(a_in, 16)

        def two_chunks(out_ap, lhs, rhs):
            for c in range(2):
                last = nc.tensor.matmul(out_ap, lhs(c), rhs(c), start=(c == 0), stop=(c == 1))
            return last

        def attn_tensor(pe):
            turn(pe, xn, full, 2, normed, NORM_A * TILES)
            pe.wait_ge(a_in, 80)
            pe.wait_ge(xT_ready, turn_base(TURN_A, 1))
            for m in range(2):
                for b in range(B):
                    last = two_chunks(bank[0:CH[m], 2 * m + b, 0:TOK],
                                      lambda c: a_w[:, c, m * 128:m * 128 + CH[m]],
                                      lambda c: xT[:, c, b, :])
                last.then_inc(a_q_done, 1)
            for i in range(TILES):
                b, j = divmod(i, NT)
                if i >= 4:
                    pe.wait_ge(a_kv_ready, i - 3)
                two_chunks(bank[0:TILE, 4 + i % 4, 0:2 * D], lambda c: xT[:, c, b, j * TILE:(j + 1) * TILE],
                           lambda c: a_w[:, c, D:3 * D]).then_inc(a_kv_done, 1)
            for b in range(B):
                for m in range(2):
                    n = CH[m]
                    if b == 0:
                        pe.wait_ge(a_qT_ready, m + 1)
                    else:
                        pe.wait_ge(a_ctx_ready, m + 1)
                    pe.wait_ge(a_kabs_ready, (b + 1) * NT)
                    for j in range(NT):
                        i = b * NT + j
                        nc.tensor.matmul(bank[0:n, m, 0:n], a_kv[:, i, m * 128:m * 128 + n],
                                         a_kv[:, i, D + m * 128:D + m * 128 + n], start=(j == 0), stop=(j == NT - 1))
                    for j in range(NT):
                        last = nc.tensor.matmul(bank[0:n, m, 256:257], a_kabs[:, b * NT + j, m * 128:m * 128 + n],
                                                ones[0:TILE, 0:1], start=(j == 0), stop=(j == NT - 1))
                    last.then_inc(a_ctx_done, 1)
            for b in range(B):
                for m in range(2):
                    n = CH[m]
                    if b == 0 and m == 0:
                        pe.wait_ge(a_kv_ready, TILES)
                    pe.wait_ge(a_ctx_ready, b * 2 + m + 1)
                    nc.tensor.matmul(bank[0:n, 4 + b * 2 + m, 0:TOK], a_ctx[0:n, b, m, 0:n], a_qT[0:n, m, b, :],
                                     start=True, stop=True).then_inc(a_att_done, 1)
            for i in range(TILES):
                b, j = divmod(i, NT)
                pe.wait_ge(a_att_ready, 2 * (b + 1))
                if i >= 4:
                    pe.wait_ge(h_attn, i - 3)
                two_chunks(bank[0:TILE, i % 4, 0:D], lambda c: a_attT[0:CH[c], c, b, j * TILE:(j + 1) * TILE],
                           lambda c: a_proj_w[0:CH[c], c, :]).then_inc(a_proj_done, 1)

        def attn_scalar(act):
            for m in range(2):
                act.wait_ge(a_q_done, m + 1)
                nc.scalar.activation(a_qT[0:CH[m], m, :, :], bank[0:CH[m], 2 * m:2 * m + 2, 0:TOK],
                                     ACT.Copy).then_inc(a_qT_ready, 1)
            for i in range(TILES):
                act.wait_ge(a_kv_done, i + 1)
                nc.scalar.activation(a_kv[:, i, :], bank[0:TILE, 4 + i % 4, 0:2 * D], ACT.Copy).then_inc(a_kv_ready, 1)
            for b in range(B):
                for m in range(2):
                    act.wait_ge(a_att_done, b * 2 + m + 1)
                    nc.scalar.activation(a_attT[0:CH[m], m, b, :], bank[0:CH[m], 4 + b * 2 + m, 0:TOK],
                                         ACT.Copy).then_inc(a_att_ready, 1)

        def attn_vector(dve):
            def step(ins):
                linked(dve, ins)
            dve.wait_ge(txt_in, 16 * B)
            dve.wait_ge(h_tok, TILES)
            norm_stats(dve, step, lambda i: H[:, i, :], full, NORM_A)
            norm_apply(dve, lambda i: H[:, i, :], lambda i: xn[:, i, :], full, NORM_A)
            turned_out(dve, TOK, 2, turn_base(TURN_A, 0))
            dve.wait_ge(a_in, 80)
            step(nc.vector.tensor_tensor(H[:, :, :], H[:, :, :], a_row[:, :].unsqueeze(1).to_broadcast([TILE, TILES, D]), ALU.add))
            for i in range(TILES):
                dve.wait_ge(a_kv_ready, i + 1)
                nc.vector.scalar_tensor_tensor(a_kabs[:, i, :], a_kv[:, i, 0:D], -1.0, a_kv[:, i, 0:D],
                                               ALU.mult, ALU.max).then_inc(a_kabs_ready, 1)
            for m in range(2):
                n = CH[m]
                dve.wait_ge(a_qT_ready, m + 1)
                nc.vector.tensor_reduce(a_qsum[0:n, m, :], a_qT[0:n, m, :, :], AX.X, ALU.add, apply_absolute_value=True)
            for b in range(B):
                for m in range(2):
                    n = CH[m]
                    dve.wait_ge(a_ctx_done, b * 2 + m + 1)
                    step(nc.vector.tensor_scalar(a_ksum[0:n, b, m:m + 1], bank[0:n, m, 256:257], 1e-12, None, ALU.max))
                    step(nc.vector.tensor_scalar(a_qsum[0:n, m, b:b + 1], a_qsum[0:n, m, b:b + 1], 1e-12, None, ALU.max))
                    step(nc.vector.reciprocal(a_ksum[0:n, b, m:m + 1], a_ksum[0:n, b, m:m + 1]))
                    step(nc.vector.reciprocal(a_qsum[0:n, m, b:b + 1], a_qsum[0:n, m, b:b + 1]))
                    step(nc.vector.tensor_tensor(a_rec[0:n, b, m:m + 1], a_ksum[0:n, b, m:m + 1],
                                                 a_qsum[0:n, m, b:b + 1], ALU.mult))
                    nc.vector.scalar_tensor_tensor(a_ctx[0:n, b, m, 0:n], bank[0:n, m, 0:n], a_rec[0:n, b, m:m + 1],
                                                   head16[0:n, 0:n], ALU.mult, ALU.mult).then_inc(a_ctx_ready, 1)
            for i in range(TILES):
                dve.wait_ge(a_proj_done, i + 1)
                nc.vector.tensor_tensor(H[:, i, :], H[:, i, :], bank[0:TILE, i % 4, 0:D], ALU.add).then_inc(h_attn, 1)
            dve.wait_ge(h_attn, TILES)

        router_in = sem("router_in")
        gate_up_in = sem("gate_up_in")
        down_in = sem("down_in")
        router_done = sem("router_done")
        m_exp_in = sem("m_exp_in")
        m_exp_done = sem("m_exp_done")
        gate_done = sem("gate_done")
        up_done = sem("up_done")
        silu_done = sem("silu_done")
        mid_ready = sem("mid_ready")
        down_done = sem("down_done")
        m_added = sem("m_added")

        def load_gate_up(sp, e):
            sp.dma_start(gate_up_w[:, 0, :], a["gate_up_a"][e]).then_inc(gate_up_in, 16)
            sp.dma_start(gate_up_w[0:64, 1, :], a["gate_up_b"][e]).then_inc(gate_up_in, 16)

        def dyn(t, e):
            return t[bass.ds(e, 1)].squeeze(0)

        def mix_sync(sp):
            sp.dma_start(router_w[:, 0, :], a["router"][0:128]).then_inc(router_in, 16)
            sp.dma_start(router_w[0:64, 1, :], a["router"][128:D]).then_inc(router_in, 16)
            load_gate_up(sp, 0)
            sp.dma_start(down_w[:, :, :], a["down"][0]).then_inc(down_in, 16)

        def mix_sync_loop(sp):
            with sp.Fori(0, E1 - 1) as e:
                sp.wait_ge(up_done, e * F1C + F1C)
                sp.dma_start(gate_up_w[:, 0, :], a["gate_up_a"][bass.ds(e + 1, 1)].rearrange("e p n -> (e p) n")).then_inc(gate_up_in, 16)
                sp.dma_start(gate_up_w[0:64, 1, :], a["gate_up_b"][bass.ds(e + 1, 1)].rearrange("e p n -> (e p) n")).then_inc(gate_up_in, 16)
                sp.wait_ge(down_done, e * TILES + TILES)
                sp.dma_start(down_w[:, :, :], a["down"][bass.ds(e + 1, 1)].rearrange("e p c n -> (e p) c n")).then_inc(down_in, 16)

        def mix_tensor(pe):
            turn(pe, xn, full, 2, normed, (NORM_M + 1) * TILES)
            pe.wait_ge(router_in, 32)
            pe.wait_ge(xT_ready, turn_base(TURN_A, 2))
            for i in range(TILES):
                b, j = divmod(i, NT)
                last = two_chunks(bank[0:TILE, 6, i * E1:(i + 1) * E1], lambda c: xT[:, c, b, j * TILE:(j + 1) * TILE],
                                  lambda c: router_w[:, c, :])
            last.then_inc(router_done, 1)
            with pe.Fori(0, E1) as e:
                pe.wait_ge(gate_up_in, e * 32 + 32)
                for m in range(F1C):
                    for up, signal in ((0, gate_done), (1, up_done)):
                        u = 2 * m + up
                        if u == 3 or u == 5:
                            pe.wait_ge(silu_done, e * F1C + (u - 3) // 2 + 1)
                        if u == 4:
                            pe.wait_ge(mid_ready, e * F1C + 1)
                        for b in range(B):
                            last = two_chunks(bank[:, 2 * (u % 3) + b, 0:TOK],
                                              lambda c: gate_up_w[:, c, up * F1 + m * 128:up * F1 + (m + 1) * 128],
                                              lambda c: xT[:, c, b, :])
                        last.then_inc(signal, 1)
                pe.wait_ge(down_in, e * 16 + 16)
                pe.wait_ge(mid_ready, e * F1C + F1C)
                for i in range(TILES):
                    b, j = divmod(i, NT)
                    if i >= 2:
                        pe.wait_ge(m_added, e * TILES + i - 1)
                    for c in range(F1C):
                        last = nc.tensor.matmul(bank[0:TILE, 6 + i % 2, 0:D], hidT[:, c, b, j * TILE:(j + 1) * TILE],
                                                down_w[:, c, :], start=(c == 0), stop=(c == F1C - 1))
                    last.then_inc(down_done, 1)

        def mix_scalar(act):
            act.wait_ge(m_exp_in, 1)
            nc.scalar.activation(m_work[:, :, :], m_work[:, :, :], ACT.Exp).then_inc(m_exp_done, 1)
            with act.Fori(0, E1) as e:
                for m in range(F1C):
                    act.wait_ge(gate_done, e * F1C + m + 1)
                    if m >= 2:
                        act.wait_ge(mid_ready, e * F1C + m - 1)
                    nc.scalar.activation(siluT[:, m % 2, :, :], bank[:, 2 * (2 * m % 3):2 * (2 * m % 3) + 2, 0:TOK],
                                         ACT.Silu).then_inc(silu_done, 1)

        def mix_pool(pool):
            norm_rstd(pool, NORM_M, eps5, NORM_M)
            norm_rstd(pool, NORM_M + 1, eps6, NORM_M + 1)

        def softmax8(dve, step, logits, exp_in, exp_done, shape):
            step(nc.vector.tensor_reduce(m_one[:, :], logits, AX.X, ALU.max))
            nc.vector.tensor_tensor(m_work[:, :, :], logits, m_one[:, :].unsqueeze(2).to_broadcast(shape),
                                    ALU.subtract).then_inc(exp_in, 1)
            dve.wait_ge(exp_done, 1)
            step(nc.vector.tensor_reduce(m_one[:, :], m_work[:, :, :], AX.X, ALU.add))
            step(nc.vector.reciprocal(m_two[:, :], m_one[:, :]))
            step(nc.vector.tensor_tensor(m_p[:, :, :], m_work[:, :, :], m_two[:, :].unsqueeze(2).to_broadcast(shape), ALU.mult))

        def mix_vector(dve):
            def step(ins):
                linked(dve, ins)
            shape = [TILE, TILES, E1]
            norm_stats(dve, step, lambda i: H[:, i, :], full, NORM_M)
            norm_apply(dve, lambda i: H[:, i, :], lambda i: m_in[:, i, :], full, NORM_M)
            dve.wait_ge(normed, (NORM_M + 1) * TILES)
            norm_stats(dve, step, lambda i: m_in[:, i, :], full, NORM_M + 1, rms=True)
            norm_apply(dve, lambda i: m_in[:, i, :], lambda i: xn[:, i, :], full, NORM_M + 1)
            turned_out(dve, TOK, 2, turn_base(TURN_A, 1), lambda c: cols[0:CH[c], C_NORMW + c:C_NORMW + c + 1])
            step(nc.vector.tensor_tensor(H[:, :, :], H[:, :, :], m_in[:, :, :], ALU.add))
            dve.wait_ge(router_done, 1)
            softmax8(dve, step, bank[0:TILE, 6, 0:TILES * E1].rearrange("p (i e) -> p i e", e=E1), m_exp_in, m_exp_done,
                     shape)
            rank = rank8[:, :, :].to_broadcast(shape)

            def best(src, dst):
                step(nc.vector.tensor_reduce(m_one[:, :], src[:, :, :], AX.X, ALU.max))
                step(nc.vector.tensor_tensor(m_work[:, :, :], src[:, :, :], m_one[:, :].unsqueeze(2).to_broadcast(shape),
                                             ALU.is_equal))
                step(nc.vector.tensor_tensor(m_work[:, :, :], m_work[:, :, :], rank, ALU.mult))
                step(nc.vector.tensor_reduce(m_one[:, :], m_work[:, :, :], AX.X, ALU.max))
                step(nc.vector.tensor_tensor(dst[:, :, :], m_work[:, :, :], m_one[:, :].unsqueeze(2).to_broadcast(shape),
                                             ALU.is_equal))
            best(m_p, m_pick)
            step(nc.vector.scalar_tensor_tensor(m_rest[:, :, :], m_pick[:, :, :], -2.0, m_p[:, :, :], ALU.mult, ALU.add))
            best(m_rest, m_rest)
            step(nc.vector.tensor_tensor(m_pick[:, :, :], m_pick[:, :, :], m_rest[:, :, :], ALU.add))
            step(nc.vector.tensor_tensor(m_prob[:, :, :].rearrange("p e i -> p i e"), m_p[:, :, :], m_pick[:, :, :], ALU.mult))
            with dve.Fori(0, E1) as e:
                for m in range(F1C):
                    dve.wait_ge(silu_done, e * F1C + m + 1)
                    dve.wait_ge(up_done, e * F1C + m + 1)
                    s = 2 * ((2 * m + 1) % 3)
                    nc.vector.tensor_tensor(hidT[:, m, :, :], siluT[:, m % 2, :, :], bank[:, s:s + 2, 0:TOK],
                                            ALU.mult).then_inc(mid_ready, 1)
                for i in range(TILES):
                    dve.wait_ge(down_done, e * TILES + i + 1)
                    nc.vector.scalar_tensor_tensor(H[:, i, :], bank[0:TILE, 6 + i % 2, 0:D],
                                                   m_prob[:, bass.ds(e, 1), i:i + 1].rearrange("p e i -> p (e i)"), H[:, i, :],
                                                   ALU.mult, ALU.add).then_inc(m_added, 1)
            dve.wait_ge(m_added, E1 * TILES)

        def pair(name):
            return [sem(f"{name}{b}") for b in range(B)]

        l_qkv_in = sem("l_qkv_in")
        l_pvec_in = sem("l_pvec_in")
        l_mvec_in = sem("l_mvec_in")
        w1_in = sem("w1_in")
        w2_in = sem("w2_in")
        presets = sem("presets")
        layer_link = sem("layer_link")
        l_var = pair("l_var")
        l_eps = pair("l_eps")
        l_rstd = pair("l_rstd")
        l_normed = pair("l_normed")
        l_turned = pair("l_turned")
        l_xT = pair("l_xT")
        qkv_done = pair("qkv_done")
        qkv_ready = pair("qkv_ready")
        hi_ready = pair("hi_ready")
        lo_ready = pair("lo_ready")
        stack_done = pair("stack_done")
        q_ready = pair("q_ready")
        k_ready = pair("k_ready")
        row_scores = pair("row_scores")
        row_taken = pair("row_taken")
        shift_done = pair("shift_done")
        shift_ready = pair("shift_ready")
        scores_done = pair("scores_done")
        probs_ready = pair("probs_ready")
        pv_done = pair("pv_done")
        o_copied = pair("o_copied")
        o_turned = pair("o_turned")
        o_added = pair("o_added")
        up_done1 = pair("up_done1")
        gelu_ready = pair("gelu_ready")
        down_done1 = pair("down_done1")
        r_biased = pair("r_biased")
        r_ready = pair("r_ready")
        h_layers = sem("h_layers")

        ROWS = NT * GROUPS
        SHIFTS = GROUPS // 2
        STEPS = QUADS * NT
        UNITS = 2 * STEPS
        STACKS = 2 * GROUPS
        MERGE_AT, APPLY_AT, UP_AT, DOWN_AT = 1, 4, 6, 13
        VALUES_AT = 1
        SIDE = 6

        class Steps:

            def norm(self, b, n, second): pass
            def apply(self, b, n, second): pass
            def turn(self, b, n, second): pass
            def clear(self, b, n): pass
            def values(self, b, n, j): pass
            def split(self, b, n, j): pass
            def stack(self, b, n, u): pass
            def row(self, b, n, u): pass
            def shift(self, b, n, t): pass
            def scores(self, b, n, k): pass
            def exps(self, b, n, k): pass
            def weigh(self, b, n, k): pass
            def collect(self, b, n, o): pass
            def turn_back(self, b, n, o): pass
            def merge(self, b, n, o): pass
            def up(self, b, n, m): pass
            def down(self, b, n, j): pass

        def project(s, b, n):
            s.norm(b, n, 0)
            s.apply(b, n, 0)
            s.turn(b, n, 0)
            for j in range(NT):
                s.values(b, n, j)
                s.split(b, n, j)
            for u in range(STACKS):
                s.stack(b, n, u)

        def mlp(s, b, n):
            s.turn_back(b, n, QUADS - 1)
            s.merge(b, n, QUADS - 1)
            s.norm(b, n, 1)
            s.apply(b, n, 1)
            s.turn(b, n, 1)
            for m in range(MLPC):
                s.up(b, n, m)
            for j in range(NT):
                s.down(b, n, j)

        def half(s, b, n, mlp_of, project_of):
            o = 1 - b
            for u in range(ROWS):
                s.row(b, n, u)
                if mlp_of is not None:
                    if u == MERGE_AT:
                        s.turn_back(o, mlp_of, QUADS - 1)
                    if u == MERGE_AT + 1:
                        s.merge(o, mlp_of, QUADS - 1)
                        s.norm(o, mlp_of, 1)
                    if u == APPLY_AT:
                        s.apply(o, mlp_of, 1)
                    if u == APPLY_AT + 1:
                        s.turn(o, mlp_of, 1)
                    if UP_AT <= u < UP_AT + MLPC:
                        s.up(o, mlp_of, u - UP_AT)
                    if u >= DOWN_AT and (u - DOWN_AT) % 2 == 0 and (u - DOWN_AT) // 2 < NT:
                        s.down(o, mlp_of, (u - DOWN_AT) // 2)
            if project_of is not None:
                s.norm(o, project_of, 0)
            for t in range(SHIFTS):
                s.shift(b, n, t)
            s.clear(b, n)
            s.scores(b, n, 0)
            if project_of is not None:
                s.apply(o, project_of, 0)
            turned_units = 0
            for k in range(STEPS):
                if k + 1 < STEPS:
                    s.scores(b, n, k + 1)
                s.exps(b, n, k)
                if k >= NT and k % NT == 0:
                    s.turn_back(b, n, k // NT - 1)
                if project_of is not None:
                    if VALUES_AT < k <= VALUES_AT + NT:
                        s.split(o, project_of, k - VALUES_AT - 1)
                    if VALUES_AT <= k < VALUES_AT + NT:
                        s.values(o, project_of, k - VALUES_AT)
                    if k > VALUES_AT + NT:
                        left = STEPS - k
                        for u in range(-(-(STACKS - turned_units) // left)):
                            s.stack(o, project_of, turned_units)
                            turned_units += 1
                s.weigh(b, n, k)
                if project_of is not None and k == VALUES_AT - 1:
                    s.turn(o, project_of, 0)
                if k >= NT and k % NT == 0:
                    s.merge(b, n, k // NT - 1)
                if k % NT == NT - 1:
                    s.collect(b, n, k // NT)

        def begin(s):
            project(s, 0, 0)
            half(s, 0, 0, None, 0)

        def body(s, n):
            half(s, 1, n, n, n + 1)
            half(s, 0, n + 1, n, n + 1)

        def end(s):
            half(s, 1, LAYERS - 1, LAYERS - 1, None)
            mlp(s, 1, LAYERS - 1)

        def one(name, n):
            t = a[name][bass.ds(n, 1)] if not isinstance(n, int) else a[name][n:n + 1]
            return t.rearrange("e p n -> (e p) n")

        def load_w1(sp, n):
            sp.dma_start(w1[:, 0, :], one("w1_a", n)).then_inc(w1_in, 16)
            sp.dma_start(w1[0:64, 1, :], one("w1_b", n)).then_inc(w1_in, 16)

        def load_w2(sp, n):
            sp.dma_start(w2[:, :, :].rearrange("p c n -> p (c n)"), one("w2", n)).then_inc(w2_in, 16)

        def load_qkv(sp, n):
            sp.dma_start(l_qkv_w[:, 0, :], one("qkv_a", n)).then_inc(l_qkv_in, 16)
            sp.dma_start(l_qkv_w[0:64, 1, 0:3 * CH[1]], one("qkv_b", n)).then_inc(l_qkv_in, 16)

        def load_project_vectors(sp, n):
            sp.dma_start(p_cols[:, :], one("p_cols", n)).then_inc(l_pvec_in, 16)
            sp.dma_start(p_row[:, :], one("p_row", n).to_broadcast([TILE, 3 * D])).then_inc(l_pvec_in, 16)

        def load_mlp_vectors(sp, n):
            sp.dma_start(m_cols[:, :], one("m_cols", n)).then_inc(l_mvec_in, 16)
            sp.dma_start(m_row[:, :], one("m_row", n).to_broadcast([TILE, D])).then_inc(l_mvec_in, 16)

        def layers_sync(sp):
            load_qkv(sp, 0)
            load_project_vectors(sp, 0)
            load_mlp_vectors(sp, 0)
            load_w1(sp, 0)
            load_w2(sp, 0)

        def layers_sync_loop(sp):
            with sp.Fori(0, LAYERS - 1) as n:
                sp.wait_ge(qkv_done[1], n * NT + NT)
                load_qkv(sp, n + 1)
                sp.wait_ge(qkv_ready[1], n * NT + NT)
                load_project_vectors(sp, n + 1)
                sp.wait_ge(up_done1[1], n * MLPC + MLPC)
                load_w1(sp, n + 1)
                sp.wait_ge(gelu_ready[1], n * MLPC + MLPC)
                sp.wait_ge(r_biased[1], n + 1)
                load_mlp_vectors(sp, n + 1)
                sp.wait_ge(down_done1[1], n * NT + NT)
                load_w2(sp, n + 1)
            n = LAYERS - 1
            sp.wait_ge(up_done1[1], n * MLPC + MLPC)
            load_w1(sp, n + 1)
            sp.wait_ge(down_done1[1], n * NT + NT)
            load_w2(sp, n + 1)
            with sp.Fori(0, E2 - 1) as e:
                sp.wait_ge(up2_done, e * MLPC + MLPC)
                load_w1(sp, e + LAYERS + 1)
                sp.wait_ge(down2_done, e * TILES + TILES)
                load_w2(sp, e + LAYERS + 1)

        def layers_tensor(pe):
            class Tensor(Steps):
                def turn(self, b, n, second):
                    pe.wait_ge(l_normed[b], 2 * n + second + 1)
                    for c in range(2):
                        for j in range(NT):
                            last = nc.tensor.transpose(bank[0:CH[c], SIDE + c, j * TILE:(j + 1) * TILE],
                                                       xn[:, b * NT + j, c * 128:c * 128 + CH[c]], ident[0:TILE, 0:TILE])
                        last.then_inc(l_turned[b], 1)

                def values(self, b, n, j):
                    if j == 0:
                        pe.wait_ge(l_qkv_in, n * 32 + 32)
                        pe.wait_ge(l_xT[b], 4 * n + 2)
                    else:
                        pe.wait_ge(qkv_ready[b], n * NT + j)
                    for c in range(2):
                        last = nc.tensor.matmul(bank[0:TILE, SIDE + c, 0:3 * CH[c]], xT[:, c, b, j * TILE:(j + 1) * TILE],
                                                l_qkv_w[:, c, 0:3 * CH[c]], start=True, stop=True)
                    last.then_inc(qkv_done[b], 1)

                def turn_parts(self, dst, which, g):
                    for j in range(NT):
                        parts = qk_parts[:, which, j, 2 * g:2 * g + 2, :].rearrange("p h r -> p (h r)")
                        last = nc.tensor.matmul(dst[:, j * TILE:(j + 1) * TILE], parts, ident_r[:, :], start=True, stop=True)
                    return last

                def stack(self, b, n, u):
                    g, which = divmod(u, 2)
                    if u == 0:
                        pe.wait_ge(lo_ready[b], n * NT + NT)
                    if g >= 1:
                        pe.wait_ge((q_ready, k_ready)[which][b], n * GROUPS + g)
                    self.turn_parts(bank[:, SIDE + u % 2, 0:TOK], which, g).then_inc(stack_done[b], 1)

                def row(self, b, n, u):
                    g, j = divmod(u, NT)
                    if u == 0:
                        pe.wait_ge(q_ready[b], n * GROUPS + GROUPS)
                        pe.wait_ge(k_ready[b], n * GROUPS + GROUPS)
                    if u >= 2:
                        pe.wait_ge(row_taken[b], n * ROWS + u - 1)
                    for r in range(2):
                        rows = slice(STACK * r, STACK * r + STACK)
                        last = nc.tensor.matmul(bank[0:TILE, 2 * (u % 2) + r, 0:TOK], q_stack[rows, g, b, j * TILE:(j + 1) * TILE],
                                                k_stack[rows, g, b, :], start=True, stop=True)
                    last.then_inc(row_scores[b], 1)

                def shift(self, b, n, t):
                    if t < 2:
                        pe.wait_ge(row_taken[b], n * ROWS + ROWS - 1 + t)
                    else:
                        pe.wait_ge(shift_ready[b], n * SHIFTS + t - 1)
                    for h in range(2):
                        last = self.turn_parts(bank[:, 2 * (t % 2) + h, 0:TOK], 0, 2 * t + h)
                    last.then_inc(shift_done[b], 1)

                def scores(self, b, n, k):
                    quad, t = divmod(k, NT)
                    for h in range(2):
                        u, g = 2 * k + h, 2 * quad + h
                        if u == 0:
                            pe.wait_ge(shift_ready[b], n * SHIFTS + SHIFTS)
                        if u >= 2:
                            pe.wait_ge(probs_ready[b], n * UNITS + u - 1)
                        for r in range(2):
                            rows = slice(STACK * r, STACK * r + STACK)
                            last = nc.tensor.matmul(bank[0:TILE, 2 * (u % 2) + r, 0:TOK],
                                                    k_stack[rows, g, b, t * TILE:(t + 1) * TILE], q_stack[rows, g, b, :],
                                                    start=True, stop=True)
                        last.then_inc(scores_done[b], 1)

                def weigh(self, b, n, k):
                    quad, t = divmod(k, NT)
                    if t == 0 and quad >= 2:
                        pe.wait_ge(o_added[b], n * QUADS + quad - 1)
                    pe.wait_ge(probs_ready[b], n * UNITS + 2 * k + 2)
                    for r in range(4):
                        last = nc.tensor.matmul(bank[32 * r:32 * r + 32, 4 + quad % 2, 0:TOK], v_ext[:, b * NT + t, 4 * quad + r, :],
                                                probs[:, (2 * k + r // 2) % 4, r % 2, :], start=(t == 0), stop=(t == NT - 1))
                    last.then_inc(pv_done[b], 1)

                def turn_back(self, b, n, o):
                    pe.wait_ge(o_copied[b], n * QUADS + o + 1)
                    for j in range(NT):
                        last = nc.tensor.transpose(bank[0:TILE, 4 + o % 2, j * 128:(j + 1) * 128],
                                                   oT[:, o % 2, j * TILE:(j + 1) * TILE], ident[:, :])
                    last.then_inc(o_turned[b], 1)

                def up(self, b, n, m):
                    if m == 0:
                        pe.wait_ge(w1_in, n * 32 + 32)
                        pe.wait_ge(l_xT[b], 4 * n + 4)
                    if m >= 2:
                        pe.wait_ge(gelu_ready[b], n * MLPC + m - 1)
                    two_chunks(bank[:, SIDE + m % 2, 0:TOK], lambda c: w1[:, c, m * 128:(m + 1) * 128],
                               lambda c: xT[:, c, b, :]).then_inc(up_done1[b], 1)

                def down(self, b, n, j):
                    if j == 0:
                        pe.wait_ge(w2_in, n * 16 + 16)
                        pe.wait_ge(gelu_ready[b], n * MLPC + MLPC)
                    if j == 2:
                        pe.wait_ge(r_ready[b], n * NT + 1)
                    for c in range(MLPC):
                        last = nc.tensor.matmul(bank[0:TILE, SIDE + j % 2, 0:D], hidT[:, c, 0, j * TILE:(j + 1) * TILE], w2[:, c, :],
                                                start=(c == 0), stop=(c == MLPC - 1))
                    last.then_inc(down_done1[b], 1)

            s = Tensor()
            pe.wait_ge(presets, 5)
            begin(s)
            with pe.Fori(0, LAYERS - 1) as n:
                body(s, n)
            end(s)

        def layers_scalar(act):
            class Scalar(Steps):
                def clear(self, b, n):
                    act.wait_ge(shift_done[b], n * SHIFTS + SHIFTS)

                def split(self, b, n, j):
                    act.wait_ge(qkv_ready[b], n * NT + j + 1)
                    for which, dst in ((0, qk_parts[:, 0, j, :, 0:32].rearrange("p h (r d) -> p h r d", d=DH)),
                                       (1, qk_parts[:, 1, j, :, :].rearrange("p h (r d) -> p h r d", d=DH)[:, :, 0:3:2, :])):
                        src = qk_sum[:, which, j, :].rearrange("p (h d) -> p h d", d=DH)
                        last = nc.scalar.activation(dst, src.unsqueeze(2).to_broadcast([TILE, HEADS, 2, DH]), ACT.Copy)
                    last.then_inc(hi_ready[b], 1)

                def stack(self, b, n, u):
                    if u % 2 == 0:
                        act.wait_ge(stack_done[b], n * STACKS + u + 1)
                        nc.scalar.activation(q_stack[:, u // 2, b, :], bank[:, SIDE, 0:TOK], ACT.Copy).then_inc(q_ready[b], 1)

                def shift(self, b, n, t):
                    act.wait_ge(shift_done[b], n * SHIFTS + t + 1)
                    nc.scalar.activation(q_stack[:, 2 * t:2 * t + 2, b, :], bank[:, 2 * (t % 2):2 * (t % 2) + 2, 0:TOK],
                                         ACT.Copy).then_inc(shift_ready[b], 1)

                def exps(self, b, n, k):
                    for u in (2 * k, 2 * k + 1):
                        act.wait_ge(scores_done[b], n * UNITS + u + 1)
                        if u >= 4:
                            act.wait_ge(pv_done[b], n * STEPS + (u - 4) // 2 + 1)
                        nc.scalar.activation(probs[:, u % 4, :, :], bank[0:TILE, 2 * (u % 2):2 * (u % 2) + 2, 0:TOK], ACT.Exp,
                                             scale=float(DH) ** -0.5).then_inc(probs_ready[b], 1)

                def up(self, b, n, m):
                    if m == 0:
                        act.wait_ge(l_mvec_in, n * 32 + 32)
                    act.wait_ge(up_done1[b], n * MLPC + m + 1)
                    nc.scalar.activation(hidT[:, m, 0, :], bank[:, SIDE + m % 2, 0:TOK], ACT.Gelu,
                                         bias=m_cols[:, M_B1 + m:M_B1 + m + 1]).then_inc(gelu_ready[b], 1)

            s = Scalar()
            begin(s)
            with act.Fori(0, LAYERS - 1) as n:
                body(s, n)
            end(s)

        def layers_pool(pool):
            class Pool(Steps):
                def norm(self, b, n, second):
                    t = slice(b * NT, (b + 1) * NT)
                    k = 2 * n + second + 1
                    pool.wait_ge(l_var[b], k)
                    nc.gpsimd.tensor_tensor(veps[:, t], mv[:, t, 1], eps5[:, t], ALU.add).then_inc(l_eps[b], 1)
                    pool.wait_ge(l_eps[b], k)
                    nc.gpsimd.tensor_tensor(rstd[:, t], veps[:, t], minus_half[:, t], ALU.pow).then_inc(l_rstd[b], 1)

                def split(self, b, n, j):
                    pool.wait_ge(hi_ready[b], n * NT + j + 1)
                    for which, low in ((0, 2), (1, 1)):
                        view = qk_parts[:, which, j, :, :]
                        last = nc.gpsimd.tensor_tensor(view[:, :, DH * low:DH * (low + 1)],
                                                       qk_sum[:, which, j, :].rearrange("p (h d) -> p h d", d=DH),
                                                       view[:, :, 0:DH].bitcast(F32), ALU.subtract)
                    last.then_inc(lo_ready[b], 1)

            norm_rstd(pool, NORM_R, eps5, NORM_R)
            s = Pool()
            begin(s)
            with pool.Fori(0, LAYERS - 1) as n:
                body(s, n)
            end(s)

        def layers_vector(dve):
            class Vector(Steps):
                def norm(self, b, n, second):
                    for i in range(b * NT, (b + 1) * NT):
                        last = nc.vector.bn_stats(stats[:, i, :], R[:, i, :])
                    self.step(last)
                    nc.vector.memset(carrier[:, :], 0.0)
                    for i in range(b * NT, (b + 1) * NT):
                        last = nc.vector.bn_aggr(mv[:, i, :], stats[:, i, :])
                    last.then_inc(l_var[b], 1)

                def apply(self, b, n, second):
                    dve.wait_ge(l_rstd[b], 2 * n + second + 1)
                    for i in range(b * NT, (b + 1) * NT):
                        last = nc.vector.tensor_scalar(xn[:, i, :], R[:, i, :], mv[:, i, 0:1], rstd[:, i:i + 1],
                                                       ALU.subtract, ALU.mult)
                    last.then_inc(l_normed[b], 1)

                def turn(self, b, n, second):
                    if second:
                        dve.wait_ge(l_mvec_in, n * 32 + 32)
                        dve.wait_ge(l_normed[b], 2 * n + 2)
                        t = R[:, b * NT:(b + 1) * NT, :]
                        nc.vector.tensor_tensor(t, t, m_row[:, :].unsqueeze(1).to_broadcast([TILE, NT, D]),
                                                ALU.add).then_inc(r_biased[b], 1)
                    else:
                        dve.wait_ge(l_pvec_in, n * 32 + 32)
                    v = m_cols if second else p_cols
                    for c in range(2):
                        r = CH[c]
                        dve.wait_ge(l_turned[b], 4 * n + 2 * second + c + 1)
                        nc.vector.tensor_scalar(xT[0:r, c, b, :], bank[0:r, SIDE + c, 0:TOK], v[0:r, c:c + 1], v[0:r, 2 + c:3 + c],
                                                ALU.mult, ALU.add).then_inc(l_xT[b], 1)

                def clear(self, b, n):
                    dve.wait_ge(shift_done[b], n * SHIFTS + SHIFTS)
                    nc.vector.memset(qk_parts[:, 0, :, :, SHIFT_ROW:SHIFT_ROW + 1].bitcast(F32), 0.0)

                def values(self, b, n, j):
                    dve.wait_ge(qkv_done[b], n * NT + j + 1)
                    for c in range(2):
                        r, h = CH[c], CH[c] // DH
                        src = bank[0:TILE, SIDE + c, 0:3 * r].rearrange("p (w f) -> p w f", w=3)
                        bias = p_row[:, :].rearrange("p (w f) -> p w f", w=3)[:, :, 128 * c:128 * c + r]
                        nc.vector.tensor_tensor(qk_sum[:, :, j, 128 * c:128 * c + r], src[:, 0:2, :], bias[:, 0:2, :], ALU.add)
                        last = nc.vector.tensor_tensor(v_ext[:, b * NT + j, 8 * c:8 * c + h, 0:DH],
                                                       src[:, 2, :].rearrange("p (h d) -> p h d", d=DH),
                                                       bias[:, 2, :].rearrange("p (h d) -> p h d", d=DH), ALU.add)
                    last.then_inc(qkv_ready[b], 1)

                def stack(self, b, n, u):
                    if u % 2 == 1:
                        dve.wait_ge(stack_done[b], n * STACKS + u + 1)
                        nc.vector.tensor_copy(k_stack[:, u // 2, b, :], bank[:, SIDE + 1, 0:TOK]).then_inc(k_ready[b], 1)

                def row(self, b, n, u):
                    g, j = divmod(u, NT)
                    dve.wait_ge(row_scores[b], n * ROWS + u + 1)
                    nc.vector.tensor_reduce(qk_parts[:, 0, j, 2 * g:2 * g + 2, SHIFT_ROW], bank[0:TILE, 2 * (u % 2):2 * (u % 2) + 2, 0:TOK],
                                            AX.X, ALU.max, negate=True).then_inc(row_taken[b], 1)

                def collect(self, b, n, o):
                    dve.wait_ge(pv_done[b], n * STEPS + (o + 1) * NT)
                    nc.vector.tensor_copy(oT[:, o % 2, :], bank[:, 4 + o % 2, 0:TOK]).then_inc(o_copied[b], 1)

                def merge(self, b, n, o):
                    dve.wait_ge(o_turned[b], n * QUADS + o + 1)
                    src = bank[0:TILE, 4 + o % 2, 0:NT * 128].rearrange("p (j h d) -> p j h d", j=NT, d=32)
                    self.step(nc.vector.reciprocal(o_rec[:, :, :], src[:, :, :, DH]))
                    self.step(nc.vector.tensor_tensor(o_tmp[:, :, :, :], src[:, :, :, 0:DH],
                                                      o_rec[:, :, :].unsqueeze(3).to_broadcast([TILE, NT, 4, DH]), ALU.mult))
                    dst = R[:, b * NT:(b + 1) * NT, o * 64:(o + 1) * 64].rearrange("p j (h d) -> p j h d", d=DH)
                    nc.vector.tensor_tensor(dst, dst, o_tmp[:, :, :, :], ALU.add).then_inc(o_added[b], 1)
                    if o == QUADS - 1:
                        dve.wait_ge(o_added[b], n * QUADS + QUADS)

                def down(self, b, n, j):
                    dve.wait_ge(down_done1[b], n * NT + j + 1)
                    if j == 0:
                        dve.wait_ge(r_biased[b], n + 1)
                    nc.vector.tensor_tensor(R[:, b * NT + j, :], R[:, b * NT + j, :], bank[0:TILE, SIDE + j % 2, 0:D],
                                            ALU.add).then_inc(r_ready[b], 1)
                    if j == NT - 1:
                        dve.wait_ge(r_ready[b], n * NT + NT)

            def step(ins):
                linked(dve, ins)
            s = Vector()
            s.step = step
            nc.vector.tensor_copy(ident_r[:, :], ident[0:TILE, 0:TILE]).then_inc(presets, 1)
            nc.vector.memset(qk_parts[:, :, :, :, SHIFT_ROW:STACK].bitcast(F32), 0.0).then_inc(presets, 1)
            dve.wait_ge(presets, 2)
            nc.vector.memset(qk_parts[:, 1, :, :, SHIFT_ROW:SHIFT_ROW + 1].bitcast(F32), 1.0).then_inc(presets, 1)
            nc.vector.memset(v_ext[:, :, :, DH + 1:32], 0.0).then_inc(presets, 1)
            nc.vector.memset(v_ext[:, :, :, DH:DH + 1], 1.0).then_inc(presets, 1)
            norm_stats(dve, step, lambda i: H[:, i, :], full, NORM_R)
            norm_apply(dve, lambda i: H[:, i, :], lambda i: R[:, i, :], full, NORM_R)
            dve.wait_ge(normed, (NORM_R + 1) * TILES)
            begin(s)
            with dve.Fori(0, LAYERS - 1) as n:
                s.step, counted = loop_linker(dve, layer_link, n * LINKS)
                body(s, n)
            assert counted[0] == LINKS, counted
            s.step = step
            end(s)
            nc.vector.tensor_tensor(H[:, :, :], H[:, :, :], R[:, :, :], ALU.add).then_inc(h_layers, 1)
            dve.wait_ge(h_layers, 1)

        LINKS = 2 * (2 + 2 * QUADS)

        up2_done = sem("up2_done")
        act2_ready = sem("act2_ready")
        down2_done = sem("down2_done")

        def mlp_tensor(pe, e):
            pe.wait_ge(w1_in, (e + LAYERS) * 32 + 32)
            for m in range(MLPC):
                if m == 3:
                    pe.wait_ge(act2_ready, e * MLPC + 1)
                if m >= 4:
                    pe.wait_ge(act2_ready, e * MLPC + m - 3)
                for b in range(B):
                    last = two_chunks(bank[:, 2 * (m % 4) + b, 0:TOK], lambda c: w1[:, c, m * 128:(m + 1) * 128],
                                      lambda c: xT[:, c, b, :])
                last.then_inc(up2_done, 1)
            pe.wait_ge(w2_in, (e + LAYERS) * 16 + 16)
            pe.wait_ge(act2_ready, e * MLPC + MLPC)
            for i in range(TILES):
                b, j = divmod(i, NT)
                for c in range(MLPC):
                    last = nc.tensor.matmul(bank[0:TILE, 2 + i, 0:D], hidT[:, c, b, j * TILE:(j + 1) * TILE], w2[:, c, :],
                                            start=(c == 0), stop=(c == MLPC - 1))
                last.then_inc(down2_done, 1)

        raw = lb("raw", [TILE, E2, TILES, D])
        s_score = lb("s_score", [TILE, E2, TILES])
        s_mark = lb("s_mark", [TILE, E2, TILES])
        s_above = lb("s_above", [TILE, E2, TILES])
        s_rank = lb("s_rank", [TILE, E2, TILES])
        s_zero = lb("s_zero", [TILE, E2 * TILES])
        s_gate = lb("s_gate", [TILE, E2, TILES])
        s_least = lb("s_least", [TILE, 1])
        s_try = lb("s_try", [TILE, 1])
        s_ok = lb("s_ok", [TILE, 1])
        s_count = lb("s_count", [TILE, 1])
        s_total = lb("s_total", [TILE, 1])
        s_gateT = lb("s_gateT", [E2, B, TOK])

        g_in = sem("g_in")
        g_logits = sem("g_logits")
        g_exp_in = sem("g_exp_in")
        g_exp_done = sem("g_exp_done")
        bits_counted = sem("bits_counted")
        bits_total = sem("bits_total")
        ties_marked = sem("ties_marked")
        ties_ranked = sem("ties_ranked")
        gate_ready = sem("gate_ready")
        gate_turned = sem("gate_turned")
        gateT_ready = sem("gateT_ready")
        bias_done = sem("bias_done")
        raw_ready = sem("raw_ready")
        y_ready = sem("y_ready")
        y_added = sem("y_added")
        search_link = sem("search_link")

        BITS = 30
        EARLY = 5

        def mix2_sync(sp):
            sp.dma_start(gate2_w[:, 0, :], a["gate2"][0:128]).then_inc(g_in, 16)
            sp.dma_start(gate2_w[0:64, 1, :], a["gate2"][128:D]).then_inc(g_in, 16)
            sp.dma_start(b2_rows[:, :], a["mix_b2"]).then_inc(g_in, 16)
            sp.dma_start(b1_cols[:, :, :], a["mix_b1"]).then_inc(g_in, 16)

        def mix2_store(sp):
            for b in range(B):
                sp.wait_ge(y_ready, (b + 1) * NT)
                sp.dma_start(out[b].rearrange("(j p) d -> p j d", p=TILE), H[:, b * NT:(b + 1) * NT, :]).then_inc(stored, 16)
            sp.wait_ge(stored, 16 * B)

        def mix2_tensor(pe):
            turn(pe, xn, full, 2, normed, NORM_E * TILES)
            pe.wait_ge(g_in, 64)
            pe.wait_ge(xT_ready, turn_base(TURN_A, 3))
            for i in range(TILES):
                b, j = divmod(i, NT)
                last = two_chunks(bank[0:TILE, 0, i * E2:(i + 1) * E2], lambda c: xT[:, c, b, j * TILE:(j + 1) * TILE],
                                  lambda c: gate2_w[:, c, :])
            last.then_inc(g_logits, 1)
            pe.wait_ge(g_exp_in, 1)

            def experts(first, end):
                with pe.Fori(first, end) as e:
                    mlp_tensor(pe, e)
                    pe.wait_ge(raw_ready, e * TILES + 4)
            experts(0, EARLY)
            pe.wait_ge(raw_ready, EARLY * TILES)
            pe.wait_ge(ties_marked, 1)
            mark = s_mark[:, :, :].rearrange("p e i -> p (e i)")
            nc.tensor.matmul(bank[0:TILE, 0, 0:E2 * TILES], lower[0:TILE, :], mark, start=True, stop=True)
            nc.tensor.matmul(bank[0:TILE, 1, 0:E2 * TILES], ones[0:TILE, 0:TILE], mark, start=True, stop=True).then_inc(ties_ranked, 1)
            pe.wait_ge(gate_ready, 1)
            for i in range(TILES):
                last = nc.tensor.transpose(bank[0:E2, 2 + i // NT, (i % NT) * TILE:(i % NT + 1) * TILE], s_gate[:, :, i],
                                           ident[0:TILE, 0:TILE])
            last.then_inc(gate_turned, 1)
            pe.wait_ge(gateT_ready, 1)
            experts(EARLY, E2)
            pe.wait_ge(raw_ready, E2 * TILES)
            for i in range(TILES):
                b, j = divmod(i, NT)
                nc.tensor.matmul(bank[0:TILE, i, 0:D], s_gateT[:, b, j * TILE:(j + 1) * TILE], b2_rows[:, :],
                                 start=True, stop=True).then_inc(bias_done, 1)

        def mix2_scalar(act):
            act.wait_ge(g_exp_in, 1)
            nc.scalar.activation(m_work[:, :, :], m_work[:, :, :], ACT.Exp).then_inc(g_exp_done, 1)
            act.wait_ge(g_in, 64)
            with act.Fori(0, E2) as e:
                for m in range(MLPC):
                    act.wait_ge(up2_done, e * MLPC + m + 1)
                    nc.scalar.activation(hidT[:, m, :, :], bank[:, 2 * (m % 4):2 * (m % 4) + 2, 0:TOK], ACT.Gelu_apprx_tanh,
                                         bias=b1_cols[:, bass.ds(e, 1), m:m + 1].rearrange("p e m -> p (e m)")).then_inc(act2_ready, 1)
                for i in range(TILES):
                    act.wait_ge(down2_done, e * TILES + i + 1)
                    nc.scalar.activation(raw[:, bass.ds(e, 1), i, :].rearrange("p e d -> p (e d)"), bank[0:TILE, 2 + i, 0:D],
                                         ACT.Copy).then_inc(raw_ready, 1)

        def mix2_pool(pool):
            norm_rstd(pool, NORM_E, eps5, NORM_E)
            for t in range(BITS):
                pool.wait_ge(bits_counted, t + 1)
                nc.gpsimd.partition_all_reduce(s_total[:, :], s_count[:, :], TILE, bass.bass_isa.ReduceOp.add).then_inc(bits_total, 1)
            pool.wait_ge(bits_counted, BITS + 1)
            nc.gpsimd.partition_all_reduce(s_total[:, :], s_count[:, :], TILE, bass.bass_isa.ReduceOp.add).then_inc(bits_total, 1)

        def mix2_vector(dve):
            def step(ins):
                linked(dve, ins)
            shape = [TILE, TILES, E2]
            norm_stats(dve, step, lambda i: H[:, i, :], full, NORM_E)
            norm_apply(dve, lambda i: H[:, i, :], lambda i: xn[:, i, :], full, NORM_E)
            turned_out(dve, TOK, 2, turn_base(TURN_A, 2))
            dve.wait_ge(g_logits, 1)
            softmax8(dve, step, bank[0:TILE, 0, 0:TILES * E2].rearrange("p (i e) -> p i e", e=E2), g_exp_in, g_exp_done,
                     shape)
            step(nc.vector.tensor_copy(s_score[:, :, :].rearrange("p e i -> p i e"), m_p[:, :, :]))
            nc.vector.memset(s_zero[:, :], 0.0)
            step(nc.vector.memset(s_least[:, :], 0.0))
            score = s_score[:, :, :].rearrange("p e i -> p (e i)")
            markf = s_mark[:, :, :].rearrange("p e i -> p (e i)")
            above = s_above[:, :, :].rearrange("p e i -> p (e i)")
            for t in range(BITS):
                step(nc.vector.tensor_scalar(s_try[:, :].bitcast(I32), s_least[:, :].bitcast(I32), 1 << (BITS - 1 - t), None,
                                             ALU.bitwise_or))
                nc.vector.tensor_scalar(markf, score, s_try[:, 0:1], None, ALU.is_ge, ALU.add,
                                        accum_out=s_count[:, :]).then_inc(bits_counted, 1)
                dve.wait_ge(bits_total, t + 1)
                step(nc.vector.tensor_scalar(s_ok[:, :], s_total[:, :], float(PICKED), s_try[:, 0:1], ALU.is_ge, ALU.mult))
                step(nc.vector.tensor_tensor(s_least[:, :], s_least[:, :], s_ok[:, :], ALU.max))
            nc.vector.tensor_scalar(above, score, s_least[:, 0:1], None, ALU.is_gt, ALU.add,
                                    accum_out=s_count[:, :]).then_inc(bits_counted, 1)
            nc.vector.tensor_scalar(markf, score, s_least[:, 0:1], None, ALU.is_equal).then_inc(ties_marked, 1)
            dve.wait_ge(ties_ranked, 1)
            dve.wait_ge(bits_total, BITS + 1)
            step(nc.vector.tensor_scalar(s_ok[:, :], s_total[:, :], -1.0, float(PICKED), ALU.mult, ALU.add))
            rank = s_rank[:, :, :].rearrange("p e i -> p (e i)")
            step(nc.vector.tensor_copy(s_gate[:, :, :].rearrange("p e i -> p (e i)"), bank[0:TILE, 1, 0:E2 * TILES]))
            gate = s_gate[:, :, :].rearrange("p e i -> p (e i)")
            step(nc.vector.tensor_tensor_scan(rank, gate, s_zero[:, :], 0.0, ALU.add, ALU.add))
            step(nc.vector.tensor_tensor(rank, rank, gate, ALU.subtract))
            step(nc.vector.tensor_tensor(rank, rank, bank[0:TILE, 0, 0:E2 * TILES], ALU.add))
            step(nc.vector.scalar_tensor_tensor(rank, rank, s_ok[:, 0:1], markf, ALU.is_lt, ALU.mult))
            step(nc.vector.tensor_tensor(rank, rank, above, ALU.add))
            nc.vector.tensor_tensor(gate, rank, score, ALU.mult).then_inc(gate_ready, 1)
            dve.wait_ge(gate_turned, 1)
            nc.vector.tensor_copy(s_gateT[:, :, :], bank[0:E2, 2:4, 0:TOK]).then_inc(gateT_ready, 1)
            dve.wait_ge(gate_ready, 1)
            with dve.Fori(0, E2) as e:
                for i in range(TILES):
                    dve.wait_ge(raw_ready, e * TILES + i + 1)
                    nc.vector.scalar_tensor_tensor(H[:, i, :], raw[:, bass.ds(e, 1), i, :].rearrange("p e d -> p (e d)"),
                                                   s_gate[:, bass.ds(e, 1), i:i + 1].rearrange("p e i -> p (e i)"), H[:, i, :],
                                                   ALU.mult, ALU.add).then_inc(y_added, 1)
                dve.wait_ge(y_added, e * TILES + TILES)
            for i in range(TILES):
                dve.wait_ge(bias_done, i + 1)
                nc.vector.tensor_tensor(H[:, i, :], H[:, i, :], bank[0:TILE, i, 0:D], ALU.add).then_inc(y_ready, 1)

        later.close()

        block = ctx.enter_context(nc.Block())

        @block.sync
        def _(sp):
            sp.dma_start(cols[:, :], a["cols"]).then_inc(cols_in, 16)
            tokenizer_sync(sp)
            attn_sync(sp)
            mix_sync(sp)
            layers_sync(sp)
            mix2_sync(sp)
            mix_sync_loop(sp)
            layers_sync_loop(sp)
            mix2_store(sp)

        @block.gpsimd
        def _(pool):
            for w in (a_w, router_w, gate_up_w, l_qkv_w, w1, gate2_w):
                nc.gpsimd.memset(w[64:128, 1, :], 0.0)
            nc.gpsimd.memset(xT[64:128, 1, :, :], 0.0).then_inc(padded, 1)
            pool.wait_ge(padded, 1)
            nc.gpsimd.memset(minus_half[:, :], -0.5)
            nc.gpsimd.memset(eps5[:, :], 1e-5)
            nc.gpsimd.memset(eps6[:, :], 1e-6)
            nc.gpsimd.memset(ident[:, :], 0.0)
            nc.gpsimd.memset(ones[:, :], 1.0)
            nc.gpsimd.memset(lower[:, :], 1.0)
            nc.gpsimd.memset(head64[:, :], float(T_DH) ** -0.5)
            nc.gpsimd.memset(head16[:, :], 1.0).then_inc(pool_const, 1)
            pool.wait_ge(pool_const, 1)
            nc.gpsimd.affine_select(out=ident[:, :], in_=ident[:, :], compare_op=ALU.not_equal, fill=1.0, base=0,
                                    pattern=[[-1, 128]], channel_multiplier=1).then_inc(consts_ready, 4)
            nc.gpsimd.affine_select(out=lower[:, :], in_=lower[:, :], compare_op=ALU.is_gt, fill=0.0, base=0,
                                    pattern=[[1, TILE]], channel_multiplier=-1).then_inc(pool_const, 1)
            n = 2
            for mask, width in ((head64, T_DH), (head16, DH)):
                view = mask[:, :].rearrange("p (h d) -> p h d", d=width)
                nc.gpsimd.affine_select(out=view, in_=view, compare_op=ALU.is_ge, fill=0.0, base=0,
                                        pattern=[[-width, 128 // width], [0, width]], channel_multiplier=1).then_inc(pool_const, 1)
                n += 1
                pool.wait_ge(pool_const, n)
                nc.gpsimd.affine_select(out=view, in_=view, compare_op=ALU.is_ge, fill=0.0, base=width - 1,
                                        pattern=[[width, 128 // width], [0, width]], channel_multiplier=-1).then_inc(pool_const, 1)
                n += 1
                pool.wait_ge(pool_const, n)
            nc.gpsimd.iota(rank8[:, 0, :], pattern=[[-1, E1]], base=E1, channel_multiplier=0,
                           allow_small_or_imprecise_dtypes=True).then_inc(masks_ready, 1)
            tokenizer_pool(pool)
            norm_rstd(pool, NORM_A, eps5, NORM_A)
            mix_pool(pool)
            layers_pool(pool)
            mix2_pool(pool)

        @block.tensor
        def _(pe):
            tokenizer_tensor(pe)
            attn_tensor(pe)
            mix_tensor(pe)
            layers_tensor(pe)
            mix2_tensor(pe)

        @block.scalar
        def _(act):
            tokenizer_scalar(act)
            attn_scalar(act)
            mix_scalar(act)
            layers_scalar(act)
            mix2_scalar(act)

        @block.vector
        def _(dve):
            dve.wait_ge(cols_in, 16)
            dve.wait_ge(masks_ready, 1)
            tokenizer_vector(dve)
            attn_vector(dve)
            mix_vector(dve)
            layers_vector(dve)
            mix2_vector(dve)


def layout(x):
    f = lambda n: np.asarray(x[n])
    rows = lambda m, n=128: np.ascontiguousarray(m.reshape(-1, n, m.shape[-1]).transpose(1, 0, 2))
    col = lambda v: np.pad(v.reshape(-1, 1), ((0, 128 - v.size), (0, 0)))
    cut = lambda v: [col(v[k:k + 128]) for k in range(0, v.size, 128)]
    p = {}
    im = f("x").reshape(B, 32, 16, 8, 16, 8).transpose(1, 3, 5, 0, 2, 4).reshape(PATCH_K, B * IMG)
    p["patches"] = rows(im)
    p["conv_w"] = rows(f("L0_tok_conv_w").transpose(1, 2, 3, 0).reshape(PATCH_K, DT))
    p["t_qkv_w"] = f("L0_tok_qkv_w").transpose(1, 0, 2)
    p["t_out_w"] = f("L0_tok_out_w").reshape(T_LAYERS, IC, 128, DT).transpose(2, 0, 1, 3)
    p["t_ff1_w"] = f("L0_tok_ff1_w").transpose(1, 0, 2)
    p["t_ff2_w"] = f("L0_tok_ff2_w").reshape(T_LAYERS, FC, 128, DT).transpose(2, 0, 1, 3)
    p["t_head_w"] = f("L0_tok_head_w")
    p["t_rows"] = np.concatenate([v for l in range(T_LAYERS) for v in (f("L0_tok_out_b")[l], f("L0_tok_ff2_b")[l])]
                                 + [f("L0_tok_head_b")])[None]
    p["txt"] = f("txt")
    c = cut(f("L0_tok_conv_b"))
    for l in range(T_LAYERS):
        for n in ("ln1_g", "ln1_b", "ln2_g", "ln2_b", "ff1_b"):
            c += cut(f("L0_tok_" + n)[l])
    c += cut(f("L0_tok_lnf_g")) + cut(f("L0_tok_lnf_b")) + cut(f("L0_ffn_norm_w"))
    p["cols"] = np.concatenate(c, 1)
    p["a_w"] = f("L0_attn_w_qkv").T
    p["a_proj_w"] = f("L0_attn_w_proj").T
    p["a_row"] = f("L0_attn_b_proj")[None]
    p["router"] = f("L0_ffn_router_w").T
    gu = np.concatenate([f("L0_ffn_gate_w").transpose(0, 2, 1), f("L0_ffn_up_w").transpose(0, 2, 1)], 2)
    p["gate_up_a"], p["gate_up_b"] = gu[:, :128], gu[:, 128:]
    p["down"] = f("L0_ffn_down_w").transpose(0, 2, 1).reshape(E1, F1C, 128, D).transpose(0, 2, 1, 3)
    blocks = np.zeros((LAYERS, 3, D, D), np.float32)
    for h in range(HEADS):
        s = slice(DH * h, DH * (h + 1))
        for which, n in enumerate("qkv"):
            blocks[:, which, s, s] = f(f"L1_attn_{n}w")[:, h].transpose(0, 2, 1)
    for n, s in (("qkv_a", slice(0, 128)), ("qkv_b", slice(128, D))):
        p[n] = blocks[:, :, s, s].transpose(0, 2, 1, 3).reshape(LAYERS, s.stop - s.start, -1)
    stacked = lambda names, rest: np.stack([np.concatenate([c for n in names for c in cut(f("L1_attn_" + n)[l])] + rest(l), 1)
                                            for l in range(LAYERS)])
    p["p_cols"] = stacked(("ln1_g", "ln1_b"), lambda l: [])
    p["m_cols"] = stacked(("ln2_g", "ln2_b", "b1"), lambda l: [])
    p["p_row"] = np.concatenate([f(f"L1_attn_{n}b").reshape(LAYERS, 1, D) for n in "qkv"], 2)
    p["m_row"] = f("L1_attn_b2").reshape(LAYERS, 1, D)
    first = np.concatenate([f("L1_attn_w1").transpose(0, 2, 1), f("L1_ffn_w1")])
    second = np.concatenate([f("L1_attn_w2").transpose(0, 2, 1), f("L1_ffn_w2")])
    p["w1_a"], p["w1_b"] = first[:, :128], first[:, 128:]
    p["w2"] = second.reshape(LAYERS + E2, MLPC, 128, D).transpose(0, 2, 1, 3).reshape(LAYERS + E2, 128, MLPC * D)
    p["gate2"] = f("L1_ffn_gate_weight").T
    p["mix_b1"] = f("L1_ffn_b1").reshape(E2, H2C, 128).transpose(2, 0, 1)
    p["mix_b2"] = f("L1_ffn_b2")
    return {n: np.ascontiguousarray(v) for n, v in p.items()}


def kernel(**inputs):
    import concourse.bacc as bacc
    from concourse.bass_utils import run_bass_kernel_spmd

    arrays = layout(inputs)
    nc = bacc.Bacc("TRN2", target_bir_lowering=False, num_devices=1)
    a = {n: nc.dram_tensor("in_" + n, v.shape, mybir.dt.from_np(v.dtype), kind="ExternalInput").ap() for n, v in arrays.items()}
    out = nc.dram_tensor("out", (B, TOK, D), F32, kind="ExternalOutput").ap()
    build(nc, a, out)
    r = run_bass_kernel_spmd(nc, [{"in_" + n: v for n, v in arrays.items()}], core_ids=[0])
    return r.results[0]["out"]
```

```python
from contextlib import ExitStack

import numpy as np

import concourse.bass as bass
from concourse import mybir

F32 = mybir.dt.float32
F32R = mybir.dt.float32r
I32 = mybir.dt.int32
ALU = mybir.AluOpType
ACT = mybir.ActivationFunctionType
AX = mybir.AxisListType

B = 2
D = 192
CH = (128, 64)
TILE = 96
NT = 3
TILES = B * NT
TOK = NT * TILE
IMG = 256
TXT = TOK - IMG

DT, T_LAYERS, T_HEADS, T_DH, T_FF = 128, 2, 8, 64, 512
INNER = T_HEADS * T_DH
PATCH_K = 32 * 8 * 8
PK = PATCH_K // 128
PATCH_LOADS = 4
T_ROWS = (TILE, TILE, IMG - 2 * TILE)
IC = INNER // 128
FC = T_FF // 128
HEADS, DH = 12, 16
E1, F1, F1C = 8, 384, 3
LAYERS, MLP, MLPC = 8, 768, 6
HALF = D // 2
GROUPS = HEADS // 2
STACK = 64
SHIFT_ROW = 48
QUADS = 3
E2, H2, H2C = 8, 768, 6
CAPACITY = 2
PICKED = B * TOK * CAPACITY

C_CONVB = 0
C_T = 1
C_T_N = 4 + FC
C_LNF = C_T + T_LAYERS * C_T_N
C_NORMW = C_LNF + 2
C_N = C_NORMW + 2

P_BQ = 4
P_N = P_BQ + 4
M_B1 = 4
M_N = M_B1 + MLPC


def build(nc, a, out):
    ctx = ExitStack()

    def sb(name, shape, dt=F32):
        return ctx.enter_context(nc.sbuf_tensor(name, shape, dt))

    def sem(name):
        return ctx.enter_context(nc.semaphore(name))

    with ctx:
        bank = ctx.enter_context(nc.psum_tensor("bank", [128, 8, 512], F32))

        ident = sb("ident", [128, 128])
        ones = sb("ones", [128, 128])
        lower = sb("lower", [128, TILE])
        head64 = sb("head64", [128, 128])
        head16 = sb("head16", [128, 128])
        rank8 = sb("rank8", [TILE, 1, E1])
        minus_half = sb("minus_half", [TILE, TILES])
        eps5 = sb("eps5", [TILE, TILES])
        eps6 = sb("eps6", [TILE, TILES])
        carrier = sb("carrier", [1, 1])
        pool_carrier = sb("pool_carrier", [1, 1])
        cols = sb("cols", [128, C_N])
        H = sb("H", [TILE, TILES, D])
        xn = sb("xn", [TILE, TILES, D])
        xT = sb("xT", [128, 2, B, TOK])
        stats = sb("stats", [TILE, TILES, 6])
        mv = sb("mv", [TILE, TILES, 2])
        veps = sb("veps", [TILE, TILES])
        rstd = sb("rstd", [TILE, TILES])

        pool_const = sem("pool_const")
        masks_ready = sem("masks_ready")
        cols_in = sem("cols_in")
        link = sem("link")
        var_ready = sem("var_ready")
        rstd_ready = sem("rstd_ready")
        pool_step = sem("pool_step")
        normed = sem("normed")
        turned = sem("turned")
        xT_ready = sem("xT_ready")
        stored = sem("stored")

        NORM_T = 0
        NORM_A = 2 * T_LAYERS + 1
        NORM_M = NORM_A + 1
        NORM_R = NORM_M + 2
        NORM_E = NORM_R + 1
        TURN_A = NORM_A
        def turn_base(n_tok, n_full):
            return n_tok * B + n_full * 2 * B

        n_link = [0]

        def linked(dve, ins):
            n_link[0] += 1
            ins.then_inc(link, 1)
            dve.wait_ge(link, n_link[0])

        def loop_linker(dve, signal, base):
            n = [0]

            def step(ins):
                n[0] += 1
                ins.then_inc(signal, 1)
                dve.wait_ge(signal, base + n[0])
            return step, n

        def norm_stats(dve, step, src, rows, norm, rms=False):
            for i in range(TILES):
                last = nc.vector.bn_stats(stats[0:rows[i % NT], i, :], src(i))
            step(last)
            nc.vector.memset(carrier[:, :], 0.0)
            for i in range(TILES):
                r = rows[i % NT]
                last = nc.vector.bn_aggr(mv[0:r, i, :], stats[0:r, i, :])
            if rms:
                step(last)
                step(nc.vector.tensor_tensor(veps[:, :], mv[:, :, 0], mv[:, :, 0], ALU.mult))
                step(nc.vector.tensor_tensor(mv[:, :, 1], mv[:, :, 1], veps[:, :], ALU.add))
                last = nc.vector.memset(mv[:, :, 0], 0.0)
            last.then_inc(var_ready, 1)

        def norm_rstd(pool, norm, eps, n_step):
            pool.wait_ge(var_ready, norm + 1)
            nc.gpsimd.tensor_tensor(veps[:, :], mv[:, :, 1], eps[:, :], ALU.add).then_inc(pool_step, 1)
            pool.wait_ge(pool_step, n_step + 1)
            nc.gpsimd.tensor_tensor(rstd[:, :], veps[:, :], minus_half[:, :], ALU.pow).then_inc(rstd_ready, 1)

        def norm_apply(dve, src, dst, rows, norm):
            dve.wait_ge(rstd_ready, norm + 1)
            for i in range(TILES):
                r = rows[i % NT]
                nc.vector.tensor_scalar(dst(i), src(i), mv[0:r, i, 0:1], rstd[0:r, i:i + 1],
                                        ALU.subtract, ALU.mult).then_inc(normed, 1)

        def turn(pe, src, rows, chunks, signal, base, first=4):
            for b in range(B):
                for c in range(chunks):
                    for j in range(NT):
                        i = b * NT + j
                        r = rows[j]
                        if c == 0:
                            pe.wait_ge(signal, base + i + 1)
                        last = nc.tensor.transpose(bank[0:CH[c], first + b * chunks + c, j * TILE:j * TILE + r],
                                                   src[0:r, i, c * 128:c * 128 + CH[c]], ident[0:r, 0:r])
                    last.then_inc(turned, 1)

        def turned_out(dve, tokens, chunks, base, gain=None, shift=None, first=4):
            for b in range(B):
                for c in range(chunks):
                    n = CH[c]
                    src = bank[0:n, first + b * chunks + c, 0:tokens]
                    dve.wait_ge(turned, base + b * chunks + c + 1)
                    if gain is None:
                        ins = nc.vector.tensor_copy(xT[0:n, c, b, 0:tokens], src)
                    elif shift is None:
                        ins = nc.vector.tensor_scalar(xT[0:n, c, b, 0:tokens], src, gain(c), None, ALU.mult)
                    else:
                        ins = nc.vector.tensor_scalar(xT[0:n, c, b, 0:tokens], src, gain(c), shift(c),
                                                      ALU.mult, ALU.add)
                    ins.then_inc(xT_ready, 1)

        full = (TILE,) * NT

        a_w = sb("a_w", [128, 2, 3 * D])
        a_proj_w = sb("a_proj_w", [128, 2, D])
        a_row = sb("a_row", [TILE, D])
        router_w = sb("router_w", [128, 2, E1])
        gate_up_w = sb("gate_up_w", [128, 2, 2 * F1])
        down_w = sb("down_w", [128, F1C, D])
        p_cols = sb("p_cols", [128, P_N])
        m_cols = sb("m_cols", [128, M_N])
        p_row = sb("p_row", [TILE, D])
        m_row = sb("m_row", [TILE, D])
        l_qkv_w = sb("l_qkv_w", [128, 2, 3 * HALF])
        w1 = sb("w1", [128, 2, MLP])
        w2 = sb("w2", [128, MLPC, D])
        gate2_w = sb("gate2_w", [128, 2, E2])
        b2_rows = sb("b2_rows", [E2, D])
        b1_cols = sb("b1_cols", [128, E2, H2C])

        stage = ExitStack()

        def tb(name, shape, dt=F32):
            return stage.enter_context(nc.sbuf_tensor(name, shape, dt))

        patches = tb("patches", [128, PK, B * IMG])
        conv_w = tb("conv_w", [128, PK, DT])
        t_qkv_w = tb("t_qkv_w", [128, T_LAYERS, 3 * INNER])
        t_out_w = tb("t_out_w", [128, T_LAYERS, IC, DT])
        t_ff1_w = tb("t_ff1_w", [128, T_LAYERS, T_FF])
        t_ff2_w = tb("t_ff2_w", [128, T_LAYERS, FC, DT])
        t_head_w = tb("t_head_w", [128, D])
        t_rows = tb("t_rows", [TILE, T_LAYERS * 2 * DT + D])
        convT = tb("convT", [128, B, IMG])
        X = tb("X", [TILE, TILES, DT])
        tq = tb("tq", [TILE, TILES, INNER])
        tv = tb("tv", [TILE, TILES, INNER])
        tk = tb("tk", [TILE, TILES, INNER])
        tkT = tb("tkT", [128, IC, B, IMG])
        tqT = tb("tqT", [128, IC, B, IMG])
        tctx = tb("tctx", [128, B, IC, 128])
        tq_max = tb("tq_max", [TILE, TILES, T_HEADS])
        tq_sum = tb("tq_sum", [TILE, TILES, T_HEADS])
        tk_max = tb("tk_max", [128, IC, B])
        tk_sum = tb("tk_sum", [128, IC, B])
        tk_rec = tb("tk_rec", [128, IC, B])

        patches_in = [sem(f"patches_in{n}") for n in range(PATCH_LOADS)]
        t_w_in = [sem(f"t_w_in{n}") for n in range(3)]
        txt_in = sem("txt_in")
        conv_done = sem("conv_done")
        convT_ready = sem("convT_ready")
        x_turned = sem("x_turned")
        x_ready = sem("x_ready")
        tq_done = sem("tq_done")
        tv_done = sem("tv_done")
        tkT_done = sem("tkT_done")
        tv_copied = sem("tv_copied")
        tq_maxed = sem("tq_maxed")
        tq_exp = sem("tq_exp")
        tq_norm = sem("tq_norm")
        tk_maxed = sem("tk_maxed")
        tk_exp = sem("tk_exp")
        tk_turned = sem("tk_turned")
        tk_ready = sem("tk_ready")
        tq_turned = sem("tq_turned")
        tqT_ready = sem("tqT_ready")
        tctx_done = sem("tctx_done")
        tctx_ready = sem("tctx_ready")
        tatt_done = sem("tatt_done")
        tatt_ready = sem("tatt_ready")
        tproj_done = sem("tproj_done")
        x_attn = sem("x_attn")
        tff1_done = sem("tff1_done")
        tff1_act = sem("tff1_act")
        tff2_done = sem("tff2_done")
        head_done = sem("head_done")
        h_tok = sem("h_tok")

        def tok_tile(t, i):
            return t[0:T_ROWS[i % NT], i, :]

        def tokenizer_sync(sp):
            sp.dma_start(conv_w[:, :, :], a["conv_w"]).then_inc(patches_in[0], 16)
            n = PK // PATCH_LOADS
            for k in range(PATCH_LOADS):
                sp.dma_start(patches[:, k * n:(k + 1) * n, :], a["patches"][:, k * n:(k + 1) * n, :]).then_inc(patches_in[k], 16)
            sp.dma_start(t_qkv_w[:, :, :], a["t_qkv_w"]).then_inc(t_w_in[0], 16)
            sp.dma_start(t_out_w[:, :, :, :], a["t_out_w"]).then_inc(t_w_in[1], 16)
            sp.dma_start(t_rows[:, :], a["t_rows"].to_broadcast([TILE, T_LAYERS * 2 * DT + D])).then_inc(t_w_in[1], 16)
            sp.dma_start(t_ff1_w[:, :, :], a["t_ff1_w"]).then_inc(t_w_in[2], 16)
            sp.dma_start(t_ff2_w[:, :, :, :], a["t_ff2_w"]).then_inc(t_w_in[2], 16)
            sp.dma_start(t_head_w[:, :], a["t_head_w"]).then_inc(t_w_in[2], 16)
            for b in range(B):
                sp.dma_start(H[T_ROWS[2]:TILE, b * NT + 2, :], a["txt"][b]).then_inc(txt_in, 16)

        def tokenizer_tensor(pe):
            n = PK // PATCH_LOADS
            for k in range(PK):
                if k % n == 0:
                    pe.wait_ge(patches_in[k // n], 32 if k == 0 else 16)
                last = nc.tensor.matmul(bank[:, 0, :], conv_w[:, k, :], patches[:, k, :], start=(k == 0), stop=(k == PK - 1))
            last.then_inc(conv_done, 1)
            pe.wait_ge(masks_ready, 1)
            pe.wait_ge(convT_ready, 1)
            for b in range(B):
                for j in range(NT):
                    r = T_ROWS[j]
                    last = nc.tensor.transpose(bank[0:r, 1 + b, j * 128:(j + 1) * 128],
                                               convT[:, b, j * TILE:j * TILE + r], ident[:, :])
                last.then_inc(x_turned, 1)
            for l in range(T_LAYERS):
                turn(pe, xn, T_ROWS, 1, normed, 2 * l * TILES)
                pe.wait_ge(t_w_in[0], 16)
                for which, signal in ((0, tq_done), (2, tv_done)):
                    for i in range(TILES):
                        b, j = divmod(i, NT)
                        if i == 0 and which == 0:
                            pe.wait_ge(xT_ready, turn_base(2 * l, 0) + B)
                        if which == 0 and i >= 4:
                            pe.wait_ge(tq_maxed, l * TILES + i - 3)
                        if which == 2:
                            if i < 4:
                                pe.wait_ge(tq_maxed, l * TILES + min(i + 5, TILES) if i < 2 else l * TILES + i + 1)
                            else:
                                pe.wait_ge(tv_copied, l * TILES + i - 3)
                        nc.tensor.matmul(bank[0:T_ROWS[j], i % 4, :], xT[:, 0, b, j * TILE:j * TILE + T_ROWS[j]],
                                         t_qkv_w[:, l, which * INNER:(which + 1) * INNER],
                                         start=True, stop=True).then_inc(signal, 1)
                for c in range(IC):
                    nc.tensor.matmul(bank[:, 4 + c, :].rearrange("p (b n) -> p b n", b=B),
                                     t_qkv_w[:, l, INNER + c * 128:INNER + (c + 1) * 128],
                                     xT[:, 0, :, 0:IMG], start=True, stop=True).then_inc(tkT_done, 1)
                for i in range(TILES):
                    b, j = divmod(i, NT)
                    r = T_ROWS[j]
                    if i < 4:
                        pe.wait_ge(tv_copied, l * TILES + (i + 5 if i < 2 else i + 1))
                    else:
                        pe.wait_ge(tk_ready, l * TILES + i - 3)
                    for c in range(IC):
                        if j == 0:
                            pe.wait_ge(tk_exp, (l * B + b) * IC + c + 1)
                        last = nc.tensor.transpose(bank[0:r, i % 4, c * 128:(c + 1) * 128],
                                                   tkT[:, c, b, j * TILE:j * TILE + r], ident[:, :])
                    last.then_inc(tk_turned, 1)
                for c in range(IC):
                    if c == 0:
                        pe.wait_ge(tk_exp, (l + 1) * B * IC)
                        pe.wait_ge(tq_norm, (l + 1) * TILES)
                    for i in range(TILES):
                        b, j = divmod(i, NT)
                        r = T_ROWS[j]
                        last = nc.tensor.transpose(bank[:, 4 + c, b * IMG + j * TILE:b * IMG + j * TILE + r],
                                                   tq[0:r, i, c * 128:(c + 1) * 128], ident[0:r, 0:r])
                    last.then_inc(tq_turned, 1)
                pe.wait_ge(tk_ready, (l + 1) * TILES)
                for b in range(B):
                    for c in range(IC):
                        if b == 1:
                            pe.wait_ge(tctx_ready, l * B * IC + c + 1)
                        for j in range(NT):
                            i = b * NT + j
                            r = T_ROWS[j]
                            last = nc.tensor.matmul(bank[:, c, 0:128], tk[0:r, i, c * 128:(c + 1) * 128],
                                                    tv[0:r, i, c * 128:(c + 1) * 128], start=(j == 0), stop=(j == NT - 1))
                        last.then_inc(tctx_done, 1)
                for c in range(IC):
                    pe.wait_ge(tqT_ready, l * IC + c + 1)
                    pe.wait_ge(tctx_ready, l * B * IC + IC + c + 1)
                    for b in range(B):
                        last = nc.tensor.matmul(bank[:, 4 + c, b * IMG:(b + 1) * IMG], tctx[:, b, c, :], tqT[:, c, b, :],
                                                start=True, stop=True)
                    last.then_inc(tatt_done, 1)
                pe.wait_ge(t_w_in[1], 32)
                for i in range(TILES):
                    b, j = divmod(i, NT)
                    r = T_ROWS[j]
                    if i == 0:
                        pe.wait_ge(tatt_ready, (l + 1) * IC)
                    if i >= 4:
                        pe.wait_ge(x_attn, l * TILES + i - 3)
                    for c in range(IC):
                        last = nc.tensor.matmul(bank[0:r, i % 4, 0:DT], tqT[:, c, b, j * TILE:j * TILE + r],
                                                t_out_w[:, l, c, :], start=(c == 0), stop=(c == IC - 1))
                    last.then_inc(tproj_done, 1)
                turn(pe, xn, T_ROWS, 1, normed, (2 * l + 1) * TILES)
                pe.wait_ge(t_w_in[2], 48)
                pe.wait_ge(xT_ready, turn_base(2 * l + 1, 0) + B)
                for c in range(FC):
                    nc.tensor.matmul(bank[:, c, :].rearrange("p (b n) -> p b n", b=B), t_ff1_w[:, l, c * 128:(c + 1) * 128],
                                     xT[:, 0, :, 0:IMG], start=True, stop=True).then_inc(tff1_done, 1)
                for i in range(TILES):
                    b, j = divmod(i, NT)
                    r = T_ROWS[j]
                    if i == 0:
                        pe.wait_ge(tff1_act, (l + 1) * FC)
                    if i >= 2:
                        pe.wait_ge(x_ready, l * TILES + i - 1)
                    for c in range(FC):
                        last = nc.tensor.matmul(bank[0:r, 6 + i % 2, 0:DT], tqT[:, c, b, j * TILE:j * TILE + r],
                                                t_ff2_w[:, l, c, :], start=(c == 0), stop=(c == FC - 1))
                    last.then_inc(tff2_done, 1)
            turn(pe, xn, T_ROWS, 1, normed, 2 * T_LAYERS * TILES)
            pe.wait_ge(xT_ready, turn_base(2 * T_LAYERS, 0) + B)
            for i in range(TILES):
                b, j = divmod(i, NT)
                r = T_ROWS[j]
                if i >= 4:
                    pe.wait_ge(h_tok, i - 3)
                nc.tensor.matmul(bank[0:r, i % 4, 0:D], xT[:, 0, b, j * TILE:j * TILE + r], t_head_w[:, :],
                                 start=True, stop=True).then_inc(head_done, 1)

        def tokenizer_scalar(act):
            act.wait_ge(cols_in, 16)
            act.wait_ge(conv_done, 1)
            nc.scalar.activation(convT[:, :, :].rearrange("p b n -> p (b n)"), bank[:, 0, :], ACT.Identity,
                                 bias=cols[:, C_CONVB:C_CONVB + 1]).then_inc(convT_ready, 1)
            for l in range(T_LAYERS):
                c0 = C_T + l * C_T_N
                for i in range(TILES):
                    act.wait_ge(tq_maxed, l * TILES + i + 1)
                    nc.scalar.activation(tok_tile(tq, i), tok_tile(tq, i), ACT.Exp).then_inc(tq_exp, 1)
                for i in range(TILES):
                    act.wait_ge(tv_done, l * TILES + i + 1)
                    nc.scalar.activation(tok_tile(tv, i), bank[0:T_ROWS[i % NT], i % 4, :], ACT.Copy).then_inc(tv_copied, 1)
                for b in range(B):
                    for c in range(IC):
                        act.wait_ge(tk_maxed, l * IC + c + 1)
                        nc.scalar.activation(tkT[:, c, b, :], bank[:, 4 + c, b * IMG:(b + 1) * IMG], ACT.Exp,
                                             bias=tk_max[:, c, b:b + 1],
                                             accum_out=tk_sum[:, c, b:b + 1]).then_inc(tk_exp, 1)
                for i in range(TILES):
                    act.wait_ge(tk_turned, l * TILES + i + 1)
                    nc.scalar.activation(tok_tile(tk, i), bank[0:T_ROWS[i % NT], i % 4, :], ACT.Copy).then_inc(tk_ready, 1)
                for c in range(IC):
                    act.wait_ge(tq_turned, l * IC + c + 1)
                    nc.scalar.activation(tqT[:, c, :, :].rearrange("p b n -> p (b n)"), bank[:, 4 + c, :],
                                         ACT.Copy).then_inc(tqT_ready, 1)
                for c in range(IC):
                    act.wait_ge(tatt_done, l * IC + c + 1)
                    nc.scalar.activation(tqT[:, c, :, :].rearrange("p b n -> p (b n)"), bank[:, 4 + c, :],
                                         ACT.Copy).then_inc(tatt_ready, 1)
                for c in range(FC):
                    act.wait_ge(tff1_done, l * FC + c + 1)
                    nc.scalar.activation(tqT[:, c, :, :].rearrange("p b n -> p (b n)"), bank[:, c, :], ACT.Gelu,
                                         bias=cols[:, c0 + 4 + c:c0 + 5 + c]).then_inc(tff1_act, 1)

        def tokenizer_pool(pool):
            for n in range(2 * T_LAYERS + 1):
                norm_rstd(pool, n, eps5, n)

        def tokenizer_vector(dve):
            def step(ins):
                linked(dve, ins)
            step(nc.vector.memset(mv[:, :, :], 1.0))
            for b in range(B):
                dve.wait_ge(x_turned, b + 1)
                src = bank[:, 1 + b, :].rearrange("p (j n) -> p j n", n=128)
                nc.vector.tensor_copy(X[:, b * NT:b * NT + 2, :], src[0:TILE, 0:2, :])
                last = nc.vector.tensor_copy(X[0:T_ROWS[2], b * NT + 2, :], src[0:T_ROWS[2], 2, :])
            step(last)
            dve.wait_ge(t_w_in[1], 32)
            for l in range(T_LAYERS):
                c0 = C_T + l * C_T_N
                norm_stats(dve, step, lambda i: tok_tile(X, i), T_ROWS, 2 * l)
                norm_apply(dve, lambda i: tok_tile(X, i), lambda i: xn[0:T_ROWS[i % NT], i, 0:DT], T_ROWS, 2 * l)
                turned_out(dve, IMG, 1, turn_base(2 * l, 0), lambda c: cols[:, c0:c0 + 1], lambda c: cols[:, c0 + 1:c0 + 2])
                for i in range(TILES):
                    r = T_ROWS[i % NT]
                    dve.wait_ge(tq_done, l * TILES + i + 1)
                    q = bank[0:r, i % 4, :].rearrange("p (h d) -> p h d", h=T_HEADS)
                    step(nc.vector.tensor_reduce(tq_max[0:r, i, :], q, AX.X, ALU.max))
                    nc.vector.tensor_tensor(tok_tile(tq, i).rearrange("p (h d) -> p h d", h=T_HEADS), q,
                                            tq_max[0:r, i, :].unsqueeze(2).to_broadcast([r, T_HEADS, T_DH]),
                                            ALU.subtract).then_inc(tq_maxed, 1)
                for c in range(IC):
                    dve.wait_ge(tkT_done, l * IC + c + 1)
                    nc.vector.tensor_reduce(tk_max[:, c, :], bank[:, 4 + c, :].rearrange("p (b n) -> p b n", b=B),
                                            AX.X, ALU.max, negate=True).then_inc(tk_maxed, 1)
                for i in range(TILES):
                    r = T_ROWS[i % NT]
                    dve.wait_ge(tq_exp, l * TILES + i + 1)
                    q = tok_tile(tq, i).rearrange("p (h d) -> p h d", h=T_HEADS)
                    step(nc.vector.tensor_reduce(tq_max[0:r, i, :], q, AX.X, ALU.add))
                    step(nc.vector.reciprocal(tq_sum[0:r, i, :], tq_max[0:r, i, :]))
                    nc.vector.tensor_tensor(q, q, tq_sum[0:r, i, :].unsqueeze(2).to_broadcast([r, T_HEADS, T_DH]),
                                            ALU.mult).then_inc(tq_norm, 1)
                dve.wait_ge(tk_exp, (l + 1) * B * IC)
                step(nc.vector.reciprocal(tk_rec[:, :, :], tk_sum[:, :, :]))
                for b in range(B):
                    for c in range(IC):
                        dve.wait_ge(tctx_done, (l * B + b) * IC + c + 1)
                        nc.vector.scalar_tensor_tensor(tctx[:, b, c, :], bank[:, c, 0:128], tk_rec[:, c, b:b + 1],
                                                       head64[:, :], ALU.mult, ALU.mult).then_inc(tctx_ready, 1)
                rb = l * 2 * DT
                for i in range(TILES):
                    r = T_ROWS[i % NT]
                    last = nc.vector.tensor_tensor(tok_tile(X, i), tok_tile(X, i), t_rows[0:r, rb:rb + DT], ALU.add)
                step(last)
                for i in range(TILES):
                    r = T_ROWS[i % NT]
                    dve.wait_ge(tproj_done, l * TILES + i + 1)
                    last = nc.vector.tensor_tensor(tok_tile(X, i), tok_tile(X, i), bank[0:r, i % 4, 0:DT], ALU.add)
                    last.then_inc(x_attn, 1)
                dve.wait_ge(x_attn, (l + 1) * TILES)
                norm_stats(dve, step, lambda i: tok_tile(X, i), T_ROWS, 2 * l + 1)
                norm_apply(dve, lambda i: tok_tile(X, i), lambda i: xn[0:T_ROWS[i % NT], i, 0:DT], T_ROWS, 2 * l + 1)
                turned_out(dve, IMG, 1, turn_base(2 * l + 1, 0), lambda c: cols[:, c0 + 2:c0 + 3],
                           lambda c: cols[:, c0 + 3:c0 + 4])
                for i in range(TILES):
                    r = T_ROWS[i % NT]
                    last = nc.vector.tensor_tensor(tok_tile(X, i), tok_tile(X, i), t_rows[0:r, rb + DT:rb + 2 * DT], ALU.add)
                step(last)
                for i in range(TILES):
                    r = T_ROWS[i % NT]
                    dve.wait_ge(tff2_done, l * TILES + i + 1)
                    nc.vector.tensor_tensor(tok_tile(X, i), tok_tile(X, i), bank[0:r, 6 + i % 2, 0:DT],
                                            ALU.add).then_inc(x_ready, 1)
                dve.wait_ge(x_ready, (l + 1) * TILES)
            norm_stats(dve, step, lambda i: tok_tile(X, i), T_ROWS, 2 * T_LAYERS)
            norm_apply(dve, lambda i: tok_tile(X, i), lambda i: xn[0:T_ROWS[i % NT], i, 0:DT], T_ROWS, 2 * T_LAYERS)
            turned_out(dve, IMG, 1, turn_base(2 * T_LAYERS, 0), lambda c: cols[:, C_LNF:C_LNF + 1],
                       lambda c: cols[:, C_LNF + 1:C_LNF + 2])
            for i in range(TILES):
                r = T_ROWS[i % NT]
                dve.wait_ge(head_done, i + 1)
                nc.vector.tensor_tensor(H[0:r, i, :], bank[0:r, i % 4, 0:D], t_rows[0:r, T_LAYERS * 2 * DT:], ALU.add).then_inc(h_tok, 1)

        stage.close()
        later = ExitStack()

        def lb(name, shape, dt=F32):
            return later.enter_context(nc.sbuf_tensor(name, shape, dt))

        a_qT = lb("a_qT", [128, 2, B, TOK])
        a_kv = lb("a_kv", [TILE, TILES, 2 * D])
        a_kabs = lb("a_kabs", [TILE, TILES, D])
        a_qsum = lb("a_qsum", [128, 2, B])
        a_ksum = lb("a_ksum", [128, B, 2])
        a_rec = lb("a_rec", [128, B, 2])
        a_ctx = lb("a_ctx", [128, B, 2, 128])
        a_attT = lb("a_attT", [128, 2, B, TOK])
        m_in = lb("m_in", [TILE, TILES, D])
        m_prob = lb("m_prob", [TILE, E1, TILES])
        m_work = lb("m_work", [TILE, TILES, E1])
        m_pick = lb("m_pick", [TILE, TILES, E1])
        m_rest = lb("m_rest", [TILE, TILES, E1])
        m_p = lb("m_p", [TILE, TILES, E1])
        m_one = lb("m_one", [TILE, TILES])
        m_two = lb("m_two", [TILE, TILES])
        siluT = lb("siluT", [128, 2, B, TOK])
        hidT = lb("hidT", [128, MLPC, B, TOK])
        layer_tensors = ExitStack()

        def rb(name, shape, dt=F32):
            return layer_tensors.enter_context(nc.sbuf_tensor(name, shape, dt))

        R = rb("R", [TILE, TILES, D])
        ident_r = rb("ident_r", [TILE, TILE], F32R)
        pT = rb("pT", [128, 2, TOK])
        qk_parts = rb("qk_parts", [HALF, 2, 4, TOK], F32R)
        qk_stack = rb("qk_stack", [128, B, HEADS, 2, TOK], F32R)
        minus_max = rb("minus_max", [TILE, NT, HEADS], F32R)
        shift_rows = rb("shift_rows", [HEADS // 2, 2, TOK], F32R)
        probs = rb("probs", [128, 4, 2, TOK])
        v_ext = rb("v_ext", [128, TILES, HEADS, 32])
        oT = rb("oT", [128, 2, TOK])
        o_rec = rb("o_rec", [TILE, NT, 4])
        o_tmp = rb("o_tmp", [TILE, NT, 4, DH])

        layer_tensors.close()

        a_in = sem("a_in")
        a_q_done = sem("a_q_done")
        a_kv_done = sem("a_kv_done")
        a_qT_ready = sem("a_qT_ready")
        a_kv_ready = sem("a_kv_ready")
        a_kabs_ready = sem("a_kabs_ready")
        a_ctx_done = sem("a_ctx_done")
        a_ctx_ready = sem("a_ctx_ready")
        a_att_done = sem("a_att_done")
        a_att_ready = sem("a_att_ready")
        a_proj_done = sem("a_proj_done")
        h_attn = sem("h_attn")

        def attn_sync(sp):
            sp.dma_start(a_w[:, 0, :], a["a_w"][0:128]).then_inc(a_in, 16)
            sp.dma_start(a_w[0:64, 1, :], a["a_w"][128:D]).then_inc(a_in, 16)
            sp.dma_start(a_proj_w[:, 0, :], a["a_proj_w"][0:128]).then_inc(a_in, 16)
            sp.dma_start(a_proj_w[0:64, 1, :], a["a_proj_w"][128:D]).then_inc(a_in, 16)
            sp.dma_start(a_row[:, :], a["a_row"].to_broadcast([TILE, D])).then_inc(a_in, 16)

        def two_chunks(out_ap, lhs, rhs):
            for c in range(2):
                last = nc.tensor.matmul(out_ap, lhs(c), rhs(c), start=(c == 0), stop=(c == 1))
            return last

        def attn_tensor(pe):
            turn(pe, xn, full, 2, normed, NORM_A * TILES)
            pe.wait_ge(a_in, 80)
            pe.wait_ge(xT_ready, turn_base(TURN_A, 1))
            for m in range(2):
                for b in range(B):
                    last = two_chunks(bank[0:CH[m], 2 * m + b, 0:TOK],
                                      lambda c: a_w[:, c, m * 128:m * 128 + CH[m]],
                                      lambda c: xT[:, c, b, :])
                last.then_inc(a_q_done, 1)
            for i in range(TILES):
                b, j = divmod(i, NT)
                if i >= 4:
                    pe.wait_ge(a_kv_ready, i - 3)
                two_chunks(bank[0:TILE, 4 + i % 4, 0:2 * D], lambda c: xT[:, c, b, j * TILE:(j + 1) * TILE],
                           lambda c: a_w[:, c, D:3 * D]).then_inc(a_kv_done, 1)
            for b in range(B):
                for m in range(2):
                    n = CH[m]
                    if b == 0:
                        pe.wait_ge(a_qT_ready, m + 1)
                    else:
                        pe.wait_ge(a_ctx_ready, m + 1)
                    pe.wait_ge(a_kabs_ready, (b + 1) * NT)
                    for j in range(NT):
                        i = b * NT + j
                        nc.tensor.matmul(bank[0:n, m, 0:n], a_kv[:, i, m * 128:m * 128 + n],
                                         a_kv[:, i, D + m * 128:D + m * 128 + n], start=(j == 0), stop=(j == NT - 1))
                    for j in range(NT):
                        last = nc.tensor.matmul(bank[0:n, m, 256:257], a_kabs[:, b * NT + j, m * 128:m * 128 + n],
                                                ones[0:TILE, 0:1], start=(j == 0), stop=(j == NT - 1))
                    last.then_inc(a_ctx_done, 1)
            for b in range(B):
                for m in range(2):
                    n = CH[m]
                    if b == 0 and m == 0:
                        pe.wait_ge(a_kv_ready, TILES)
                    pe.wait_ge(a_ctx_ready, b * 2 + m + 1)
                    nc.tensor.matmul(bank[0:n, 4 + b * 2 + m, 0:TOK], a_ctx[0:n, b, m, 0:n], a_qT[0:n, m, b, :],
                                     start=True, stop=True).then_inc(a_att_done, 1)
            for i in range(TILES):
                b, j = divmod(i, NT)
                pe.wait_ge(a_att_ready, 2 * (b + 1))
                if i >= 4:
                    pe.wait_ge(h_attn, i - 3)
                two_chunks(bank[0:TILE, i % 4, 0:D], lambda c: a_attT[0:CH[c], c, b, j * TILE:(j + 1) * TILE],
                           lambda c: a_proj_w[0:CH[c], c, :]).then_inc(a_proj_done, 1)

        def attn_scalar(act):
            for m in range(2):
                act.wait_ge(a_q_done, m + 1)
                nc.scalar.activation(a_qT[0:CH[m], m, :, :], bank[0:CH[m], 2 * m:2 * m + 2, 0:TOK],
                                     ACT.Copy).then_inc(a_qT_ready, 1)
            for i in range(TILES):
                act.wait_ge(a_kv_done, i + 1)
                nc.scalar.activation(a_kv[:, i, :], bank[0:TILE, 4 + i % 4, 0:2 * D], ACT.Copy).then_inc(a_kv_ready, 1)
            for b in range(B):
                for m in range(2):
                    act.wait_ge(a_att_done, b * 2 + m + 1)
                    nc.scalar.activation(a_attT[0:CH[m], m, b, :], bank[0:CH[m], 4 + b * 2 + m, 0:TOK],
                                         ACT.Copy).then_inc(a_att_ready, 1)

        def attn_vector(dve):
            def step(ins):
                linked(dve, ins)
            dve.wait_ge(txt_in, 16 * B)
            dve.wait_ge(h_tok, TILES)
            norm_stats(dve, step, lambda i: H[:, i, :], full, NORM_A)
            norm_apply(dve, lambda i: H[:, i, :], lambda i: xn[:, i, :], full, NORM_A)
            turned_out(dve, TOK, 2, turn_base(TURN_A, 0))
            dve.wait_ge(a_in, 80)
            step(nc.vector.tensor_tensor(H[:, :, :], H[:, :, :], a_row[:, :].unsqueeze(1).to_broadcast([TILE, TILES, D]), ALU.add))
            for i in range(TILES):
                dve.wait_ge(a_kv_ready, i + 1)
                nc.vector.scalar_tensor_tensor(a_kabs[:, i, :], a_kv[:, i, 0:D], -1.0, a_kv[:, i, 0:D],
                                               ALU.mult, ALU.max).then_inc(a_kabs_ready, 1)
            for m in range(2):
                n = CH[m]
                dve.wait_ge(a_qT_ready, m + 1)
                nc.vector.tensor_reduce(a_qsum[0:n, m, :], a_qT[0:n, m, :, :], AX.X, ALU.add, apply_absolute_value=True)
            for b in range(B):
                for m in range(2):
                    n = CH[m]
                    dve.wait_ge(a_ctx_done, b * 2 + m + 1)
                    step(nc.vector.tensor_scalar(a_ksum[0:n, b, m:m + 1], bank[0:n, m, 256:257], 1e-12, None, ALU.max))
                    step(nc.vector.tensor_scalar(a_qsum[0:n, m, b:b + 1], a_qsum[0:n, m, b:b + 1], 1e-12, None, ALU.max))
                    step(nc.vector.reciprocal(a_ksum[0:n, b, m:m + 1], a_ksum[0:n, b, m:m + 1]))
                    step(nc.vector.reciprocal(a_qsum[0:n, m, b:b + 1], a_qsum[0:n, m, b:b + 1]))
                    step(nc.vector.tensor_tensor(a_rec[0:n, b, m:m + 1], a_ksum[0:n, b, m:m + 1],
                                                 a_qsum[0:n, m, b:b + 1], ALU.mult))
                    nc.vector.scalar_tensor_tensor(a_ctx[0:n, b, m, 0:n], bank[0:n, m, 0:n], a_rec[0:n, b, m:m + 1],
                                                   head16[0:n, 0:n], ALU.mult, ALU.mult).then_inc(a_ctx_ready, 1)
            for i in range(TILES):
                dve.wait_ge(a_proj_done, i + 1)
                nc.vector.tensor_tensor(H[:, i, :], H[:, i, :], bank[0:TILE, i % 4, 0:D], ALU.add).then_inc(h_attn, 1)
            dve.wait_ge(h_attn, TILES)

        router_in = sem("router_in")
        gate_up_in = sem("gate_up_in")
        down_in = sem("down_in")
        router_done = sem("router_done")
        exp8_in = sem("exp8_in")
        exp8_done = sem("exp8_done")
        gate_done = sem("gate_done")
        up_done = sem("up_done")
        silu_done = sem("silu_done")
        mid_ready = sem("mid_ready")
        down_done = sem("down_done")
        m_added = sem("m_added")

        def load_gate_up(sp, e):
            sp.dma_start(gate_up_w[:, 0, :], a["gate_up_a"][e]).then_inc(gate_up_in, 16)
            sp.dma_start(gate_up_w[0:64, 1, :], a["gate_up_b"][e]).then_inc(gate_up_in, 16)

        def dyn(t, e):
            return t[bass.ds(e, 1)].squeeze(0)

        def mix_sync(sp):
            sp.dma_start(router_w[:, 0, :], a["router"][0:128]).then_inc(router_in, 16)
            sp.dma_start(router_w[0:64, 1, :], a["router"][128:D]).then_inc(router_in, 16)
            load_gate_up(sp, 0)
            sp.dma_start(down_w[:, :, :], a["down"][0]).then_inc(down_in, 16)

        def mix_sync_loop(sp):
            with sp.Fori(0, E1 - 1) as e:
                sp.wait_ge(up_done, e * F1C + F1C)
                sp.dma_start(gate_up_w[:, 0, :], a["gate_up_a"][bass.ds(e + 1, 1)].rearrange("e p n -> (e p) n")).then_inc(gate_up_in, 16)
                sp.dma_start(gate_up_w[0:64, 1, :], a["gate_up_b"][bass.ds(e + 1, 1)].rearrange("e p n -> (e p) n")).then_inc(gate_up_in, 16)
                sp.wait_ge(down_done, e * TILES + TILES)
                sp.dma_start(down_w[:, :, :], a["down"][bass.ds(e + 1, 1)].rearrange("e p c n -> (e p) c n")).then_inc(down_in, 16)

        def mix_tensor(pe):
            turn(pe, xn, full, 2, normed, (NORM_M + 1) * TILES)
            pe.wait_ge(router_in, 32)
            pe.wait_ge(xT_ready, turn_base(TURN_A, 2))
            for i in range(TILES):
                b, j = divmod(i, NT)
                last = two_chunks(bank[0:TILE, 6, i * E1:(i + 1) * E1], lambda c: xT[:, c, b, j * TILE:(j + 1) * TILE],
                                  lambda c: router_w[:, c, :])
            last.then_inc(router_done, 1)
            with pe.Fori(0, E1) as e:
                pe.wait_ge(gate_up_in, e * 32 + 32)
                for m in range(F1C):
                    for up, signal in ((0, gate_done), (1, up_done)):
                        u = 2 * m + up
                        if u == 3 or u == 5:
                            pe.wait_ge(silu_done, e * F1C + (u - 3) // 2 + 1)
                        if u == 4:
                            pe.wait_ge(mid_ready, e * F1C + 1)
                        for b in range(B):
                            last = two_chunks(bank[:, 2 * (u % 3) + b, 0:TOK],
                                              lambda c: gate_up_w[:, c, up * F1 + m * 128:up * F1 + (m + 1) * 128],
                                              lambda c: xT[:, c, b, :])
                        last.then_inc(signal, 1)
                pe.wait_ge(down_in, e * 16 + 16)
                pe.wait_ge(mid_ready, e * F1C + F1C)
                for i in range(TILES):
                    b, j = divmod(i, NT)
                    if i >= 2:
                        pe.wait_ge(m_added, e * TILES + i - 1)
                    for c in range(F1C):
                        last = nc.tensor.matmul(bank[0:TILE, 6 + i % 2, 0:D], hidT[:, c, b, j * TILE:(j + 1) * TILE],
                                                down_w[:, c, :], start=(c == 0), stop=(c == F1C - 1))
                    last.then_inc(down_done, 1)

        def mix_scalar(act):
            act.wait_ge(exp8_in, 1)
            nc.scalar.activation(m_work[:, :, :], m_work[:, :, :], ACT.Exp).then_inc(exp8_done, 1)
            with act.Fori(0, E1) as e:
                for m in range(F1C):
                    act.wait_ge(gate_done, e * F1C + m + 1)
                    if m >= 2:
                        act.wait_ge(mid_ready, e * F1C + m - 1)
                    nc.scalar.activation(siluT[:, m % 2, :, :], bank[:, 2 * (2 * m % 3):2 * (2 * m % 3) + 2, 0:TOK],
                                         ACT.Silu).then_inc(silu_done, 1)

        def mix_pool(pool):
            norm_rstd(pool, NORM_M, eps5, NORM_M)
            norm_rstd(pool, NORM_M + 1, eps6, NORM_M + 1)

        def softmax8(dve, step, logits, mixture, shape):
            step(nc.vector.tensor_reduce(m_one[:, :], logits, AX.X, ALU.max))
            nc.vector.tensor_tensor(m_work[:, :, :], logits, m_one[:, :].unsqueeze(2).to_broadcast(shape),
                                    ALU.subtract).then_inc(exp8_in, 1)
            dve.wait_ge(exp8_done, mixture)
            step(nc.vector.tensor_reduce(m_one[:, :], m_work[:, :, :], AX.X, ALU.add))
            step(nc.vector.reciprocal(m_two[:, :], m_one[:, :]))
            step(nc.vector.tensor_tensor(m_p[:, :, :], m_work[:, :, :], m_two[:, :].unsqueeze(2).to_broadcast(shape), ALU.mult))

        def mix_vector(dve):
            def step(ins):
                linked(dve, ins)
            shape = [TILE, TILES, E1]
            norm_stats(dve, step, lambda i: H[:, i, :], full, NORM_M)
            norm_apply(dve, lambda i: H[:, i, :], lambda i: m_in[:, i, :], full, NORM_M)
            dve.wait_ge(normed, (NORM_M + 1) * TILES)
            norm_stats(dve, step, lambda i: m_in[:, i, :], full, NORM_M + 1, rms=True)
            norm_apply(dve, lambda i: m_in[:, i, :], lambda i: xn[:, i, :], full, NORM_M + 1)
            turned_out(dve, TOK, 2, turn_base(TURN_A, 1), lambda c: cols[0:CH[c], C_NORMW + c:C_NORMW + c + 1])
            step(nc.vector.tensor_tensor(H[:, :, :], H[:, :, :], m_in[:, :, :], ALU.add))
            dve.wait_ge(router_done, 1)
            softmax8(dve, step, bank[0:TILE, 6, 0:TILES * E1].rearrange("p (i e) -> p i e", e=E1), 1,
                     shape)
            rank = rank8[:, :, :].to_broadcast(shape)

            def best(src, dst):
                step(nc.vector.tensor_reduce(m_one[:, :], src[:, :, :], AX.X, ALU.max))
                step(nc.vector.tensor_tensor(m_work[:, :, :], src[:, :, :], m_one[:, :].unsqueeze(2).to_broadcast(shape),
                                             ALU.is_equal))
                step(nc.vector.tensor_tensor(m_work[:, :, :], m_work[:, :, :], rank, ALU.mult))
                step(nc.vector.tensor_reduce(m_one[:, :], m_work[:, :, :], AX.X, ALU.max))
                step(nc.vector.tensor_tensor(dst[:, :, :], m_work[:, :, :], m_one[:, :].unsqueeze(2).to_broadcast(shape),
                                             ALU.is_equal))
            best(m_p, m_pick)
            step(nc.vector.scalar_tensor_tensor(m_rest[:, :, :], m_pick[:, :, :], -2.0, m_p[:, :, :], ALU.mult, ALU.add))
            best(m_rest, m_rest)
            step(nc.vector.tensor_tensor(m_pick[:, :, :], m_pick[:, :, :], m_rest[:, :, :], ALU.add))
            step(nc.vector.tensor_tensor(m_prob[:, :, :].rearrange("p e i -> p i e"), m_p[:, :, :], m_pick[:, :, :], ALU.mult))
            with dve.Fori(0, E1) as e:
                for m in range(F1C):
                    dve.wait_ge(silu_done, e * F1C + m + 1)
                    dve.wait_ge(up_done, e * F1C + m + 1)
                    s = 2 * ((2 * m + 1) % 3)
                    nc.vector.tensor_tensor(hidT[:, m, :, :], siluT[:, m % 2, :, :], bank[:, s:s + 2, 0:TOK],
                                            ALU.mult).then_inc(mid_ready, 1)
                for i in range(TILES):
                    dve.wait_ge(down_done, e * TILES + i + 1)
                    nc.vector.scalar_tensor_tensor(H[:, i, :], bank[0:TILE, 6 + i % 2, 0:D],
                                                   m_prob[:, bass.ds(e, 1), i:i + 1].rearrange("p e i -> p (e i)"), H[:, i, :],
                                                   ALU.mult, ALU.add).then_inc(m_added, 1)
            dve.wait_ge(m_added, E1 * TILES)

        def pair(name):
            return [sem(f"{name}{b}") for b in range(B)]

        l_qkv_in = sem("l_qkv_in")
        l_pvec_in = sem("l_pvec_in")
        l_mvec_in = sem("l_mvec_in")
        w1_in = sem("w1_in")
        w2_in = sem("w2_in")
        presets = sem("presets")
        layer_link = sem("layer_link")
        l_var = pair("l_var")
        l_eps = pair("l_eps")
        l_rstd = pair("l_rstd")
        l_normed = pair("l_normed")
        l_turned = pair("l_turned")
        pT_ready = pair("pT_ready")
        xT_up = pair("xT_up")
        qk_done = pair("qk_done")
        hi_ready = pair("hi_ready")
        lo_ready = pair("lo_ready")
        q_cleared = pair("q_cleared")
        stacked = pair("stacked")
        v_done = pair("v_done")
        v_ready = pair("v_ready")
        row_scores = pair("row_scores")
        row_taken = pair("row_taken")
        shift_turned = pair("shift_turned")
        shift_copied = pair("shift_copied")
        shift_in = [[sem(f"shift_in{b}{c}") for c in range(2)] for b in range(B)]
        scores_done = pair("scores_done")
        probs_ready = pair("probs_ready")
        pv_done = pair("pv_done")
        o_copied = pair("o_copied")
        o_turned = pair("o_turned")
        o_added = pair("o_added")
        up_done1 = pair("up_done1")
        gelu_ready = pair("gelu_ready")
        down_done1 = pair("down_done1")
        r_biased = pair("r_biased")
        r_ready = pair("r_ready")
        h_layers = sem("h_layers")

        ROWS = NT * GROUPS
        QK_UNITS = 4
        PARTS = 3
        STEPS = QUADS * NT
        UNITS = 2 * STEPS
        MERGE_AT, APPLY_AT, UP_AT, FIRST_SHIFT, DOWN_AT = 0, 2, 4, 10, (14, 17)
        QUERY_AT = 1
        SIDE = 6

        class Steps:

            def norm(self, b, n, second): pass
            def apply(self, b, n, second): pass
            def turn(self, b, n, second): pass
            def query(self, b, n, u): pass
            def split(self, b, n, u): pass
            def stack(self, b, n, c): pass
            def values(self, b, n, j): pass
            def row(self, b, n, u): pass
            def shift(self, b, n, c): pass
            def scores(self, b, n, k): pass
            def exps(self, b, n, k): pass
            def weigh(self, b, n, k): pass
            def collect(self, b, n, o): pass
            def turn_back(self, b, n, o): pass
            def merge(self, b, n, o): pass
            def up(self, b, n, m): pass
            def down(self, b, n, j): pass
            def load_project(self, n): pass
            def load_mlp(self, n): pass

        def project(s, b, n):
            s.norm(b, n, 0)
            s.apply(b, n, 0)
            s.turn(b, n, 0)
            for u in range(QK_UNITS):
                s.query(b, n, u)
                s.split(b, n, u)
            for c in range(2):
                s.stack(b, n, c)
            for j in range(NT):
                s.values(b, n, j)

        def mlp(s, b, n):
            s.turn_back(b, n, QUADS - 1)
            s.merge(b, n, QUADS - 1)
            s.norm(b, n, 1)
            s.apply(b, n, 1)
            s.turn(b, n, 1)
            for m in range(MLPC):
                s.up(b, n, m)
            for j in range(NT):
                s.down(b, n, j)

        def half(s, b, n, mlp_of, project_of):
            o = 1 - b
            for u in range(ROWS):
                s.row(b, n, u)
                if u == FIRST_SHIFT:
                    s.shift(b, n, 0)
                if mlp_of is not None:
                    if u == MERGE_AT:
                        s.turn_back(o, mlp_of, QUADS - 1)
                    if u == MERGE_AT + 1:
                        s.merge(o, mlp_of, QUADS - 1)
                        s.norm(o, mlp_of, 1)
                    if u == APPLY_AT:
                        s.apply(o, mlp_of, 1)
                    if u == APPLY_AT + 1:
                        s.turn(o, mlp_of, 1)
                    if UP_AT <= u < UP_AT + MLPC:
                        s.up(o, mlp_of, u - UP_AT)
                    if u in DOWN_AT:
                        s.down(o, mlp_of, DOWN_AT.index(u))
            s.shift(b, n, 1)
            if mlp_of is not None:
                for j in range(len(DOWN_AT), NT):
                    s.down(o, mlp_of, j)
            if project_of is not None:
                s.norm(o, project_of, 0)
            s.scores(b, n, 0)
            for k in range(STEPS):
                if k + 1 < STEPS:
                    s.scores(b, n, k + 1)
                s.exps(b, n, k)
                if k >= NT and k % NT == 0:
                    s.turn_back(b, n, k // NT - 1)
                if project_of is not None:
                    if k == 0:
                        s.apply(o, project_of, 0)
                    u = k - QUERY_AT
                    if 1 <= u <= QK_UNITS:
                        s.split(o, project_of, u - 1)
                        if u % 2 == 0:
                            s.stack(o, project_of, u // 2 - 1)
                    if 0 <= u < QK_UNITS:
                        s.query(o, project_of, u)
                    if 0 <= u - QK_UNITS < NT:
                        s.values(o, project_of, u - QK_UNITS)
                s.weigh(b, n, k)
                if project_of is not None and k == QUERY_AT - 1:
                    s.turn(o, project_of, 0)
                if k >= NT and k % NT == 0:
                    s.merge(b, n, k // NT - 1)
                if k % NT == NT - 1:
                    s.collect(b, n, k // NT)

        def begin(s):
            project(s, 0, 0)
            half(s, 0, 0, None, 0)

        def body(s, n):
            s.load_project(n)
            half(s, 1, n, n, n + 1)
            half(s, 0, n + 1, n, n + 1)
            s.load_mlp(n)

        def end(s):
            half(s, 1, LAYERS - 1, LAYERS - 1, None)
            mlp(s, 1, LAYERS - 1)

        def one(name, n):
            t = a[name][bass.ds(n, 1)] if not isinstance(n, int) else a[name][n:n + 1]
            return t.rearrange("e p n -> (e p) n")

        def load_w1(sp, n):
            sp.dma_start(w1[:, 0, :], one("w1_a", n)).then_inc(w1_in, 16)
            sp.dma_start(w1[0:64, 1, :], one("w1_b", n)).then_inc(w1_in, 16)

        def load_w2(sp, n):
            sp.dma_start(w2[:, :, :].rearrange("p c n -> p (c n)"), one("w2", n)).then_inc(w2_in, 16)

        def load_qkv(sp, n):
            sp.dma_start(l_qkv_w[0:HALF, :, :].rearrange("p c n -> p (c n)"), one("qkv", n)).then_inc(l_qkv_in, 16)

        def load_project_vectors(sp, n):
            sp.dma_start(p_cols[:, :], one("p_cols", n)).then_inc(l_pvec_in, 16)
            sp.dma_start(p_row[:, :], one("p_row", n).to_broadcast([TILE, D])).then_inc(l_pvec_in, 16)

        def load_mlp_vectors(sp, n):
            sp.dma_start(m_cols[:, :], one("m_cols", n)).then_inc(l_mvec_in, 16)
            sp.dma_start(m_row[:, :], one("m_row", n).to_broadcast([TILE, D])).then_inc(l_mvec_in, 16)

        def layers_sync(sp):
            load_qkv(sp, 0)
            load_project_vectors(sp, 0)
            load_mlp_vectors(sp, 0)
            load_w1(sp, 0)
            load_w2(sp, 0)

        def layers_sync_loop(sp):
            class Sync(Steps):
                def stack(self, b, n, c):
                    if c == 0:
                        sp.wait_ge(q_cleared[b], n + 1)
                    sp.wait_ge(lo_ready[b], n * QK_UNITS + 2 * c + 2)
                    picks = (slice(0, 3, 2), slice(0, 4, 3), slice(1, 3))
                    for part, pick in enumerate(picks):
                        heads = slice(c * HEADS // 2, (c + 1) * HEADS // 2)
                        sp.dma_start(qk_stack[DH * part:DH * (part + 1), b, heads, :, :].bitcast(F32),
                                     qk_parts[:, c, pick, :].bitcast(F32)).then_inc(stacked[b], 16)

                def shift(self, b, n, c):
                    sp.wait_ge(shift_copied[b], 2 * n + c + 1)
                    sp.dma_start(qk_stack[SHIFT_ROW:SHIFT_ROW + 1, b, c * HEADS // 2:(c + 1) * HEADS // 2, 0, :].bitcast(F32),
                                 shift_rows[:, c, :].bitcast(F32)).then_inc(shift_in[b][c], 16)

                def load_project(self, n):
                    sp.wait_ge(v_done[1], n * NT + NT)
                    load_qkv(sp, n + 1)
                    sp.wait_ge(v_ready[1], n * NT + NT)
                    load_project_vectors(sp, n + 1)

                def load_mlp(self, n):
                    sp.wait_ge(up_done1[1], n * MLPC + MLPC)
                    load_w1(sp, n + 1)
                    sp.wait_ge(gelu_ready[1], n * MLPC + MLPC)
                    sp.wait_ge(r_biased[1], n + 1)
                    load_mlp_vectors(sp, n + 1)
                    sp.wait_ge(down_done1[1], n * NT + NT)
                    load_w2(sp, n + 1)

            s = Sync()
            begin(s)
            with sp.Fori(0, LAYERS - 1) as n:
                body(s, n)
            end(s)
            n = LAYERS - 1
            sp.wait_ge(up_done1[1], n * MLPC + MLPC)
            load_w1(sp, n + 1)
            sp.wait_ge(down_done1[1], n * NT + NT)
            load_w2(sp, n + 1)
            with sp.Fori(0, E2 - 1) as e:
                sp.wait_ge(up2_done, e * MLPC + MLPC)
                load_w1(sp, e + LAYERS + 1)
                sp.wait_ge(down2_done, e * TILES + TILES)
                load_w2(sp, e + LAYERS + 1)

        def layers_tensor(pe):
            class Tensor(Steps):
                def turn(self, b, n, second):
                    pe.wait_ge(l_normed[b], 2 * n + second + 1)
                    chunks = CH if second else (HALF, HALF)
                    for c in range(2):
                        for j in range(NT):
                            last = nc.tensor.transpose(bank[0:chunks[c], SIDE + c, j * TILE:(j + 1) * TILE],
                                                       xn[:, b * NT + j, c * chunks[0]:c * chunks[0] + chunks[c]],
                                                       ident[0:TILE, 0:TILE])
                        last.then_inc(l_turned[b], 1)

                def query(self, b, n, u):
                    c, which = divmod(u, 2)
                    if u == 0:
                        pe.wait_ge(l_qkv_in, n * 16 + 16)
                        pe.wait_ge(pT_ready[b], 2 * n + 2)
                    if u >= 2:
                        pe.wait_ge(lo_ready[b], n * QK_UNITS + u - 1)
                    nc.tensor.matmul(bank[0:HALF, SIDE + which, 0:TOK], l_qkv_w[:, c, which * HALF:(which + 1) * HALF],
                                     pT[:, c, :], start=True, stop=True).then_inc(qk_done[b], 1)

                def values(self, b, n, j):
                    if j < 2:
                        pe.wait_ge(lo_ready[b], n * QK_UNITS + QK_UNITS - 1 + j)
                    else:
                        pe.wait_ge(v_ready[b], n * NT + j - 1)
                    for c in range(2):
                        last = nc.tensor.matmul(bank[0:TILE, SIDE + j % 2, c * HALF:(c + 1) * HALF],
                                                pT[:, c, j * TILE:(j + 1) * TILE], l_qkv_w[:, c, 2 * HALF:3 * HALF],
                                                start=True, stop=True)
                    last.then_inc(v_done[b], 1)

                def row(self, b, n, u):
                    g, j = divmod(u, NT)
                    if u == 0:
                        pe.wait_ge(stacked[b], (n + 1) * 2 * PARTS * 16)
                    if u >= 2:
                        pe.wait_ge(row_taken[b], n * ROWS + u - 1)
                    for r in range(2):
                        last = nc.tensor.matmul(bank[0:TILE, 2 * (u % 2) + r, 0:TOK],
                                                qk_stack[:, b, 2 * g + r, 0, j * TILE:(j + 1) * TILE],
                                                qk_stack[:, b, 2 * g + r, 1, :],
                                                start=True, stop=True)
                    last.then_inc(row_scores[b], 1)

                def shift(self, b, n, c):
                    pe.wait_ge(row_taken[b], n * ROWS + (c + 1) * ROWS // 2)
                    if c == 1:
                        pe.wait_ge(shift_copied[b], 2 * n + 1)
                    for j in range(NT):
                        last = nc.tensor.matmul(bank[0:HEADS // 2, 5, j * TILE:(j + 1) * TILE], minus_max[:, j, c * HEADS // 2:(c + 1) * HEADS // 2],
                                                ident_r[:, :], start=True, stop=True)
                    last.then_inc(shift_turned[b], 1)

                def scores(self, b, n, k):
                    quad, t = divmod(k, NT)
                    for h in range(2):
                        u, g = 2 * k + h, 2 * quad + h
                        if k == 0 and h == 0:
                            pe.wait_ge(shift_in[b][0], n * 16 + 16)
                            pe.wait_ge(row_taken[b], n * ROWS + ROWS)
                        if k == NT and h == 0:
                            pe.wait_ge(shift_in[b][1], n * 16 + 16)
                        if u >= 2:
                            pe.wait_ge(probs_ready[b], n * UNITS + u - 1)
                        for r in range(2):
                            last = nc.tensor.matmul(bank[0:TILE, 2 * (u % 2) + r, 0:TOK],
                                                    qk_stack[:, b, 2 * g + r, 1, t * TILE:(t + 1) * TILE],
                                                    qk_stack[:, b, 2 * g + r, 0, :],
                                                    start=True, stop=True)
                        last.then_inc(scores_done[b], 1)

                def weigh(self, b, n, k):
                    quad, t = divmod(k, NT)
                    if t == 0 and quad >= 2:
                        pe.wait_ge(o_added[b], n * QUADS + quad - 1)
                    pe.wait_ge(probs_ready[b], n * UNITS + 2 * k + 2)
                    if k == 0:
                        pe.wait_ge(v_ready[b], n * NT + NT)
                    for r in range(4):
                        last = nc.tensor.matmul(bank[32 * r:32 * r + 32, 4 + quad % 2, 0:TOK], v_ext[:, b * NT + t, 4 * quad + r, :],
                                                probs[:, (2 * k + r // 2) % 4, r % 2, :], start=(t == 0), stop=(t == NT - 1))
                    last.then_inc(pv_done[b], 1)

                def turn_back(self, b, n, o):
                    pe.wait_ge(o_copied[b], n * QUADS + o + 1)
                    for j in range(NT):
                        last = nc.tensor.transpose(bank[0:TILE, 4 + o % 2, j * 128:(j + 1) * 128],
                                                   oT[:, o % 2, j * TILE:(j + 1) * TILE], ident[:, :])
                    last.then_inc(o_turned[b], 1)

                def up(self, b, n, m):
                    if m == 0:
                        pe.wait_ge(w1_in, n * 32 + 32)
                        pe.wait_ge(xT_up[b], 2 * n + 2)
                    if m >= 2:
                        pe.wait_ge(gelu_ready[b], n * MLPC + m - 1)
                    two_chunks(bank[:, SIDE + m % 2, 0:TOK], lambda c: w1[:, c, m * 128:(m + 1) * 128],
                               lambda c: xT[:, c, b, :]).then_inc(up_done1[b], 1)

                def down(self, b, n, j):
                    if j == 0:
                        pe.wait_ge(w2_in, n * 16 + 16)
                        pe.wait_ge(gelu_ready[b], n * MLPC + MLPC)
                    if j == 2:
                        pe.wait_ge(r_ready[b], n * NT + 1)
                    for c in range(MLPC):
                        last = nc.tensor.matmul(bank[0:TILE, SIDE + j % 2, 0:D], hidT[:, c, 0, j * TILE:(j + 1) * TILE], w2[:, c, :],
                                                start=(c == 0), stop=(c == MLPC - 1))
                    last.then_inc(down_done1[b], 1)

            s = Tensor()
            pe.wait_ge(presets, 4)
            begin(s)
            with pe.Fori(0, LAYERS - 1) as n:
                body(s, n)
            end(s)

        def layers_scalar(act):
            class Scalar(Steps):
                def turn(self, b, n, second):
                    if second:
                        act.wait_ge(l_mvec_in, n * 32 + 32)
                        for c in range(2):
                            r = CH[c]
                            act.wait_ge(l_turned[b], 4 * n + 2 + c + 1)
                            nc.scalar.activation(xT[0:r, c, b, :], bank[0:r, SIDE + c, 0:TOK], ACT.Identity,
                                                 scale=m_cols[0:r, c:c + 1], bias=m_cols[0:r, 2 + c:3 + c]).then_inc(xT_up[b], 1)

                def split(self, b, n, u):
                    c, which = divmod(u, 2)
                    act.wait_ge(qk_done[b], n * QK_UNITS + u + 1)
                    nc.scalar.activation(qk_parts[:, c, 2 * which, :], bank[0:HALF, SIDE + which, 0:TOK], ACT.Identity,
                                         bias=p_cols[0:HALF, P_BQ + u:P_BQ + u + 1]).then_inc(hi_ready[b], 1)

                def shift(self, b, n, c):
                    act.wait_ge(shift_turned[b], 2 * n + c + 1)
                    nc.scalar.activation(shift_rows[:, c, :], bank[0:HEADS // 2, 5, 0:TOK], ACT.Copy).then_inc(shift_copied[b], 1)

                def exps(self, b, n, k):
                    for u in (2 * k, 2 * k + 1):
                        act.wait_ge(scores_done[b], n * UNITS + u + 1)
                        if u >= 4:
                            act.wait_ge(pv_done[b], n * STEPS + (u - 4) // 2 + 1)
                        nc.scalar.activation(probs[0:TILE, u % 4, :, :], bank[0:TILE, 2 * (u % 2):2 * (u % 2) + 2, 0:TOK], ACT.Exp,
                                             scale=float(DH) ** -0.5).then_inc(probs_ready[b], 1)

                def up(self, b, n, m):
                    if m == 0:
                        act.wait_ge(l_mvec_in, n * 32 + 32)
                    act.wait_ge(up_done1[b], n * MLPC + m + 1)
                    nc.scalar.activation(hidT[:, m, 0, :], bank[:, SIDE + m % 2, 0:TOK], ACT.Gelu,
                                         bias=m_cols[:, M_B1 + m:M_B1 + m + 1]).then_inc(gelu_ready[b], 1)

            s = Scalar()
            begin(s)
            with act.Fori(0, LAYERS - 1) as n:
                body(s, n)
            end(s)

        def layers_pool(pool):
            class Pool(Steps):
                def norm(self, b, n, second):
                    t = slice(b * NT, (b + 1) * NT)
                    k = 2 * n + second + 1
                    pool.wait_ge(l_var[b], k)
                    nc.gpsimd.tensor_tensor(veps[:, t], mv[:, t, 1], eps5[:, t], ALU.add).then_inc(l_eps[b], 1)
                    pool.wait_ge(l_eps[b], k)
                    nc.gpsimd.tensor_tensor(rstd[:, t], veps[:, t], minus_half[:, t], ALU.pow).then_inc(l_rstd[b], 1)

                def turn(self, b, n, second):
                    if second:
                        pool.wait_ge(l_mvec_in, n * 32 + 32)
                        pool.wait_ge(l_normed[b], 2 * n + 2)
                        t = R[:, b * NT:(b + 1) * NT, :]
                        nc.gpsimd.tensor_tensor(t, t, m_row[:, :].unsqueeze(1).to_broadcast([TILE, NT, D]),
                                                ALU.add).then_inc(r_biased[b], 1)

                def query(self, b, n, u):
                    if u == 0:
                        pool.wait_ge(l_turned[b], 4 * n + 2)
                        nc.gpsimd.tensor_tensor(pool_carrier[:, :], eps5[0:1, 0:1], eps5[0:1, 0:1], ALU.add)
                        nc.gpsimd.memset(qk_stack[32:STACK, b, :, 0, :].bitcast(F32), 0.0).then_inc(q_cleared[b], 1)

            nc.gpsimd.memset(v_ext[:, :, :, DH + 1:32], 0.0)
            nc.gpsimd.memset(v_ext[:, :, :, DH:DH + 1], 1.0)
            nc.gpsimd.memset(qk_stack[:, :, :, 0, :].bitcast(F32), 0.0).then_inc(presets, 1)
            pool.wait_ge(presets, 1)
            nc.gpsimd.memset(qk_stack[32:64, :, :, 1, :].bitcast(F32), 1.0).then_inc(presets, 1)
            pool.wait_ge(presets, 2)
            nc.gpsimd.memset(qk_stack[64:128, :, :, 1, :].bitcast(F32), 0.0).then_inc(presets, 1)
            pool.wait_ge(presets, 3)
            nc.gpsimd.memset(l_qkv_w[HALF:128, :, :], 0.0)
            nc.gpsimd.memset(pT[HALF:128, :, :], 0.0)
            nc.gpsimd.memset(probs[TILE:128, :, :, :], 0.0)
            nc.gpsimd.memset(v_ext[TILE:128, :, :, :], 0.0).then_inc(presets, 1)
            pool.wait_ge(presets, 4)
            norm_rstd(pool, NORM_R, eps5, NORM_R)
            s = Pool()
            begin(s)
            with pool.Fori(0, LAYERS - 1) as n:
                body(s, n)
            end(s)

        def layers_vector(dve):
            class Vector(Steps):
                def norm(self, b, n, second):
                    for i in range(b * NT, (b + 1) * NT):
                        last = nc.vector.bn_stats(stats[:, i, :], R[:, i, :])
                    self.step(last)
                    nc.vector.memset(carrier[:, :], 0.0)
                    for i in range(b * NT, (b + 1) * NT):
                        last = nc.vector.bn_aggr(mv[:, i, :], stats[:, i, :])
                    last.then_inc(l_var[b], 1)

                def apply(self, b, n, second):
                    dve.wait_ge(l_rstd[b], 2 * n + second + 1)
                    for i in range(b * NT, (b + 1) * NT):
                        last = nc.vector.tensor_scalar(xn[:, i, :], R[:, i, :], mv[:, i, 0:1], rstd[:, i:i + 1],
                                                       ALU.subtract, ALU.mult)
                    last.then_inc(l_normed[b], 1)

                def turn(self, b, n, second):
                    if not second:
                        dve.wait_ge(l_pvec_in, n * 32 + 32)
                        for c in range(2):
                            dve.wait_ge(l_turned[b], 4 * n + c + 1)
                            nc.vector.tensor_scalar(pT[0:HALF, c, :], bank[0:HALF, SIDE + c, 0:TOK], p_cols[0:HALF, c:c + 1],
                                                    p_cols[0:HALF, 2 + c:3 + c], ALU.mult, ALU.add).then_inc(pT_ready[b], 1)

                def split(self, b, n, u):
                    c, which = divmod(u, 2)
                    dve.wait_ge(hi_ready[b], n * QK_UNITS + u + 1)
                    hi, lo = 2 * which, 2 * which + 1
                    nc.vector.scalar_tensor_tensor(qk_parts[:, c, lo, :], bank[0:HALF, SIDE + which, 0:TOK],
                                                   p_cols[0:HALF, P_BQ + u:P_BQ + u + 1], qk_parts[:, c, hi, :].bitcast(F32),
                                                   ALU.add, ALU.subtract).then_inc(lo_ready[b], 1)

                def values(self, b, n, j):
                    dve.wait_ge(v_done[b], n * NT + j + 1)
                    nc.vector.tensor_tensor(v_ext[0:TILE, b * NT + j, :, 0:DH],
                                            bank[0:TILE, SIDE + j % 2, 0:D].rearrange("p (h d) -> p h d", d=DH),
                                            p_row[:, :].rearrange("p (h d) -> p h d", d=DH), ALU.add).then_inc(v_ready[b], 1)

                def row(self, b, n, u):
                    g, j = divmod(u, NT)
                    dve.wait_ge(row_scores[b], n * ROWS + u + 1)
                    nc.vector.tensor_reduce(minus_max[:, j, 2 * g:2 * g + 2], bank[0:TILE, 2 * (u % 2):2 * (u % 2) + 2, 0:TOK],
                                            AX.X, ALU.max, negate=True).then_inc(row_taken[b], 1)

                def collect(self, b, n, o):
                    dve.wait_ge(pv_done[b], n * STEPS + (o + 1) * NT)
                    nc.vector.tensor_copy(oT[:, o % 2, :], bank[:, 4 + o % 2, 0:TOK]).then_inc(o_copied[b], 1)

                def merge(self, b, n, o):
                    dve.wait_ge(o_turned[b], n * QUADS + o + 1)
                    src = bank[0:TILE, 4 + o % 2, 0:NT * 128].rearrange("p (j h d) -> p j h d", j=NT, d=32)
                    self.step(nc.vector.reciprocal(o_rec[:, :, :], src[:, :, :, DH]))
                    self.step(nc.vector.tensor_tensor(o_tmp[:, :, :, :], src[:, :, :, 0:DH],
                                                      o_rec[:, :, :].unsqueeze(3).to_broadcast([TILE, NT, 4, DH]), ALU.mult))
                    dst = R[:, b * NT:(b + 1) * NT, o * 64:(o + 1) * 64].rearrange("p j (h d) -> p j h d", d=DH)
                    nc.vector.tensor_tensor(dst, dst, o_tmp[:, :, :, :], ALU.add).then_inc(o_added[b], 1)
                    if o == QUADS - 1:
                        dve.wait_ge(o_added[b], n * QUADS + QUADS)

                def down(self, b, n, j):
                    dve.wait_ge(down_done1[b], n * NT + j + 1)
                    if j == 0:
                        dve.wait_ge(r_biased[b], n + 1)
                    nc.vector.tensor_tensor(R[:, b * NT + j, :], R[:, b * NT + j, :], bank[0:TILE, SIDE + j % 2, 0:D],
                                            ALU.add).then_inc(r_ready[b], 1)
                    if j == NT - 1:
                        dve.wait_ge(r_ready[b], n * NT + NT)

            def step(ins):
                linked(dve, ins)
            s = Vector()
            s.step = step
            nc.vector.tensor_copy(ident_r[:, :], ident[0:TILE, 0:TILE])
            norm_stats(dve, step, lambda i: H[:, i, :], full, NORM_R)
            norm_apply(dve, lambda i: H[:, i, :], lambda i: R[:, i, :], full, NORM_R)
            dve.wait_ge(normed, (NORM_R + 1) * TILES)
            begin(s)
            with dve.Fori(0, LAYERS - 1) as n:
                s.step, counted = loop_linker(dve, layer_link, n * LINKS)
                body(s, n)
            assert counted[0] == LINKS, counted
            s.step = step
            end(s)
            nc.vector.tensor_tensor(H[:, :, :], H[:, :, :], R[:, :, :], ALU.add).then_inc(h_layers, 1)
            dve.wait_ge(h_layers, 1)

        LINKS = 2 * (2 + 2 * QUADS)

        up2_done = sem("up2_done")
        act2_ready = sem("act2_ready")
        down2_done = sem("down2_done")

        def mlp_tensor(pe, e):
            pe.wait_ge(w1_in, (e + LAYERS) * 32 + 32)
            for m in range(MLPC):
                if m == 3:
                    pe.wait_ge(act2_ready, e * MLPC + 1)
                if m >= 4:
                    pe.wait_ge(act2_ready, e * MLPC + m - 3)
                for b in range(B):
                    last = two_chunks(bank[:, 2 * (m % 4) + b, 0:TOK], lambda c: w1[:, c, m * 128:(m + 1) * 128],
                                      lambda c: xT[:, c, b, :])
                last.then_inc(up2_done, 1)
            pe.wait_ge(w2_in, (e + LAYERS) * 16 + 16)
            pe.wait_ge(act2_ready, e * MLPC + MLPC)
            for i in range(TILES):
                b, j = divmod(i, NT)
                for c in range(MLPC):
                    last = nc.tensor.matmul(bank[0:TILE, 2 + i, 0:D], hidT[:, c, b, j * TILE:(j + 1) * TILE], w2[:, c, :],
                                            start=(c == 0), stop=(c == MLPC - 1))
                last.then_inc(down2_done, 1)

        raw = lb("raw", [TILE, E2, TILES, D])
        s_score = lb("s_score", [TILE, E2, TILES])
        s_mark = lb("s_mark", [TILE, E2, TILES])
        s_above = lb("s_above", [TILE, E2, TILES])
        s_rank = lb("s_rank", [TILE, E2, TILES])
        s_zero = lb("s_zero", [TILE, E2 * TILES])
        s_gate = lb("s_gate", [TILE, E2, TILES])
        s_least = lb("s_least", [TILE, 1])
        s_try = lb("s_try", [TILE, 1])
        s_ok = lb("s_ok", [TILE, 1])
        s_count = lb("s_count", [TILE, 1])
        s_total = lb("s_total", [TILE, 1])
        s_gateT = lb("s_gateT", [E2, B, TOK])

        g_in = sem("g_in")
        g_logits = sem("g_logits")
        bits_counted = sem("bits_counted")
        bits_total = sem("bits_total")
        ties_marked = sem("ties_marked")
        ties_ranked = sem("ties_ranked")
        gate_ready = sem("gate_ready")
        gate_turned = sem("gate_turned")
        gateT_ready = sem("gateT_ready")
        bias_done = sem("bias_done")
        raw_ready = sem("raw_ready")
        y_ready = sem("y_ready")
        y_added = sem("y_added")

        BITS = 30
        EARLY = 5

        def mix2_sync(sp):
            sp.dma_start(gate2_w[:, 0, :], a["gate2"][0:128]).then_inc(g_in, 16)
            sp.dma_start(gate2_w[0:64, 1, :], a["gate2"][128:D]).then_inc(g_in, 16)
            sp.dma_start(b2_rows[:, :], a["mix_b2"]).then_inc(g_in, 16)
            sp.dma_start(b1_cols[:, :, :], a["mix_b1"]).then_inc(g_in, 16)

        def mix2_store(sp):
            for b in range(B):
                sp.wait_ge(y_ready, (b + 1) * NT)
                sp.dma_start(out[b].rearrange("(j p) d -> p j d", p=TILE), H[:, b * NT:(b + 1) * NT, :]).then_inc(stored, 16)
            sp.wait_ge(stored, 16 * B)

        def mix2_tensor(pe):
            turn(pe, xn, full, 2, normed, NORM_E * TILES)
            pe.wait_ge(g_in, 64)
            pe.wait_ge(xT_ready, turn_base(TURN_A, 3))
            for i in range(TILES):
                b, j = divmod(i, NT)
                last = two_chunks(bank[0:TILE, 0, i * E2:(i + 1) * E2], lambda c: xT[:, c, b, j * TILE:(j + 1) * TILE],
                                  lambda c: gate2_w[:, c, :])
            last.then_inc(g_logits, 1)
            pe.wait_ge(exp8_in, 2)

            def experts(first, end):
                with pe.Fori(first, end) as e:
                    mlp_tensor(pe, e)
                    pe.wait_ge(raw_ready, e * TILES + 4)
            experts(0, EARLY)
            pe.wait_ge(raw_ready, EARLY * TILES)
            pe.wait_ge(ties_marked, 1)
            mark = s_mark[:, :, :].rearrange("p e i -> p (e i)")
            nc.tensor.matmul(bank[0:TILE, 0, 0:E2 * TILES], lower[0:TILE, :], mark, start=True, stop=True)
            nc.tensor.matmul(bank[0:TILE, 1, 0:E2 * TILES], ones[0:TILE, 0:TILE], mark, start=True, stop=True).then_inc(ties_ranked, 1)
            pe.wait_ge(gate_ready, 1)
            for i in range(TILES):
                last = nc.tensor.transpose(bank[0:E2, 2 + i // NT, (i % NT) * TILE:(i % NT + 1) * TILE], s_gate[:, :, i],
                                           ident[0:TILE, 0:TILE])
            last.then_inc(gate_turned, 1)
            pe.wait_ge(gateT_ready, 1)
            experts(EARLY, E2)
            pe.wait_ge(raw_ready, E2 * TILES)
            for i in range(TILES):
                b, j = divmod(i, NT)
                nc.tensor.matmul(bank[0:TILE, i, 0:D], s_gateT[:, b, j * TILE:(j + 1) * TILE], b2_rows[:, :],
                                 start=True, stop=True).then_inc(bias_done, 1)

        def mix2_scalar(act):
            act.wait_ge(exp8_in, 2)
            nc.scalar.activation(m_work[:, :, :], m_work[:, :, :], ACT.Exp).then_inc(exp8_done, 1)
            act.wait_ge(g_in, 64)
            with act.Fori(0, E2) as e:
                for m in range(MLPC):
                    act.wait_ge(up2_done, e * MLPC + m + 1)
                    nc.scalar.activation(hidT[:, m, :, :], bank[:, 2 * (m % 4):2 * (m % 4) + 2, 0:TOK], ACT.Gelu_apprx_tanh,
                                         bias=b1_cols[:, bass.ds(e, 1), m:m + 1].rearrange("p e m -> p (e m)")).then_inc(act2_ready, 1)
                for i in range(TILES):
                    act.wait_ge(down2_done, e * TILES + i + 1)
                    nc.scalar.activation(raw[:, bass.ds(e, 1), i, :].rearrange("p e d -> p (e d)"), bank[0:TILE, 2 + i, 0:D],
                                         ACT.Copy).then_inc(raw_ready, 1)

        def mix2_pool(pool):
            norm_rstd(pool, NORM_E, eps5, NORM_E)
            for t in range(BITS):
                pool.wait_ge(bits_counted, t + 1)
                nc.gpsimd.partition_all_reduce(s_total[:, :], s_count[:, :], TILE, bass.bass_isa.ReduceOp.add).then_inc(bits_total, 1)
            pool.wait_ge(bits_counted, BITS + 1)
            nc.gpsimd.partition_all_reduce(s_total[:, :], s_count[:, :], TILE, bass.bass_isa.ReduceOp.add).then_inc(bits_total, 1)

        def mix2_vector(dve):
            def step(ins):
                linked(dve, ins)
            shape = [TILE, TILES, E2]
            norm_stats(dve, step, lambda i: H[:, i, :], full, NORM_E)
            norm_apply(dve, lambda i: H[:, i, :], lambda i: xn[:, i, :], full, NORM_E)
            turned_out(dve, TOK, 2, turn_base(TURN_A, 2))
            dve.wait_ge(g_logits, 1)
            softmax8(dve, step, bank[0:TILE, 0, 0:TILES * E2].rearrange("p (i e) -> p i e", e=E2), 2,
                     shape)
            step(nc.vector.tensor_copy(s_score[:, :, :].rearrange("p e i -> p i e"), m_p[:, :, :]))
            nc.vector.memset(s_zero[:, :], 0.0)
            step(nc.vector.memset(s_least[:, :], 0.0))
            score = s_score[:, :, :].rearrange("p e i -> p (e i)")
            markf = s_mark[:, :, :].rearrange("p e i -> p (e i)")
            above = s_above[:, :, :].rearrange("p e i -> p (e i)")
            for t in range(BITS):
                step(nc.vector.tensor_scalar(s_try[:, :].bitcast(I32), s_least[:, :].bitcast(I32), 1 << (BITS - 1 - t), None,
                                             ALU.bitwise_or))
                nc.vector.tensor_scalar(markf, score, s_try[:, 0:1], None, ALU.is_ge, ALU.add,
                                        accum_out=s_count[:, :]).then_inc(bits_counted, 1)
                dve.wait_ge(bits_total, t + 1)
                step(nc.vector.tensor_scalar(s_ok[:, :], s_total[:, :], float(PICKED), s_try[:, 0:1], ALU.is_ge, ALU.mult))
                step(nc.vector.tensor_tensor(s_least[:, :], s_least[:, :], s_ok[:, :], ALU.max))
            nc.vector.tensor_scalar(above, score, s_least[:, 0:1], None, ALU.is_gt, ALU.add,
                                    accum_out=s_count[:, :]).then_inc(bits_counted, 1)
            nc.vector.tensor_scalar(markf, score, s_least[:, 0:1], None, ALU.is_equal).then_inc(ties_marked, 1)
            dve.wait_ge(ties_ranked, 1)
            dve.wait_ge(bits_total, BITS + 1)
            step(nc.vector.tensor_scalar(s_ok[:, :], s_total[:, :], -1.0, float(PICKED), ALU.mult, ALU.add))
            rank = s_rank[:, :, :].rearrange("p e i -> p (e i)")
            step(nc.vector.tensor_copy(s_gate[:, :, :].rearrange("p e i -> p (e i)"), bank[0:TILE, 1, 0:E2 * TILES]))
            gate = s_gate[:, :, :].rearrange("p e i -> p (e i)")
            step(nc.vector.tensor_tensor_scan(rank, gate, s_zero[:, :], 0.0, ALU.add, ALU.add))
            step(nc.vector.tensor_tensor(rank, rank, gate, ALU.subtract))
            step(nc.vector.tensor_tensor(rank, rank, bank[0:TILE, 0, 0:E2 * TILES], ALU.add))
            step(nc.vector.scalar_tensor_tensor(rank, rank, s_ok[:, 0:1], markf, ALU.is_lt, ALU.mult))
            step(nc.vector.tensor_tensor(rank, rank, above, ALU.add))
            nc.vector.tensor_tensor(gate, rank, score, ALU.mult).then_inc(gate_ready, 1)
            dve.wait_ge(gate_turned, 1)
            nc.vector.tensor_copy(s_gateT[:, :, :], bank[0:E2, 2:4, 0:TOK]).then_inc(gateT_ready, 1)
            dve.wait_ge(gate_ready, 1)
            with dve.Fori(0, E2) as e:
                for i in range(TILES):
                    dve.wait_ge(raw_ready, e * TILES + i + 1)
                    nc.vector.scalar_tensor_tensor(H[:, i, :], raw[:, bass.ds(e, 1), i, :].rearrange("p e d -> p (e d)"),
                                                   s_gate[:, bass.ds(e, 1), i:i + 1].rearrange("p e i -> p (e i)"), H[:, i, :],
                                                   ALU.mult, ALU.add).then_inc(y_added, 1)
                dve.wait_ge(y_added, e * TILES + TILES)
            for i in range(TILES):
                dve.wait_ge(bias_done, i + 1)
                nc.vector.tensor_tensor(H[:, i, :], H[:, i, :], bank[0:TILE, i, 0:D], ALU.add).then_inc(y_ready, 1)

        later.close()

        block = ctx.enter_context(nc.Block())

        @block.sync
        def _(sp):
            sp.dma_start(cols[:, :], a["cols"]).then_inc(cols_in, 16)
            tokenizer_sync(sp)
            attn_sync(sp)
            mix_sync(sp)
            layers_sync(sp)
            mix2_sync(sp)
            mix_sync_loop(sp)
            layers_sync_loop(sp)
            mix2_store(sp)

        @block.gpsimd
        def _(pool):
            for w in (a_w, router_w, gate_up_w, w1, gate2_w):
                nc.gpsimd.memset(w[64:128, 1, :], 0.0)
            nc.gpsimd.memset(xT[64:128, 1, :, :], 0.0).then_inc(pool_const, 1)
            pool.wait_ge(pool_const, 1)
            nc.gpsimd.memset(minus_half[:, :], -0.5)
            nc.gpsimd.memset(eps5[:, :], 1e-5)
            nc.gpsimd.memset(eps6[:, :], 1e-6)
            nc.gpsimd.memset(ident[:, :], 0.0)
            nc.gpsimd.memset(ones[:, :], 1.0)
            nc.gpsimd.memset(lower[:, :], 1.0)
            nc.gpsimd.memset(head64[:, :], float(T_DH) ** -0.5)
            nc.gpsimd.memset(head16[:, :], 1.0).then_inc(pool_const, 1)
            pool.wait_ge(pool_const, 2)
            nc.gpsimd.affine_select(out=ident[:, :], in_=ident[:, :], compare_op=ALU.not_equal, fill=1.0, base=0,
                                    pattern=[[-1, 128]], channel_multiplier=1)
            nc.gpsimd.affine_select(out=lower[:, :], in_=lower[:, :], compare_op=ALU.is_gt, fill=0.0, base=0,
                                    pattern=[[1, TILE]], channel_multiplier=-1).then_inc(pool_const, 1)
            n = 3
            for mask, width in ((head64, T_DH), (head16, DH)):
                view = mask[:, :].rearrange("p (h d) -> p h d", d=width)
                nc.gpsimd.affine_select(out=view, in_=view, compare_op=ALU.is_ge, fill=0.0, base=0,
                                        pattern=[[-width, 128 // width], [0, width]], channel_multiplier=1).then_inc(pool_const, 1)
                n += 1
                pool.wait_ge(pool_const, n)
                nc.gpsimd.affine_select(out=view, in_=view, compare_op=ALU.is_ge, fill=0.0, base=width - 1,
                                        pattern=[[width, 128 // width], [0, width]], channel_multiplier=-1).then_inc(pool_const, 1)
                n += 1
                pool.wait_ge(pool_const, n)
            nc.gpsimd.iota(rank8[:, 0, :], pattern=[[-1, E1]], base=E1, channel_multiplier=0,
                           allow_small_or_imprecise_dtypes=True).then_inc(masks_ready, 1)
            tokenizer_pool(pool)
            norm_rstd(pool, NORM_A, eps5, NORM_A)
            mix_pool(pool)
            layers_pool(pool)
            mix2_pool(pool)

        @block.tensor
        def _(pe):
            tokenizer_tensor(pe)
            attn_tensor(pe)
            mix_tensor(pe)
            layers_tensor(pe)
            mix2_tensor(pe)

        @block.scalar
        def _(act):
            tokenizer_scalar(act)
            attn_scalar(act)
            mix_scalar(act)
            layers_scalar(act)
            mix2_scalar(act)

        @block.vector
        def _(dve):
            dve.wait_ge(cols_in, 16)
            dve.wait_ge(masks_ready, 1)
            tokenizer_vector(dve)
            attn_vector(dve)
            mix_vector(dve)
            layers_vector(dve)
            mix2_vector(dve)


def layout(x):
    f = lambda n: np.asarray(x[n])
    rows = lambda m, n=128: np.ascontiguousarray(m.reshape(-1, n, m.shape[-1]).transpose(1, 0, 2))
    col = lambda v: np.pad(v.reshape(-1, 1), ((0, 128 - v.size), (0, 0)))
    cut = lambda v: [col(v[k:k + 128]) for k in range(0, v.size, 128)]
    p = {}
    im = f("x").reshape(B, 32, 16, 8, 16, 8).transpose(1, 3, 5, 0, 2, 4).reshape(PATCH_K, B * IMG)
    p["patches"] = rows(im)
    p["conv_w"] = rows(f("L0_tok_conv_w").transpose(1, 2, 3, 0).reshape(PATCH_K, DT))
    p["t_qkv_w"] = f("L0_tok_qkv_w").transpose(1, 0, 2)
    p["t_out_w"] = f("L0_tok_out_w").reshape(T_LAYERS, IC, 128, DT).transpose(2, 0, 1, 3)
    p["t_ff1_w"] = f("L0_tok_ff1_w").transpose(1, 0, 2)
    p["t_ff2_w"] = f("L0_tok_ff2_w").reshape(T_LAYERS, FC, 128, DT).transpose(2, 0, 1, 3)
    p["t_head_w"] = f("L0_tok_head_w")
    p["t_rows"] = np.concatenate([v for l in range(T_LAYERS) for v in (f("L0_tok_out_b")[l], f("L0_tok_ff2_b")[l])]
                                 + [f("L0_tok_head_b")])[None]
    p["txt"] = f("txt")
    c = cut(f("L0_tok_conv_b"))
    for l in range(T_LAYERS):
        for n in ("ln1_g", "ln1_b", "ln2_g", "ln2_b", "ff1_b"):
            c += cut(f("L0_tok_" + n)[l])
    c += cut(f("L0_tok_lnf_g")) + cut(f("L0_tok_lnf_b")) + cut(f("L0_ffn_norm_w"))
    p["cols"] = np.concatenate(c, 1)
    p["a_w"] = f("L0_attn_w_qkv").T
    p["a_proj_w"] = f("L0_attn_w_proj").T
    p["a_row"] = f("L0_attn_b_proj")[None]
    p["router"] = f("L0_ffn_router_w").T
    gu = np.concatenate([f("L0_ffn_gate_w").transpose(0, 2, 1), f("L0_ffn_up_w").transpose(0, 2, 1)], 2)
    p["gate_up_a"], p["gate_up_b"] = gu[:, :128], gu[:, 128:]
    p["down"] = f("L0_ffn_down_w").transpose(0, 2, 1).reshape(E1, F1C, 128, D).transpose(0, 2, 1, 3)
    blocks = np.zeros((LAYERS, HALF, 2, 3, HALF), np.float32)
    for h in range(HEADS):
        c, g = divmod(h, GROUPS)
        for which, n in enumerate("qkv"):
            to = slice(DH * g, DH * (g + 1)) if n == "v" else slice(g, None, GROUPS)
            blocks[:, DH * g:DH * (g + 1), c, which, to] = f(f"L1_attn_{n}w")[:, h].transpose(0, 2, 1)
    p["qkv"] = blocks.reshape(LAYERS, HALF, -1)
    half = lambda v: [col(v[k:k + HALF]) for k in range(0, v.size, HALF)]
    apart = lambda l: [col(f(f"L1_attn_{n}b")[l, GROUPS * c:GROUPS * (c + 1)].T.reshape(-1)) for c in range(2) for n in "qk"]
    per_layer = lambda of: np.stack([np.concatenate(of(l), 1) for l in range(LAYERS)])
    p["p_cols"] = per_layer(lambda l: half(f("L1_attn_ln1_g")[l]) + half(f("L1_attn_ln1_b")[l]) + apart(l))
    p["m_cols"] = per_layer(lambda l: [c for n in ("ln2_g", "ln2_b", "b1") for c in cut(f("L1_attn_" + n)[l])])
    p["p_row"] = f("L1_attn_vb").reshape(LAYERS, 1, D)
    p["m_row"] = f("L1_attn_b2").reshape(LAYERS, 1, D)
    first = np.concatenate([f("L1_attn_w1").transpose(0, 2, 1), f("L1_ffn_w1")])
    second = np.concatenate([f("L1_attn_w2").transpose(0, 2, 1), f("L1_ffn_w2")])
    p["w1_a"], p["w1_b"] = first[:, :128], first[:, 128:]
    p["w2"] = second.reshape(LAYERS + E2, MLPC, 128, D).transpose(0, 2, 1, 3).reshape(LAYERS + E2, 128, MLPC * D)
    p["gate2"] = f("L1_ffn_gate_weight").T
    p["mix_b1"] = f("L1_ffn_b1").reshape(E2, H2C, 128).transpose(2, 0, 1)
    p["mix_b2"] = f("L1_ffn_b2")
    return {n: np.ascontiguousarray(v) for n, v in p.items()}


def kernel(**inputs):
    import concourse.bacc as bacc
    from concourse.bass_utils import run_bass_kernel_spmd

    arrays = layout(inputs)
    nc = bacc.Bacc("TRN2", target_bir_lowering=False, num_devices=1)
    a = {n: nc.dram_tensor("in_" + n, v.shape, mybir.dt.from_np(v.dtype), kind="ExternalInput").ap() for n, v in arrays.items()}
    out = nc.dram_tensor("out", (B, TOK, D), F32, kind="ExternalOutput").ap()
    build(nc, a, out)
    r = run_bass_kernel_spmd(nc, [{"in_" + n: v for n, v in arrays.items()}], core_ids=[0])
    return r.results[0]["out"]
```
